# Optimizing a Trainium2 kernel written in Bass

```python
import numpy as np
import jax
import jax.numpy as jnp

def _softmax(x, axis=-1):
    return jax.nn.softmax(x, axis=axis)

def _gelu(x):
    return jax.nn.gelu(x, approximate=True)

def _silu(x):
    return jax.nn.silu(x)

def _sigmoid(x):
    return jax.nn.sigmoid(x)

def _layernorm(x, axis=-1, eps=1e-05):
    m = jnp.mean(x, axis=axis, keepdims=True)
    v = jnp.var(x, axis=axis, keepdims=True)
    return (x - m) / jnp.sqrt(v + eps)

def _scatter_add(tgt, idx, src, axis=0):
    return tgt.at[idx].add(src)

def _segment_sum(src, seg, n):
    return jax.ops.segment_sum(src, seg, n)
kernel_name = 'mk_flamingo_gated_d4_seqx_r8_c2d2f0'

def setup_inputs(seed: int=0):
    np.random.seed(seed)
    _w = jnp.asarray

    def _rec_inputs():
        import jax
        import jax.numpy as jnp
        _rk = jax.random.key(seed)
        x = -0.000125 + 0.9999 * jax.random.normal(jax.random.fold_in(_rk, 1), (4, 256, 256), jnp.float32)
        _lenS = 256 - jax.random.randint(jax.random.fold_in(_rk, 7), (4,), 0, max(1, 256 // 4) + 1, jnp.int32)
        _lenS2 = 256 - jax.random.randint(jax.random.fold_in(_rk, 8), (4,), 0, max(1, 256 // 4) + 1, jnp.int32)
        fside_BxS2xS2_0 = -3.05549e-07 + 0.0199987 * jax.random.normal(jax.random.fold_in(_rk, 11), (4, 256, 256), jnp.float32)
        _ctx_1024P = jax.random.normal(jax.random.fold_in(_rk, 12), (4, 16, 128), jnp.float32)
        _ctx_1024c = jax.random.dirichlet(jax.random.fold_in(_rk, 512), 0.3 * jnp.ones((16,), jnp.float32), (4, 256))
        _ctx_1024t = jnp.einsum('bsk,bkd->bsd', _ctx_1024c, _ctx_1024P)
        _ctx_1024t = _ctx_1024t * jax.lax.rsqrt(jnp.mean(jnp.square(_ctx_1024t)) + 1e-12) * 0.953939
        ctx_1024 = 6.82029e-06 + 0.0200006 * (_ctx_1024t + 0.3 * jax.random.normal(jax.random.fold_in(_rk, 612), (4, 256, 128), jnp.float32))
        fside_BxSx2_0 = jax.random.uniform(jax.random.fold_in(_rk, 13), (4, 256, 2), jnp.float32, 0.0, 0.999707)
        _validS = jnp.arange(256)[None, :] < _lenS[:, None]
        _validS2 = jnp.arange(256)[None, :] < _lenS2[:, None]
        _causal = jnp.tril(jnp.ones((256, 256), dtype=bool))
        mask_BxS2_bf1 = jnp.ones((4, 256), dtype=bool)
        _g = jax.random.normal(jax.random.fold_in(_rk, 9001), (2, 4), jnp.float32)
        _g = jnp.sign(_g) * jnp.maximum(jnp.abs(_g), 1.0) + (_g == 0) * 1.0
        g_xattn = _g[0]
        g_ffn = _g[1]
        return (x, fside_BxS2xS2_0, ctx_1024, fside_BxSx2_0, mask_BxS2_bf1, g_xattn, g_ffn)
    x, fside_BxS2xS2_0, ctx_1024, fside_BxSx2_0, mask_BxS2_bf1, g_xattn, g_ffn = _rec_inputs()

    def _L0_xattn_setup():
        import jax, jax.numpy as jnp
        import numpy as np
        EPS = 1e-06
        QMAX = 127.0

        def _smooth_quant_linear(x, w):
            amax_x = jnp.max(jnp.abs(x), axis=0)
            amax_w = jnp.max(jnp.abs(w), axis=0)
            s = jnp.sqrt(jnp.maximum(amax_x, EPS) / jnp.maximum(amax_w, EPS))
            s = jnp.maximum(s, EPS)
            xs = x / s
            ws = w * s
            x_scale = jnp.maximum(jnp.max(jnp.abs(xs), axis=-1, keepdims=True), EPS) / QMAX
            w_scale = jnp.maximum(jnp.max(jnp.abs(ws), axis=-1, keepdims=True), EPS) / QMAX
            x_q = jnp.clip(jnp.round(xs / x_scale), -QMAX, QMAX)
            w_q = jnp.clip(jnp.round(ws / w_scale), -QMAX, QMAX)
            return x_q @ w_q.T * x_scale * w_scale.T

        def _expert_forward(xe, guw, dw):
            h = _smooth_quant_linear(xe, guw)
            gate, up = jnp.split(h, 2, axis=-1)
            a = jax.nn.silu(gate) * up
            return _smooth_quant_linear(a, dw)
        key = jax.random.key(seed)
        k1, k2, k3 = jax.random.split(key, 3)
        E, T, D, I = (8, 256, 256, 128)
        x = jax.random.normal(k1, (E, T, D), dtype=jnp.float32)
        gate_up_weight = jax.random.normal(k2, (E, 2 * I, D), dtype=jnp.float32) * 0.02
        down_weight = jax.random.normal(k3, (E, D, I), dtype=jnp.float32) * 0.02
        return {'x': x, 'gate_up_weight': gate_up_weight, 'down_weight': down_weight}
    _L0_xattn_all = _L0_xattn_setup()
    _L0_xattn_in = {k: v for k, v in _L0_xattn_all.items() if k in ()}
    del _L0_xattn_all

    def _L0_ffn_setup():
        import jax, jax.numpy as jnp
        import numpy as np
        H, F, E, K = (256, 128, 16, 4)
        ROUTED_SCALE = 1.0
        key = jax.random.key(seed)
        ks = jax.random.split(key, 9)
        s = 0.02
        return {'x': jax.random.normal(ks[0], (4, 64, H), jnp.float32), 'router_w': jax.random.normal(ks[1], (E, H), jnp.float32) * s, 'router_bias': jnp.zeros((E,), jnp.float32), 'expert_gate_w': jax.random.normal(ks[2], (E, F, H), jnp.float32) * s, 'expert_up_w': jax.random.normal(ks[3], (E, F, H), jnp.float32) * s, 'expert_down_w': jax.random.normal(ks[4], (E, H, F), jnp.float32) * s, 'shared_gate_w': jax.random.normal(ks[5], (F, H), jnp.float32) * s, 'shared_up_w': jax.random.normal(ks[6], (F, H), jnp.float32) * s, 'shared_down_w': jax.random.normal(ks[7], (H, F), jnp.float32) * s}
    _L0_ffn_all = _L0_ffn_setup()
    _L0_ffn_in = {k: v for k, v in _L0_ffn_all.items() if k in ('router_w', 'router_bias', 'expert_gate_w', 'expert_up_w', 'expert_down_w', 'shared_gate_w', 'shared_up_w', 'shared_down_w')}
    del _L0_ffn_all

    def _L1_xattn_setup():
        import jax, jax.numpy as jnp
        import numpy as np
        EPS = 1e-05

        def rmsnorm(x, g, eps=EPS):
            var = jnp.mean(jnp.square(x), axis=-1, keepdims=True)
            return x * jax.lax.rsqrt(var + eps) * g
        key = jax.random.key(seed)
        ks = jax.random.split(key, 8)
        B, Sq, Skv = (2, 512, 64)
        dim, cdim, H, D = (256, 128, 16, 128)
        inner = H * D
        s = lambda f: 1.0 / np.sqrt(f)
        return {'hidden_states': jax.random.normal(ks[0], (B, Sq, dim), jnp.float32), 'encoder_hidden_states': jax.random.normal(ks[1], (B, Skv, cdim), jnp.float32), 'Wq': jax.random.normal(ks[2], (dim, inner), jnp.float32) * s(dim), 'Wk': jax.random.normal(ks[3], (cdim, inner), jnp.float32) * s(cdim), 'Wv': jax.random.normal(ks[4], (cdim, inner), jnp.float32) * s(cdim), 'Wo': jax.random.normal(ks[5], (inner, dim), jnp.float32) * s(inner), 'gq': jnp.ones((D,), jnp.float32), 'gk': jnp.ones((D,), jnp.float32)}
    _L1_xattn_all = _L1_xattn_setup()
    _L1_xattn_in = {k: v for k, v in _L1_xattn_all.items() if k in ('Wq', 'Wk', 'Wv', 'Wo', 'gq', 'gk')}
    del _L1_xattn_all

    def _L1_ffn_setup():
        import jax, jax.numpy as jnp
        import numpy as np
        NUM_EXPERTS = 8
        TOP_K = 2
        EMB = 256
        MLP = 512
        B, S = (4, 128)
        key = jax.random.key(seed)
        ks = jax.random.split(key, 5)
        scale_x = 1.0
        return {'x': jax.random.normal(ks[0], (B, S, EMB), dtype=jnp.float32), 'gate_kernel': jax.random.normal(ks[1], (EMB, NUM_EXPERTS), dtype=jnp.float32) / np.sqrt(EMB), 'w0_kernel': jax.random.normal(ks[2], (NUM_EXPERTS, EMB, MLP), dtype=jnp.float32) / np.sqrt(EMB), 'w1_kernel': jax.random.normal(ks[3], (NUM_EXPERTS, EMB, MLP), dtype=jnp.float32) / np.sqrt(EMB), 'wo_kernel': jax.random.normal(ks[4], (NUM_EXPERTS, MLP, EMB), dtype=jnp.float32) / np.sqrt(MLP)}
    _L1_ffn_all = _L1_ffn_setup()
    _L1_ffn_in = {k: v for k, v in _L1_ffn_all.items() if k in ('gate_kernel', 'w0_kernel', 'w1_kernel', 'wo_kernel')}
    del _L1_ffn_all

    def _L2_xattn_setup():
        import jax, jax.numpy as jnp
        import numpy as np
        DIM = 256
        CTX_DIM = 128
        N_HEADS = 32
        HEAD_DIM = DIM // N_HEADS
        POS_DIM = 2
        B, N, CTXN = (2, 256, 256)
        ROPE_BASE = 10000.0

        def apply_axial_rope(x, pos):
            b, n, h, d = x.shape
            p = pos.shape[-1]
            dpa = d // p
            half = dpa // 2
            freqs = ROPE_BASE ** (-jnp.arange(half, dtype=x.dtype) / half)
            ang = pos[..., :, None] * freqs
            cos = jnp.cos(ang)[:, :, None, :, :]
            sin = jnp.sin(ang)[:, :, None, :, :]
            xr = x.reshape(b, n, h, p, half, 2)
            x1, x2 = (xr[..., 0], xr[..., 1])
            out = jnp.stack([x1 * cos - x2 * sin, x1 * sin + x2 * cos], axis=-1)
            return out.reshape(b, n, h, d)
        key = jax.random.key(seed)
        ks = jax.random.split(key, 8)
        x = jax.random.normal(ks[0], (B, N, DIM), jnp.float32)
        ctx = jax.random.normal(ks[1], (B, CTXN, CTX_DIM), jnp.float32)
        pos_map = jax.random.uniform(ks[2], (B, N, POS_DIM), jnp.float32)
        ctx_pos_map = jax.random.uniform(ks[3], (B, CTXN, POS_DIM), jnp.float32)
        Wq = jax.random.normal(ks[4], (DIM, DIM), jnp.float32) / np.sqrt(DIM)
        Wkv = jax.random.normal(ks[5], (CTX_DIM, 2 * DIM), jnp.float32) / np.sqrt(CTX_DIM)
        Wout = jax.random.normal(ks[6], (DIM, DIM), jnp.float32) / np.sqrt(DIM)
        bout = jnp.zeros((DIM,), jnp.float32)
        return {'x': x, 'ctx': ctx, 'pos_map': pos_map, 'ctx_pos_map': ctx_pos_map, 'Wq': Wq, 'Wkv': Wkv, 'Wout': Wout, 'bout': bout}
    _L2_xattn_all = _L2_xattn_setup()
    _L2_xattn_in = {k: v for k, v in _L2_xattn_all.items() if k in ('Wq', 'Wkv', 'Wout', 'bout')}
    del _L2_xattn_all

    def _L2_ffn_setup():
        import jax, jax.numpy as jnp
        import numpy as np
        B, S, H, F, E, R, K = (2, 128, 256, 896, 8, 32, 2)

        def _gather_slot(a_all, e):
            return jnp.take_along_axis(a_all, e[:, None, None], axis=1)[:, 0]
        key = jax.random.key(seed)
        ks = jax.random.split(key, 12)
        sc = 0.02
        n = lambda k, shape, s: jax.random.normal(k, shape, dtype=jnp.float32) * s
        return {'hidden_states': n(ks[0], (B, S, H), 1.0), 'Wg': n(ks[1], (E, H), sc), 'W1': n(ks[2], (F, H), sc), 'W2': n(ks[3], (H, F), sc), 'W3': n(ks[4], (F, H), sc), 'A1': n(ks[5], (E, R, H), sc), 'B1': n(ks[6], (E, F, R), sc), 'A2': n(ks[7], (E, R, F), sc), 'B2': n(ks[8], (E, H, R), sc), 'A3': n(ks[9], (E, R, H), sc), 'B3': n(ks[10], (E, F, R), sc)}
    _L2_ffn_all = _L2_ffn_setup()
    _L2_ffn_in = {k: v for k, v in _L2_ffn_all.items() if k in ('Wg', 'W1', 'W2', 'W3', 'A1', 'B1', 'A2', 'B2', 'A3', 'B3')}
    del _L2_ffn_all

    def _L3_xattn_setup():
        import jax, jax.numpy as jnp
        import numpy as np
        N_HEADS = 16
        N_KV_HEADS = 8
        HEAD_DIM = 128
        D_TEXT = 256
        D_VISION = 128
        GROUPS = N_HEADS // N_KV_HEADS
        key = jax.random.key(seed)
        ks = jax.random.split(key, 6)
        B, T_text, T_vis = (4, 256, 72)
        text_hidden = jax.random.normal(ks[0], (B, T_text, D_TEXT), dtype=jnp.float32)
        vision_tokens = jax.random.normal(ks[1], (B, T_vis, D_VISION), dtype=jnp.float32)
        vision_mask = jnp.ones((B, T_vis), dtype=bool)
        s = 0.02
        Wq = jax.random.normal(ks[2], (D_TEXT, N_HEADS * HEAD_DIM), dtype=jnp.float32) * s
        Wk = jax.random.normal(ks[3], (D_VISION, N_KV_HEADS * HEAD_DIM), dtype=jnp.float32) * s
        Wv = jax.random.normal(ks[4], (D_VISION, N_KV_HEADS * HEAD_DIM), dtype=jnp.float32) * s
        Wo = jax.random.normal(ks[5], (N_HEADS * HEAD_DIM, D_TEXT), dtype=jnp.float32) * s
        return {'text_hidden': text_hidden, 'vision_tokens': vision_tokens, 'vision_mask': vision_mask, 'Wq': Wq, 'Wk': Wk, 'Wv': Wv, 'Wo': Wo}
    _L3_xattn_all = _L3_xattn_setup()
    _L3_xattn_in = {k: v for k, v in _L3_xattn_all.items() if k in ('Wq', 'Wk', 'Wv', 'Wo')}
    del _L3_xattn_all

    def _L3_ffn_setup():
        import jax, jax.numpy as jnp
        import numpy as np
        N_GROUPS = 4
        TOPK_GROUPS = 2
        TOPK = 4
        ROUTE_SCALE = 1.0

        def _gate(xt, gate_w):
            T = xt.shape[0]
            E = gate_w.shape[0]
            scores = jax.nn.sigmoid(xt @ gate_w.T)
            original_scores = scores
            sg = scores.reshape(T, N_GROUPS, E // N_GROUPS)
            group_scores = sg.max(axis=-1)
            _, gidx = jax.lax.top_k(group_scores, TOPK_GROUPS)
            gmask = jax.nn.one_hot(gidx, N_GROUPS, dtype=scores.dtype).sum(axis=1)
            masked = (sg * gmask[:, :, None]).reshape(T, E)
            _, idx = jax.lax.top_k(masked, TOPK)
            w = jnp.take_along_axis(original_scores, idx, axis=-1)
            w = w / w.sum(axis=-1, keepdims=True) * ROUTE_SCALE
            return (w, idx)
        key = jax.random.key(seed)
        ks = jax.random.split(key, 8)
        B, S, D = (1, 256, 256)
        E, I = (16, 176)
        SH = 2 * I
        s = 0.02
        return {'x': jax.random.normal(ks[0], (B, S, D), dtype=jnp.float32), 'gate_w': jax.random.normal(ks[1], (E, D), dtype=jnp.float32) * s, 'W1': jax.random.normal(ks[2], (E, I, D), dtype=jnp.float32) * s, 'W2': jax.random.normal(ks[3], (E, D, I), dtype=jnp.float32) * s, 'W3': jax.random.normal(ks[4], (E, I, D), dtype=jnp.float32) * s, 'Ws1': jax.random.normal(ks[5], (SH, D), dtype=jnp.float32) * s, 'Ws2': jax.random.normal(ks[6], (D, SH), dtype=jnp.float32) * s, 'Ws3': jax.random.normal(ks[7], (SH, D), dtype=jnp.float32) * s}
    _L3_ffn_all = _L3_ffn_setup()
    _L3_ffn_in = {k: v for k, v in _L3_ffn_all.items() if k in ('gate_w', 'W1', 'W2', 'W3', 'Ws1', 'Ws2', 'Ws3')}
    del _L3_ffn_all
    return {'x': x, 'fside_BxS2xS2_0': fside_BxS2xS2_0, 'ctx_1024': ctx_1024, 'fside_BxSx2_0': fside_BxSx2_0, 'mask_BxS2_bf1': mask_BxS2_bf1, 'g_xattn': g_xattn, 'g_ffn': g_ffn, 'L0_ffn_router_w': _L0_ffn_in['router_w'], 'L0_ffn_router_bias': _L0_ffn_in['router_bias'], 'L0_ffn_expert_gate_w': _L0_ffn_in['expert_gate_w'], 'L0_ffn_expert_up_w': _L0_ffn_in['expert_up_w'], 'L0_ffn_expert_down_w': _L0_ffn_in['expert_down_w'], 'L0_ffn_shared_gate_w': _L0_ffn_in['shared_gate_w'], 'L0_ffn_shared_up_w': _L0_ffn_in['shared_up_w'], 'L0_ffn_shared_down_w': _L0_ffn_in['shared_down_w'], 'L1_xattn_Wq': _L1_xattn_in['Wq'], 'L1_xattn_Wk': _L1_xattn_in['Wk'], 'L1_xattn_Wv': _L1_xattn_in['Wv'], 'L1_xattn_Wo': _L1_xattn_in['Wo'], 'L1_xattn_gq': _L1_xattn_in['gq'], 'L1_xattn_gk': _L1_xattn_in['gk'], 'L1_ffn_gate_kernel': _L1_ffn_in['gate_kernel'], 'L1_ffn_w0_kernel': _L1_ffn_in['w0_kernel'], 'L1_ffn_w1_kernel': _L1_ffn_in['w1_kernel'], 'L1_ffn_wo_kernel': _L1_ffn_in['wo_kernel'], 'L2_xattn_Wq': _L2_xattn_in['Wq'], 'L2_xattn_Wkv': _L2_xattn_in['Wkv'], 'L2_xattn_Wout': _L2_xattn_in['Wout'], 'L2_xattn_bout': _L2_xattn_in['bout'], 'L2_ffn_Wg': _L2_ffn_in['Wg'], 'L2_ffn_W1': _L2_ffn_in['W1'], 'L2_ffn_W2': _L2_ffn_in['W2'], 'L2_ffn_W3': _L2_ffn_in['W3'], 'L2_ffn_A1': _L2_ffn_in['A1'], 'L2_ffn_B1': _L2_ffn_in['B1'], 'L2_ffn_A2': _L2_ffn_in['A2'], 'L2_ffn_B2': _L2_ffn_in['B2'], 'L2_ffn_A3': _L2_ffn_in['A3'], 'L2_ffn_B3': _L2_ffn_in['B3'], 'L3_xattn_Wq': _L3_xattn_in['Wq'], 'L3_xattn_Wk': _L3_xattn_in['Wk'], 'L3_xattn_Wv': _L3_xattn_in['Wv'], 'L3_xattn_Wo': _L3_xattn_in['Wo'], 'L3_ffn_gate_w': _L3_ffn_in['gate_w'], 'L3_ffn_W1': _L3_ffn_in['W1'], 'L3_ffn_W2': _L3_ffn_in['W2'], 'L3_ffn_W3': _L3_ffn_in['W3'], 'L3_ffn_Ws1': _L3_ffn_in['Ws1'], 'L3_ffn_Ws2': _L3_ffn_in['Ws2'], 'L3_ffn_Ws3': _L3_ffn_in['Ws3']}

def reference(x, fside_BxS2xS2_0, ctx_1024, fside_BxSx2_0, mask_BxS2_bf1, g_xattn, g_ffn, L0_ffn_router_w, L0_ffn_router_bias, L0_ffn_expert_gate_w, L0_ffn_expert_up_w, L0_ffn_expert_down_w, L0_ffn_shared_gate_w, L0_ffn_shared_up_w, L0_ffn_shared_down_w, L1_xattn_Wq, L1_xattn_Wk, L1_xattn_Wv, L1_xattn_Wo, L1_xattn_gq, L1_xattn_gk, L1_ffn_gate_kernel, L1_ffn_w0_kernel, L1_ffn_w1_kernel, L1_ffn_wo_kernel, L2_xattn_Wq, L2_xattn_Wkv, L2_xattn_Wout, L2_xattn_bout, L2_ffn_Wg, L2_ffn_W1, L2_ffn_W2, L2_ffn_W3, L2_ffn_A1, L2_ffn_B1, L2_ffn_A2, L2_ffn_B2, L2_ffn_A3, L2_ffn_B3, L3_xattn_Wq, L3_xattn_Wk, L3_xattn_Wv, L3_xattn_Wo, L3_ffn_gate_w, L3_ffn_W1, L3_ffn_W2, L3_ffn_W3, L3_ffn_Ws1, L3_ffn_Ws2, L3_ffn_Ws3):
    import jax
    import jax.numpy as jnp

    def _L0_xattn_ref(x, gate_up_weight, down_weight):
        import jax, jax.numpy as jnp
        import numpy as np
        EPS = 1e-06
        QMAX = 127.0

        def _smooth_quant_linear(x, w):
            amax_x = jnp.max(jnp.abs(x), axis=0)
            amax_w = jnp.max(jnp.abs(w), axis=0)
            s = jnp.sqrt(jnp.maximum(amax_x, EPS) / jnp.maximum(amax_w, EPS))
            s = jnp.maximum(s, EPS)
            xs = x / s
            ws = w * s
            x_scale = jnp.maximum(jnp.max(jnp.abs(xs), axis=-1, keepdims=True), EPS) / QMAX
            w_scale = jnp.maximum(jnp.max(jnp.abs(ws), axis=-1, keepdims=True), EPS) / QMAX
            x_q = jnp.clip(jnp.round(xs / x_scale), -QMAX, QMAX)
            w_q = jnp.clip(jnp.round(ws / w_scale), -QMAX, QMAX)
            return x_q @ w_q.T * x_scale * w_scale.T

        def _expert_forward(xe, guw, dw):
            h = _smooth_quant_linear(xe, guw)
            gate, up = jnp.split(h, 2, axis=-1)
            a = jax.nn.silu(gate) * up
            return _smooth_quant_linear(a, dw)
        return jax.vmap(_expert_forward)(x, gate_up_weight, down_weight)

    def _L0_ffn_ref(x, router_w, router_bias, expert_gate_w, expert_up_w, expert_down_w, shared_gate_w, shared_up_w, shared_down_w):
        import jax, jax.numpy as jnp
        import numpy as np
        H, F, E, K = (256, 128, 16, 4)
        ROUTED_SCALE = 1.0
        orig_shape = x.shape
        h = x.reshape(-1, orig_shape[-1])
        T = h.shape[0]
        logits = h @ router_w.T
        scores = jax.nn.sigmoid(logits)
        choice = scores + router_bias[None, :]
        _, topk_idx = jax.lax.top_k(choice, K)
        topk_w = jnp.take_along_axis(scores, topk_idx, axis=1)
        topk_w = topk_w / (topk_w.sum(-1, keepdims=True) + 1e-20)
        topk_w = topk_w * ROUTED_SCALE
        comb = jnp.zeros((T, E), h.dtype).at[jnp.arange(T)[:, None], topk_idx].set(topk_w)
        g = jnp.einsum('th,efh->tef', h, expert_gate_w)
        u = jnp.einsum('th,efh->tef', h, expert_up_w)
        a = jax.nn.silu(g) * u
        routed = jnp.einsum('tef,te,ehf->th', a, comb, expert_down_w)
        shared = jax.nn.silu(h @ shared_gate_w.T) * (h @ shared_up_w.T) @ shared_down_w.T
        return (routed + shared).reshape(orig_shape)

    def _L1_xattn_ref(hidden_states, encoder_hidden_states, Wq, Wk, Wv, Wo, gq, gk):
        import jax, jax.numpy as jnp
        import numpy as np
        EPS = 1e-05

        def rmsnorm(x, g, eps=EPS):
            var = jnp.mean(jnp.square(x), axis=-1, keepdims=True)
            return x * jax.lax.rsqrt(var + eps) * g
        B, Sq, _ = hidden_states.shape
        Skv = encoder_hidden_states.shape[1]
        D = gq.shape[0]
        H = Wq.shape[1] // D
        scale = 1.0 / np.sqrt(D)
        q = (hidden_states @ Wq).reshape(B, Sq, H, D)
        k = (encoder_hidden_states @ Wk).reshape(B, Skv, H, D)
        v = (encoder_hidden_states @ Wv).reshape(B, Skv, H, D)
        q = rmsnorm(q, gq)
        k = rmsnorm(k, gk)
        scores = jnp.einsum('bqhd,bkhd->bhqk', q, k) * scale
        attn = jax.nn.softmax(scores, axis=-1)
        out = jnp.einsum('bhqk,bkhd->bqhd', attn, v)
        out = out.reshape(B, Sq, H * D)
        return out @ Wo

    def _L1_ffn_ref(x, gate_kernel, w0_kernel, w1_kernel, wo_kernel):
        import jax, jax.numpy as jnp
        import numpy as np
        NUM_EXPERTS = 8
        TOP_K = 2
        EMB = 256
        MLP = 512
        B, S = (4, 128)
        gate_logits = jnp.einsum('bsd,de->bse', x, gate_kernel)
        top_k_weights, top_k_indices = jax.lax.top_k(gate_logits, TOP_K)
        top_k_weights = jax.nn.softmax(top_k_weights.astype(jnp.float32), axis=-1).astype(x.dtype)
        one_hot = jax.nn.one_hot(top_k_indices, NUM_EXPERTS, dtype=x.dtype)
        combine = jnp.einsum('bsk,bske->bse', top_k_weights, one_hot)
        h0 = jnp.einsum('bsd,edm->bsem', x, w0_kernel)
        h1 = jnp.einsum('bsd,edm->bsem', x, w1_kernel)
        inter = jax.nn.silu(h0) * h1
        out = jnp.einsum('bse,bsem,emd->bsd', combine, inter, wo_kernel)
        return out

    def _L2_xattn_ref(x, ctx, pos_map, ctx_pos_map, Wq, Wkv, Wout, bout):
        import jax, jax.numpy as jnp
        import numpy as np
        DIM = 256
        CTX_DIM = 128
        N_HEADS = 32
        HEAD_DIM = DIM // N_HEADS
        POS_DIM = 2
        B, N, CTXN = (2, 256, 256)
        ROPE_BASE = 10000.0

        def apply_axial_rope(x, pos):
            b, n, h, d = x.shape
            p = pos.shape[-1]
            dpa = d // p
            half = dpa // 2
            freqs = ROPE_BASE ** (-jnp.arange(half, dtype=x.dtype) / half)
            ang = pos[..., :, None] * freqs
            cos = jnp.cos(ang)[:, :, None, :, :]
            sin = jnp.sin(ang)[:, :, None, :, :]
            xr = x.reshape(b, n, h, p, half, 2)
            x1, x2 = (xr[..., 0], xr[..., 1])
            out = jnp.stack([x1 * cos - x2 * sin, x1 * sin + x2 * cos], axis=-1)
            return out.reshape(b, n, h, d)
        b, n, _ = x.shape
        ctx_n = ctx.shape[1]
        q = (x @ Wq).reshape(b, n, N_HEADS, HEAD_DIM)
        k, v = jnp.split(ctx @ Wkv, 2, axis=-1)
        k = k.reshape(b, ctx_n, N_HEADS, HEAD_DIM)
        v = v.reshape(b, ctx_n, N_HEADS, HEAD_DIM)
        q = apply_axial_rope(q, pos_map)
        k = apply_axial_rope(k, ctx_pos_map)
        scale = 1.0 / np.sqrt(HEAD_DIM).astype(np.float32)
        logits = jnp.einsum('bqhd,bkhd->bhqk', q, k) * scale
        w = jax.nn.softmax(logits, axis=-1)
        attn = jnp.einsum('bhqk,bkhd->bqhd', w, v)
        attn = attn.reshape(b, n, N_HEADS * HEAD_DIM)
        return attn @ Wout + bout

    def _L2_ffn_ref(hidden_states, Wg, W1, W2, W3, A1, B1, A2, B2, A3, B3):
        import jax, jax.numpy as jnp
        import numpy as np
        B, S, H, F, E, R, K = (2, 128, 256, 896, 8, 32, 2)

        def _gather_slot(a_all, e):
            return jnp.take_along_axis(a_all, e[:, None, None], axis=1)[:, 0]
        b, s, h = hidden_states.shape
        x = hidden_states.reshape(-1, h)
        nE = Wg.shape[0]
        logits = x @ Wg.T
        probs = jax.nn.softmax(logits.astype(jnp.float32), axis=-1)
        rw, sel = jax.lax.top_k(probs, K)
        rw = (rw / rw.sum(axis=-1, keepdims=True)).astype(x.dtype)
        base1 = x @ W1.T
        base3 = x @ W3.T
        a1_all = jnp.einsum('th,erh->ter', x, A1)
        a3_all = jnp.einsum('th,erh->ter', x, A3)
        out = jnp.zeros_like(x)
        for k in range(K):
            e = sel[:, k]
            mask = jax.nn.one_hot(e, nE, dtype=x.dtype)
            a1 = _gather_slot(a1_all, e)
            a3 = _gather_slot(a3_all, e)
            lora1 = jnp.einsum('ter,efr->tf', mask[:, :, None] * a1[:, None, :], B1)
            lora3 = jnp.einsum('ter,efr->tf', mask[:, :, None] * a3[:, None, :], B3)
            x1 = base1 + lora1
            x3 = base3 + lora3
            x2 = jax.nn.silu(x1) * x3
            down = x2 @ W2.T
            a2_all = jnp.einsum('tf,erf->ter', x2, A2)
            a2 = _gather_slot(a2_all, e)
            lora2 = jnp.einsum('ter,ehr->th', mask[:, :, None] * a2[:, None, :], B2)
            out = out + (down + lora2) * rw[:, k:k + 1]
        return out.reshape(b, s, h)

    def _L3_xattn_ref(text_hidden, vision_tokens, vision_mask, Wq, Wk, Wv, Wo):
        import jax, jax.numpy as jnp
        import numpy as np
        N_HEADS = 16
        N_KV_HEADS = 8
        HEAD_DIM = 128
        D_TEXT = 256
        D_VISION = 128
        GROUPS = N_HEADS // N_KV_HEADS
        B, T_text, _ = text_hidden.shape
        T_vis = vision_tokens.shape[1]
        scale = jnp.float32(np.sqrt(HEAD_DIM))
        q = (text_hidden @ Wq).reshape(B, T_text, N_HEADS, HEAD_DIM).transpose(0, 2, 1, 3)
        k = (vision_tokens @ Wk).reshape(B, T_vis, N_KV_HEADS, HEAD_DIM).transpose(0, 2, 1, 3)
        v = (vision_tokens @ Wv).reshape(B, T_vis, N_KV_HEADS, HEAD_DIM).transpose(0, 2, 1, 3)
        k = jnp.repeat(k, GROUPS, axis=1)
        v = jnp.repeat(v, GROUPS, axis=1)
        scores = jnp.einsum('bhtd,bhsd->bhts', q, k) / scale
        mask = vision_mask[:, None, None, :]
        scores = jnp.where(mask, scores, -jnp.inf)
        attn = jax.nn.softmax(scores, axis=-1)
        attn = jnp.nan_to_num(attn, nan=0.0)
        out = jnp.einsum('bhts,bhsd->bhtd', attn, v)
        out = out.transpose(0, 2, 1, 3).reshape(B, T_text, N_HEADS * HEAD_DIM)
        return out @ Wo

    def _L3_ffn_ref(x, gate_w, W1, W2, W3, Ws1, Ws2, Ws3):
        import jax, jax.numpy as jnp
        import numpy as np
        N_GROUPS = 4
        TOPK_GROUPS = 2
        TOPK = 4
        ROUTE_SCALE = 1.0

        def _gate(xt, gate_w):
            T = xt.shape[0]
            E = gate_w.shape[0]
            scores = jax.nn.sigmoid(xt @ gate_w.T)
            original_scores = scores
            sg = scores.reshape(T, N_GROUPS, E // N_GROUPS)
            group_scores = sg.max(axis=-1)
            _, gidx = jax.lax.top_k(group_scores, TOPK_GROUPS)
            gmask = jax.nn.one_hot(gidx, N_GROUPS, dtype=scores.dtype).sum(axis=1)
            masked = (sg * gmask[:, :, None]).reshape(T, E)
            _, idx = jax.lax.top_k(masked, TOPK)
            w = jnp.take_along_axis(original_scores, idx, axis=-1)
            w = w / w.sum(axis=-1, keepdims=True) * ROUTE_SCALE
            return (w, idx)
        shape = x.shape
        D = shape[-1]
        xt = x.reshape(-1, D)
        E = W1.shape[0]
        weights, indices = _gate(xt, gate_w)
        combine = jnp.einsum('tk,tke->te', weights, jax.nn.one_hot(indices, E, dtype=weights.dtype))
        h1 = jnp.einsum('td,eid->tei', xt, W1)
        h3 = jnp.einsum('td,eid->tei', xt, W3)
        g = jax.nn.silu(h1) * h3 * combine[:, :, None]
        y = jnp.einsum('tei,edi->td', g, W2)
        z = jax.nn.silu(xt @ Ws1.T) * (xt @ Ws3.T) @ Ws2.T
        return (y + z).reshape(shape)
    x = x + jnp.tanh(g_xattn[0]) * _L0_xattn_ref(_layernorm(x, axis=-1), fside_BxS2xS2_0, ctx_1024)
    x = x + jnp.tanh(g_ffn[0]) * _L0_ffn_ref(_layernorm(x, axis=-1), L0_ffn_router_w, L0_ffn_router_bias, L0_ffn_expert_gate_w, L0_ffn_expert_up_w, L0_ffn_expert_down_w, L0_ffn_shared_gate_w, L0_ffn_shared_up_w, L0_ffn_shared_down_w)
    x = x + jnp.tanh(g_xattn[1]) * _L1_xattn_ref(_layernorm(x, axis=-1), ctx_1024, L1_xattn_Wq, L1_xattn_Wk, L1_xattn_Wv, L1_xattn_Wo, L1_xattn_gq, L1_xattn_gk)
    x = x + jnp.tanh(g_ffn[1]) * _L1_ffn_ref(_layernorm(x, axis=-1), L1_ffn_gate_kernel, L1_ffn_w0_kernel, L1_ffn_w1_kernel, L1_ffn_wo_kernel)
    x = x + jnp.tanh(g_xattn[2]) * _L2_xattn_ref(_layernorm(x, axis=-1), ctx_1024, fside_BxSx2_0, fside_BxSx2_0, L2_xattn_Wq, L2_xattn_Wkv, L2_xattn_Wout, L2_xattn_bout)
    x = x + jnp.tanh(g_ffn[2]) * _L2_ffn_ref(_layernorm(x, axis=-1), L2_ffn_Wg, L2_ffn_W1, L2_ffn_W2, L2_ffn_W3, L2_ffn_A1, L2_ffn_B1, L2_ffn_A2, L2_ffn_B2, L2_ffn_A3, L2_ffn_B3)
    x = x + jnp.tanh(g_xattn[3]) * _L3_xattn_ref(_layernorm(x, axis=-1), ctx_1024, mask_BxS2_bf1, L3_xattn_Wq, L3_xattn_Wk, L3_xattn_Wv, L3_xattn_Wo)
    x = x + jnp.tanh(g_ffn[3]) * _L3_ffn_ref(_layernorm(x, axis=-1), L3_ffn_gate_w, L3_ffn_W1, L3_ffn_W2, L3_ffn_W3, L3_ffn_Ws1, L3_ffn_Ws2, L3_ffn_Ws3)
    return x

_drawn_inputs = setup_inputs


def setup_inputs(seed=0):
    import zlib

    import numpy as np

    out = dict(_drawn_inputs(seed))
    spreads = {'L0_ffn_router_bias': (0.0, 0.541),
     'L1_xattn_gq': (1.0, 0.6),
     'L1_xattn_gk': (1.0, 0.6),
     'L2_xattn_bout': (0.0, 0.1)}
    factors = {'fside_BxS2xS2_0': 2.677,
     'fside_BxSx2_0': 8.0,
     'g_ffn': 30.256,
     'L0_ffn_router_w': 3.71,
     'L0_ffn_expert_gate_w': 2.965,
     'L0_ffn_expert_up_w': 2.969,
     'L0_ffn_expert_down_w': 3.527,
     'L1_xattn_Wq': 2.889,
     'L1_xattn_Wk': 2.812,
     'L2_xattn_Wq': 8.0,
     'L2_xattn_Wkv': 8.0,
     'L2_xattn_Wout': 7.785,
     'L2_ffn_Wg': 8.0,
     'L2_ffn_A1': 8.0,
     'L2_ffn_B1': 8.0,
     'L2_ffn_A2': 8.0,
     'L2_ffn_B2': 8.0,
     'L2_ffn_A3': 8.0,
     'L2_ffn_B3': 8.0,
     'L3_xattn_Wq': 64.0,
     'L3_xattn_Wk': 64.0,
     'L3_xattn_Wv': 8.0,
     'L3_xattn_Wo': 8.0,
     'L3_ffn_gate_w': 8.0,
     'L3_ffn_W1': 8.0,
     'L3_ffn_W2': 8.0,
     'L3_ffn_W3': 8.0,
     'L3_ffn_Ws1': 3.621,
     'L3_ffn_Ws2': 3.58,
     'L3_ffn_Ws3': 3.603}
    for name, (base, spread) in spreads.items():
        noise = np.random.default_rng([zlib.crc32(name.encode()), seed]).standard_normal(out[name].shape)
        drawn = base * np.exp(spread * noise) if base else spread * noise
        out[name] = jnp.asarray(drawn.astype(out[name].dtype))
    for name, factor in factors.items():
        out[name] = (out[name] * factor).astype(out[name].dtype)
    return out
```

```python
from contextlib import ExitStack

import concourse.bass as bass
from concourse import mybir

ALU = mybir.AluOpType
ACT = mybir.ActivationFunctionType
AX_X = mybir.AxisListType.X
F32 = mybir.dt.float32
F32R = mybir.dt.float32r
BF16 = mybir.dt.bfloat16
U8 = mybir.dt.uint8

P = 128
B = 4
S = 256
TOK = B * S
D = 256
CH = D // P
CD = 128
HALF = TOK // 2
TILES = TOK // P
BLOCK = 3 * D


class Core:

    def __init__(self, nc, ctx):
        self.nc = nc
        self.ctx = ctx
        self.at = 17 * 1024
        self.phase = 0

    def sem(self, name):
        if self.phase:
            return self.nc.alloc_semaphore(name=name)
        return self.ctx.enter_context(self.nc.semaphore(name))

    def phase_sems(self):
        self.phase += 1
        names = ("mean_ready", "squared", "var_ready", "rstd_ready", "rstd_row_ready", "centred", "var_copied",
                 "normed", "h_hi_ready", "h_lo_ready", "x_ready")
        (self.mean_ready, self.squared, self.var_ready, self.rstd_ready, self.rstd_row_ready, self.centred,
         self.var_copied, self.normed, self.h_hi_ready, self.h_lo_ready, self.x_ready) = (
            self.sem(f"{name}{self.phase}") for name in names)

    def sb(self, name, shape, dt):
        size = 2 if dt == BF16 else 1 if dt == U8 else 4
        for n in shape[1:]:
            size *= n
        self.at = (self.at + 31) // 32 * 32
        t = self.nc.alloc_sbuf_tensor_at(name, shape, dt, offset=self.at)
        self.at += size
        return t


def f32(ap):
    return ap.bitcast(F32)


def mm3(pe, out, w_hi, w_lo, v_hi, v_lo, first, last):
    pe.matmul(out, w_hi, v_hi, start=first, stop=False)
    pe.matmul(out, w_lo, v_hi, start=False, stop=False)
    return pe.matmul(out, w_hi, v_lo, start=False, stop=last)


class Chain:

    def __init__(self, eng, sem, count=0):
        self.eng, self.sem, self.count = eng, sem, count

    def done(self, ins):
        self.count += 1
        ins.then_inc(self.sem, 1)
        self.eng.wait_ge(self.sem, self.count)




def norm_tensor(pe, k, half):
    n = half
    cols = slice(half * HALF, (half + 1) * HALF)
    for c in range(CH):
        last = pe.matmul(k.bank[half][:, :], k.mean_w[:, :], k.x[:, c, cols], start=(c == 0), stop=(c == CH - 1))
    last.then_inc(k.mean_ready, 1)
    pe.wait_ge(k.squared, n + 1)
    for t in range(half * 4, half * 4 + 4):
        for c in range(CH):
            last = pe.matmul(k.bank[7][:, 504 + t:505 + t], k.sq[:, c, t * P:(t + 1) * P], k.mean_w[:, 0:1],
                             start=(c == 0), stop=(c == CH - 1))
    last.then_inc(k.var_ready, 1)
    pe.wait_ge(k.rstd_ready, n + 1)
    for t in range(4):
        last = pe.transpose(k.bank[2 + half][:, t * P:(t + 1) * P],
                            k.rstd[:, half * 4 + t:half * 4 + t + 1].to_broadcast([P, P]), k.ident[:, :])
    last.then_inc(k.rstd_row_ready, 1)


def norm_scalar(act, k, half, parts=True):
    n = half
    cols = slice(half * HALF, (half + 1) * HALF)
    act.wait_ge(k.centred, n + 1)
    act.activation(k.sq[:, :, cols], k.cen[:, :, cols], ACT.Square).then_inc(k.squared, 1)
    if parts:
        act.wait_ge(k.normed, n + 1)
        act.activation(k.h_hi[:, :, cols], k.cen[:, :, cols], ACT.Copy).then_inc(k.h_hi_ready, 1)


def norm_vector(dve, k, half):
    n = half
    cols = slice(half * HALF, (half + 1) * HALF)
    dve.wait_ge(k.mean_ready, n + 1)
    dve.tensor_tensor(k.cen[:, :, cols], k.x[:, :, cols],
                      k.bank[half][:, :].unsqueeze(1).to_broadcast([P, CH, HALF]), ALU.subtract).then_inc(k.centred, 1)
    dve.wait_ge(k.var_ready, n + 1)
    dve.tensor_scalar(k.var[:, half * 4:half * 4 + 4], k.bank[7][:, 504 + half * 4:508 + half * 4], 1e-5, None,
                      ALU.add).then_inc(k.var_copied, 1)
    dve.wait_ge(k.squared, n + 1)
    dve.wait_ge(k.rstd_row_ready, n + 1)
    dve.tensor_tensor(k.cen[:, :, cols], k.cen[:, :, cols],
                      k.bank[2 + half][:, :].unsqueeze(1).to_broadcast([P, CH, HALF]), ALU.mult).then_inc(k.normed, 1)


def norm_gpsimd(pool, k, half, parts=True):
    n = half
    cols = slice(half * HALF, (half + 1) * HALF)
    pool.wait_ge(k.var_copied, n + 1)
    pool.tensor_tensor(k.rstd[:, half * 4:half * 4 + 4], k.var[:, half * 4:half * 4 + 4],
                       k.minus_half[:, :].to_broadcast([P, 4]), ALU.pow).then_inc(k.rstd_ready, 1)
    if not parts:
        return
    pool.wait_ge(k.h_hi_ready, n + 1)
    pool.tensor_tensor(k.h_lo[:, :, cols], k.cen[:, :, cols], f32(k.h_hi[:, :, cols]), ALU.subtract)\
        .then_inc(k.h_lo_ready, 1)




def rank(dve, chain, k, out, values, n, tiles=TILES):
    gt = k.cmp_gt[:, 0:tiles * n * n].rearrange("p (t i j) -> p t i j", t=tiles, i=n)
    eq = k.cmp_eq[:, 0:tiles * n * n].rearrange("p (t i j) -> p t i j", t=tiles, i=n)
    before = k.before[:, :].rearrange("p (i j) -> p i j", i=16)[:, 0:n, 0:n]
    vj = values.unsqueeze(2).to_broadcast([P, tiles, n, n])
    vi = values.unsqueeze(3).to_broadcast([P, tiles, n, n])
    dve.tensor_tensor(gt, vj, vi, ALU.is_gt)
    chain.done(dve.tensor_tensor(eq, vj, vi, ALU.is_equal))
    chain.done(dve.tensor_tensor(eq, eq, before.unsqueeze(1).to_broadcast([P, tiles, n, n]), ALU.mult))
    chain.done(dve.tensor_tensor(gt, gt, eq, ALU.add))
    chain.done(dve.tensor_reduce(out, gt, AX_X, ALU.add))


def route_vector(dve, chain, k, f):
    n = f.experts
    if f.kind == "sigmoid_top4":
        dve.wait_ge(f.score_ready, 1)
        chain.done(dve.tensor_tensor(f.choice[:, :, :], f.score[:, :, :],
                                     f.bias[:, :].unsqueeze(1).to_broadcast([P, TILES, n]), ALU.add))
        rank(dve, chain, k, f.rank[:, :, :], f.choice[:, :, :], n)
        keep = 4
    elif f.kind == "group_top4":
        dve.wait_ge(f.score_ready, 1)
        groups = n // 4
        chain.done(dve.tensor_reduce(f.group[:, :, :], f.score[:, :, :].rearrange("p t (g e) -> p t g e", e=4),
                                     AX_X, ALU.max))
        rank(dve, chain, k, f.group_rank[:, :, :], f.group[:, :, :], groups)
        chain.done(dve.tensor_scalar(f.group[:, :, :], f.group_rank[:, :, :], 2.0, None, ALU.is_lt))
        chain.done(dve.tensor_tensor(f.choice[:, :, :].rearrange("p t (g e) -> p (t g) e", e=4),
                                     f.score[:, :, :].rearrange("p t (g e) -> p (t g) e", e=4),
                                     f.group[:, :, :].rearrange("p t g -> p (t g)").unsqueeze(2)
                                     .to_broadcast([P, TILES * groups, 4]), ALU.mult))
        rank(dve, chain, k, f.rank[:, :, :], f.choice[:, :, :], n)
        keep = 4
    else:
        dve.wait_ge(f.logits_ready, 1)
        chain.done(dve.tensor_copy(f.choice[:, :, :], f.logits))
        chain.done(dve.tensor_reduce(f.top[:, :], f.choice[:, :, :], AX_X, ALU.max))
        dve.tensor_tensor(f.shifted[:, :, :], f.choice[:, :, :],
                          f.top[:, :].unsqueeze(2).to_broadcast([P, TILES, n]), ALU.subtract)\
            .then_inc(f.shifted_ready, 1)
        rank(dve, chain, k, f.rank[:, :, :], f.choice[:, :, :], n)
        dve.wait_ge(f.score_ready, 1)
        keep = 2
    chain.done(dve.scalar_tensor_tensor(f.chosen[:, :, :], f.rank[:, :, :], float(keep), f.score[:, :, :],
                                        ALU.is_lt, ALU.mult))
    chain.done(dve.tensor_reduce(f.total[:, :], f.chosen[:, :, :], AX_X, ALU.add))
    if f.kind == "sigmoid_top4":
        chain.done(dve.tensor_scalar(f.total[:, :], f.total[:, :], 1e-20, None, ALU.add))
    chain.done(dve.reciprocal(f.total[:, :], f.total[:, :]))
    chain.done(dve.tensor_tensor(f.comb[:, :, 0:n], f.chosen[:, :, :],
                                 f.total[:, :].unsqueeze(2).to_broadcast([P, TILES, n]), ALU.mult))


def three_parts(dve, chain, parts, values, rest, n):
    chain.done(dve.tensor_copy(parts[:, :, 0:n], values))
    chain.done(dve.tensor_tensor(rest, values, parts[:, :, 0:n], ALU.subtract))
    chain.done(dve.tensor_copy(parts[:, :, 32:32 + n], rest))
    chain.done(dve.tensor_tensor(rest, rest, parts[:, :, 32:32 + n], ALU.subtract))
    return dve.tensor_copy(parts[:, :, 64:64 + n], rest)


class Ffn:
    pass


def ffn_phase(k, tag, kind, experts, shared, blocks, gate, weights, router, select, bias):
    nc = k.nc
    f = Ffn()
    f.kind, f.experts = kind, experts
    base = k.at
    rows = experts + (1 if shared else 0)
    raw = [k.sb(f"{tag}_raw{s}", [P, BLOCK], F32) for s in range(2)]
    w_hi = [k.sb(f"{tag}_w_hi{s}", [P, BLOCK], F32R) for s in range(2)]
    w_lo = [k.sb(f"{tag}_w_lo{s}", [P, BLOCK], F32R) for s in range(2)]
    silu = [k.sb(f"{tag}_silu{s}", [P, HALF], F32) for s in range(2)]
    gated = [k.sb(f"{tag}_gated{s}", [P, HALF], F32) for s in range(2)]
    act32 = [k.sb(f"{tag}_act32{s}", [P, HALF], F32) for s in range(2)]
    a_hi = [k.sb(f"{tag}_a_hi{s}", [P, HALF], F32R) for s in range(2)]
    a_lo = [k.sb(f"{tag}_a_lo{s}", [P, HALF], F32R) for s in range(2)]
    sel = k.sb(f"{tag}_sel", [P, blocks * P], BF16)
    rw = k.sb(f"{tag}_rw", [P, CH, experts], F32)
    rw_hi = k.sb(f"{tag}_rw_hi", [P, CH, experts], F32R)
    rw_lo = k.sb(f"{tag}_rw_lo", [P, CH, experts], F32R)
    if bias is not None:
        f.bias = k.sb(f"{tag}_bias", [P, experts], F32)
    f.score, f.choice, f.shifted, f.rank, f.chosen = (
        k.sb(f"{tag}_{name}", [P, TILES, experts], F32) for name in ("score", "choice", "shifted", "rank", "chosen"))
    k.cmp_gt = k.sb(f"{tag}_cmp_gt", [P, TILES * 256], F32)
    k.cmp_eq = k.sb(f"{tag}_cmp_eq", [P, TILES * 256], F32)
    f.group = k.sb(f"{tag}_group", [P, TILES, 4], F32)
    f.group_rank = k.sb(f"{tag}_group_rank", [P, TILES, 4], F32)
    f.top = k.sb(f"{tag}_top", [P, TILES], F32)
    f.total = k.sb(f"{tag}_total", [P, TILES], F32)
    f.comb = k.sb(f"{tag}_comb", [P, TILES, rows], F32)
    rest = k.sb(f"{tag}_rest", [P, TILES, rows], F32)
    parts = k.sb(f"{tag}_parts", [P, TILES, P], BF16)
    comb_t = k.sb(f"{tag}_comb_t", [P, TOK], BF16)

    names = ("small_loaded", "router_hi", "router_lo", "zeroed", "logits_ready", "shifted_ready", "score_ready",
             "chain", "parts_ready", "turned", "comb_t_ready", "w_hi_ready", "w_lo_ready", "g_ready", "u_ready",
             "cb_ready", "silu_ready", "gated_ready", "act_ready", "a_hi_ready", "a_lo_ready", "y_done")
    sem = {name: k.sem(f"{tag}_{name}") for name in names}
    raw_loaded = [k.sem(f"{tag}_raw_loaded{s}") for s in range(2)]
    f.logits_ready, f.shifted_ready, f.score_ready = sem["logits_ready"], sem["shifted_ready"], sem["score_ready"]
    small_loaded, chain_sem, y_done = sem["small_loaded"], sem["chain"], sem["y_done"]
    w_hi_ready, w_lo_ready = sem["w_hi_ready"], sem["w_lo_ready"]
    g_ready, u_ready, cb_ready = sem["g_ready"], sem["u_ready"], sem["cb_ready"]
    silu_ready, gated_ready, act_ready = sem["silu_ready"], sem["gated_ready"], sem["act_ready"]
    a_hi_ready, a_lo_ready = sem["a_hi_ready"], sem["a_lo_ready"]

    y = [[k.bank[2 * c + half] for half in range(2)] for c in range(CH)]
    g_ps, u_ps, cb_ps = k.bank[4], k.bank[5], k.bank[6]
    f.logits = k.bank[7][:, 0:TILES * experts].rearrange("p (t e) -> p t e", e=experts)
    turned = k.bank[7][:, :].bitcast(BF16)
    small_loads = 2 + (1 if bias is not None else 0)

    loop_to = (blocks - 1) // 2

    def over_blocks(eng, body):
        body(0, 0, True)
        body(1, 1, True)
        with eng.Fori(1, loop_to) as pair:
            body(pair * 2, 0, True)
            body(pair * 2 + 1, 1, True)
        for b in range(2 * loop_to, blocks):
            body(b, b % 2, b + 1 < blocks)

    def static(b):
        return isinstance(b, int)

    with nc.Block() as block:

        @block.sync
        def _(sp):
            sp.dma_start(raw[0][:, :], weights[0, :, :]).then_inc(raw_loaded[0], 16)
            sp.dma_start(rw[:, :, :], router).then_inc(small_loaded, 16)
            sp.dma_start(sel[:, :], select).then_inc(small_loaded, 16)
            if bias is not None:
                sp.dma_start(f.bias[:, :], bias.partition_broadcast(P)).then_inc(small_loaded, 16)
            sp.dma_start(raw[1][:, :], weights[1, :, :]).then_inc(raw_loaded[1], 16)

            def load(b, s):
                sp.wait_ge(w_hi_ready, b - 1)
                sp.wait_ge(w_lo_ready, b - 1)
                sp.dma_start(raw[s][:, :], weights[bass.ds(b, 1), :, :].rearrange("b p n -> p (b n)"))\
                    .then_inc(raw_loaded[s], 16)

            with sp.Fori(1, loop_to) as pair:
                load(pair * 2, 0)
                load(pair * 2 + 1, 1)
            for b in range(2 * loop_to, blocks):
                load(b, b % 2)

        @block.tensor
        def _(pe):
            norm_tensor(pe, k, 0)
            norm_tensor(pe, k, 1)
            pe.wait_ge(k.h_hi_ready, 2)
            pe.wait_ge(k.h_lo_ready, 2)
            pe.wait_ge(sem["router_hi"], 1)
            pe.wait_ge(sem["router_lo"], 1)
            for t in range(TILES):
                cols = slice(t * P, (t + 1) * P)
                for c in range(CH):
                    last = mm3(pe, f.logits[:, t, :], k.h_hi[:, c, cols], k.h_lo[:, c, cols], rw_hi[:, c, :],
                               rw_lo[:, c, :], c == 0, c == CH - 1)
            last.then_inc(f.logits_ready, 1)
            pe.wait_ge(sem["zeroed"], 1)
            for c in range(CH):
                for half in range(2):
                    pe.matmul(y[c][half][:, :], k.zeros[:, 0:P], k.zeros[:, :], start=True, stop=False)

            def add_y(j, half, s, last_block=False):
                pe.wait_ge(a_hi_ready, j + 1)
                pe.wait_ge(a_lo_ready, j + 1)
                for c in range(CH):
                    w = slice(2 * D + c * P, 2 * D + (c + 1) * P)
                    last = mm3(pe, y[c][half][:, :], w_hi[s][:, w], w_lo[s][:, w], a_hi[half][:, :],
                               a_lo[half][:, :], False, last_block)
                last.then_inc(y_done, 1)

            def body(b, s, _more):
                pe.wait_ge(w_hi_ready, b + 1)
                pe.wait_ge(w_lo_ready, b + 1)
                for half in range(2):
                    j = b * 2 + half
                    cols = slice(half * HALF, (half + 1) * HALF)
                    first = static(b) and j == 0
                    for out, at, ready, free in ((g_ps, 0, g_ready, silu_ready), (u_ps, D, u_ready, gated_ready)):
                        if not first:
                            pe.wait_ge(free, j)
                        for c in range(CH):
                            w = slice(at + c * P, at + (c + 1) * P)
                            last = mm3(pe, out[:, :], w_hi[s][:, w], w_lo[s][:, w], k.h_hi[:, c, cols],
                                       k.h_lo[:, c, cols], c == 0, c == CH - 1)
                        last.then_inc(ready, 1)
                    if first:
                        for t in range(TILES):
                            if t == 0:
                                pe.wait_ge(sem["parts_ready"], 1)
                            last = pe.transpose(turned[:, t * P:(t + 1) * P], parts[:, t, :], k.ident_bf[:, :])
                        last.then_inc(sem["turned"], 1)
                        pe.wait_ge(sem["comb_t_ready"], 1)
                    else:
                        pe.wait_ge(act_ready, j)
                    sel_b = sel[:, bass.ds(b * P, P)]
                    pe.matmul(cb_ps[:, :], sel_b, comb_t[:, cols], start=True, stop=True).then_inc(cb_ready, 1)
                    if not first:
                        add_y(j - 1, 1 - half, 1 - s if half == 0 else s,
                              static(b) and b == blocks - 1 and half == 1)

            over_blocks(pe, body)
            add_y(2 * blocks - 1, 1, (blocks - 1) % 2, True)

        @block.scalar
        def _(act):
            def split(b, s):
                act.wait_ge(raw_loaded[s], (b // 2) * 16 + 16 if static(b) else b * 8 + (16 - 8 * s))
                if not static(b) or b >= 2:
                    act.wait_ge(y_done, b * 2 - 2)
                act.activation(w_hi[s][:, :], raw[s][:, :], ACT.Copy).then_inc(w_hi_ready, 1)

            split(0, 0)
            act.wait_ge(small_loaded, 16 * small_loads)
            act.activation(rw_hi[:, :, :], rw[:, :, :], ACT.Copy).then_inc(sem["router_hi"], 1)
            norm_scalar(act, k, 0)
            norm_scalar(act, k, 1)
            if kind == "softmax_top2":
                act.wait_ge(f.shifted_ready, 1)
                act.activation(f.score[:, :, :], f.shifted[:, :, :], ACT.Exp).then_inc(f.score_ready, 1)
            else:
                act.wait_ge(f.logits_ready, 1)
                act.activation(f.score[:, :, :], f.logits, ACT.Sigmoid).then_inc(f.score_ready, 1)

            def body(b, s, more):
                for half in range(2):
                    j = b * 2 + half
                    act.wait_ge(g_ready, j + 1)
                    if not static(b) or j >= 2:
                        act.wait_ge(gated_ready, j - 1)
                    act.activation(silu[half][:, :], g_ps[:, :], ACT.Silu).then_inc(silu_ready, 1)
                    act.wait_ge(act_ready, j + 1)
                    if not static(b) or j >= 2:
                        act.wait_ge(y_done, j - 1)
                    act.activation(a_hi[half][:, :], act32[half][:, :], ACT.Copy).then_inc(a_hi_ready, 1)
                    if half == 0 and more:
                        split(b + 1, 1 - s)

            over_blocks(act, body)

        @block.gpsimd
        def _(pool):
            pool.memset(parts[:, :, :], 0.0).then_inc(sem["zeroed"], 1)

            def split(b, s):
                pool.wait_ge(w_hi_ready, b + 1)
                pool.tensor_tensor(w_lo[s][:, :], raw[s][:, :], f32(w_hi[s][:, :]), ALU.subtract)\
                    .then_inc(w_lo_ready, 1)

            split(0, 0)
            pool.wait_ge(sem["router_hi"], 1)
            pool.tensor_tensor(rw_lo[:, :, :], rw[:, :, :], f32(rw_hi[:, :, :]), ALU.subtract)\
                .then_inc(sem["router_lo"], 1)
            norm_gpsimd(pool, k, 0)
            norm_gpsimd(pool, k, 1)
            split(1, 1)
            with pool.Fori(1, loop_to) as pair:
                split(pair * 2, 0)
                split(pair * 2 + 1, 1)
            for b in range(2 * loop_to, blocks):
                split(b, b % 2)

        @block.vector
        def _(dve):
            chain = Chain(dve, chain_sem)
            norm_vector(dve, k, 0)
            norm_vector(dve, k, 1)
            dve.wait_ge(sem["zeroed"], 1)
            dve.wait_ge(small_loaded, 16 * small_loads)
            route_vector(dve, chain, k, f)
            if shared:
                chain.done(dve.memset(f.comb[:, :, experts:experts + 1], 1.0))
            three_parts(dve, chain, parts, f.comb[:, :, :], rest[:, :, :], rows).then_inc(sem["parts_ready"], 1)
            dve.wait_ge(sem["turned"], 1)
            dve.tensor_copy(comb_t[:, :], turned).then_inc(sem["comb_t_ready"], 1)

            def body(b, _s, _more):
                for half in range(2):
                    j = b * 2 + half
                    dve.wait_ge(silu_ready, j + 1)
                    dve.wait_ge(u_ready, j + 1)
                    dve.tensor_tensor(gated[half][:, :], silu[half][:, :], u_ps[:, :], ALU.mult)\
                        .then_inc(gated_ready, 1)
                    dve.wait_ge(gated_ready, j + 1)
                    dve.wait_ge(cb_ready, j + 1)
                    dve.tensor_tensor(act32[half][:, :], gated[half][:, :], cb_ps[:, :], ALU.mult)\
                        .then_inc(act_ready, 1)
                    dve.wait_ge(a_hi_ready, j + 1)
                    dve.tensor_tensor(a_lo[half][:, :], act32[half][:, :], f32(a_hi[half][:, :]), ALU.subtract)\
                        .then_inc(a_lo_ready, 1)

            over_blocks(dve, body)
            dve.wait_ge(y_done, 2 * blocks)
            for c in range(CH):
                for half in range(2):
                    cols = slice(half * HALF, (half + 1) * HALF)
                    dve.scalar_tensor_tensor(k.x[:, c, cols], y[c][half][:, :], k.gates[:, gate:gate + 1],
                                             k.x[:, c, cols], ALU.mult, ALU.add).then_inc(k.x_ready, 1)

    k.at = base



HEADS = 16
HD = 128
STEPS_PER_HEAD = B


def need(eng, sem, value):
    if not isinstance(value, int) or value > 0:
        eng.wait_ge(sem, value)


def over_heads(eng, body):
    body(0, True, False)
    with eng.Fori(1, HEADS - 1) as h:
        body(h, False, False)
    body(HEADS - 1, False, True)


def xattn_phase(k, tag, normed, gate, weights, gq, gk, masked):
    nc = k.nc
    base = k.at
    scale = float(HD) ** -0.5
    raw = k.sb(f"{tag}_raw", [P, BLOCK], F32)
    w_hi = k.sb(f"{tag}_w_hi", [P, BLOCK], F32R)
    w_lo = k.sb(f"{tag}_w_lo", [P, BLOCK], F32R)
    vo_hi = k.sb(f"{tag}_vo_hi", [P, D], F32R)
    vo_lo = k.sb(f"{tag}_vo_lo", [P, D], F32R)
    q32 = k.sb(f"{tag}_q32", [P, S], F32)
    q_hi = [k.sb(f"{tag}_q_hi{s}", [P, S], F32R) for s in range(2)]
    q_lo = [k.sb(f"{tag}_q_lo{s}", [P, S], F32R) for s in range(2)]
    if normed:
        q_sq = k.sb(f"{tag}_q_sq", [P, S], F32)
        k_sq = k.sb(f"{tag}_k_sq", [P, S], F32)
        k_raw = k.sb(f"{tag}_k_raw", [P, S], F32)
        k32 = k.sb(f"{tag}_k32", [P, S], F32)
        k_hi = [k.sb(f"{tag}_k_hi{s}", [P, S], F32R) for s in range(2)]
        k_lo = [k.sb(f"{tag}_k_lo{s}", [P, S], F32R) for s in range(2)]
        rms = k.sb(f"{tag}_rms", [P, 4], F32)
        rrms = [k.sb(f"{tag}_rrms{s}", [P, 4], F32) for s in range(2)]
        gain = k.sb(f"{tag}_gain", [P, 2], F32)
        gains = k.sb(f"{tag}_gains", [P, 1], F32)
    else:
        am_hi = k.sb(f"{tag}_am_hi", [P, CH, CD], F32R)
        am_lo = k.sb(f"{tag}_am_lo", [P, CH, CD], F32R)
        s_masked = k.sb(f"{tag}_s_masked", [P, 2, S], F32)
        unread = k.sb(f"{tag}_unread", [P, 1], F32)
    probs = k.sb(f"{tag}_probs", [P, 2, S], F32)
    top = k.sb(f"{tag}_top", [P, 2], F32)
    shift = k.sb(f"{tag}_shift", [P, 2], F32)
    total = k.sb(f"{tag}_total", [P, 2], F32)
    rtotal = k.sb(f"{tag}_rtotal", [P, 2], F32)
    pt_hi = k.sb(f"{tag}_pt_hi", [P, 2, S], F32R)
    pt_lo = k.sb(f"{tag}_pt_lo", [P, 2, S], F32R)
    z_hi = k.sb(f"{tag}_z_hi", [P, S], F32R)
    z_lo = k.sb(f"{tag}_z_lo", [P, S], F32R)

    def sem(name):
        return k.sem(f"{tag}_{name}")

    raw_loaded, small_loaded, small_ready = sem("raw_loaded"), sem("small_loaded"), sem("small_ready")
    w_hi_ready, w_lo_ready = sem("w_hi_ready"), sem("w_lo_ready")
    vo_made, vo_hi_ready, vo_lo_ready = sem("vo_made"), sem("vo_hi_ready"), sem("vo_lo_ready")
    am_made, am_hi_ready, am_lo_ready = sem("am_made"), sem("am_hi_ready"), sem("am_lo_ready")
    q_made, q_copied, q_hi_ready, q_lo_ready = sem("q_made"), sem("q_copied"), sem("q_hi_ready"), sem("q_lo_ready")
    k_copied, squares_ready, stats_ready, rms_ready = (
        sem("k_copied"), sem("squares_ready"), sem("stats_ready"), sem("rms_ready"))
    rrms_ready, row_ready, k_normed = sem("rrms_ready"), sem("row_ready"), sem("k_normed")
    k_hi_ready, k_lo_ready = sem("k_hi_ready"), sem("k_lo_ready")
    scores_ready, top_ready, shift_ready = sem("scores_ready"), sem("top_ready"), sem("shift_ready")
    exp_ready, rtotal_ready, probs_ready = sem("exp_ready"), sem("rtotal_ready"), sem("probs_ready")
    turned, pt_hi_ready, pt_lo_ready = sem("turned"), sem("pt_hi_ready"), sem("pt_lo_ready")
    z_made, z_hi_ready, z_lo_ready, y_done = sem("z_made"), sem("z_hi_ready"), sem("z_lo_ready"), sem("y_done")

    y = [[k.bank[2 * c + half] for half in range(2)] for c in range(CH)]
    q_ps, k_ps = k.bank[4][:, 0:S], k.bank[4][:, S:2 * S]
    s_ps = k.bank[5][:, :].rearrange("p (t n) -> p t n", t=2)
    t_ps = k.bank[6][:, :].rearrange("p (t n) -> p t n", t=2)
    z_ps, am_ps = k.bank[7][:, 0:S], k.bank[7][:, S:2 * S]
    row_ps, stats_ps = k.bank[6][:, 0:S], k.bank[6][:, S:S + 4]
    steps = HEADS * STEPS_PER_HEAD

    with nc.Block() as block:

        @block.sync
        def _(sp):
            sp.dma_start(raw[:, :], weights[0, :, :]).then_inc(raw_loaded, 16)
            if normed:
                sp.dma_start(gain[:, 0:1], gq.unsqueeze(1)).then_inc(small_loaded, 16)
                sp.dma_start(gain[:, 1:2], gk.unsqueeze(1)).then_inc(small_loaded, 16)
            with sp.Fori(1, HEADS) as h:
                sp.wait_ge(w_hi_ready, h)
                sp.wait_ge(w_lo_ready, h)
                sp.dma_start(raw[:, :], weights[bass.ds(h, 1), :, :].rearrange("h p n -> p (h n)"))\
                    .then_inc(raw_loaded, 16)

        @block.tensor
        def _(pe):
            norm_tensor(pe, k, 0)
            norm_tensor(pe, k, 1)

            def make_am(h):
                pe.wait_ge(w_hi_ready, h + 1)
                pe.wait_ge(w_lo_ready, h + 1)
                need(pe, z_hi_ready, h * STEPS_PER_HEAD - 3)
                need(pe, z_lo_ready, h * STEPS_PER_HEAD - 3)
                for c in range(CH):
                    w = slice(c * P, (c + 1) * P)
                    last = mm3(pe, am_ps[:, c * CD:(c + 1) * CD], w_hi[:, w], w_lo[:, w], w_hi[:, D:D + CD],
                               w_lo[:, D:D + CD], True, True)
                last.then_inc(am_made, 1)

            def make_vo(h, j):
                pe.wait_ge(q_copied, j + 1)
                if normed:
                    pe.wait_ge(squares_ready, 2 * j + 2)
                    pe.wait_ge(k_copied, j + 1)
                w = slice(D + CD, 2 * D)
                mm3(pe, q_ps, w_hi[:, w], w_lo[:, w], w_hi[:, 2 * D:], w_lo[:, 2 * D:], True, True)\
                    .then_inc(vo_made, 1)

            def project(h, b, j):
                if b == 0:
                    if normed:
                        pe.wait_ge(w_hi_ready, h + 1)
                        pe.wait_ge(w_lo_ready, h + 1)
                    else:
                        pe.wait_ge(am_hi_ready, h + 1)
                        pe.wait_ge(am_lo_ready, h + 1)
                if b == 3:
                    pe.wait_ge(vo_hi_ready, h + 1)
                    pe.wait_ge(vo_lo_ready, h + 1)
                need(pe, q_copied, j)
                if normed:
                    need(pe, squares_ready, 2 * j)
                    need(pe, k_copied, j)
                cols = slice(b * S, (b + 1) * S)
                for c in range(CH):
                    if normed:
                        part_hi, part_lo = w_hi[:, c * P:(c + 1) * P], w_lo[:, c * P:(c + 1) * P]
                    else:
                        part_hi, part_lo = am_hi[:, c, :], am_lo[:, c, :]
                    last = mm3(pe, q_ps, part_hi, part_lo, k.h_hi[:, c, cols], k.h_lo[:, c, cols], c == 0,
                               c == CH - 1)
                if normed:
                    last = mm3(pe, k_ps, w_hi[:, D:D + CD], w_lo[:, D:D + CD], k.ctx_hi[:, cols], k.ctx_lo[:, cols],
                               True, True)
                last.then_inc(q_made, 1)

            def stats(j):
                pe.wait_ge(squares_ready, 2 * j + 2)
                need(pe, pt_hi_ready, j - 1)
                need(pe, pt_lo_ready, j - 1)
                for n, sq in enumerate((q_sq, k_sq)):
                    for t in range(2):
                        last = pe.matmul(stats_ps[:, 2 * n + t:2 * n + t + 1], sq[:, t * P:(t + 1) * P],
                                         k.head_w[:, :], start=True, stop=True)
                last.then_inc(stats_ready, 1)

            def key_row(s, j):
                pe.wait_ge(rrms_ready, j + 1)
                for t in range(2):
                    last = pe.transpose(row_ps[:, t * P:(t + 1) * P], rrms[s][:, 2 + t:3 + t].to_broadcast([P, P]),
                                        k.ident[:, :])
                last.then_inc(row_ready, 1)

            def scores(b, j):
                s = b % 2
                cols = slice(b * S, (b + 1) * S)
                pe.wait_ge(q_hi_ready, j + 1)
                pe.wait_ge(q_lo_ready, j + 1)
                if normed:
                    pe.wait_ge(k_hi_ready, j + 1)
                    pe.wait_ge(k_lo_ready, j + 1)
                    need(pe, exp_ready, 2 * j)
                    right_hi, right_lo = k_hi[s][:, :], k_lo[s][:, :]
                else:
                    need(pe, top_ready, 2 * j)
                    right_hi, right_lo = k.ctx_hi[:, cols], k.ctx_lo[:, cols]
                for t in range(2):
                    rows = slice(t * P, (t + 1) * P)
                    last = mm3(pe, s_ps[:, t, :], q_hi[s][:, rows], q_lo[s][:, rows], right_hi, right_lo, True, True)
                last.then_inc(scores_ready, 1)

            def turn(j, more):
                pe.wait_ge(probs_ready, j + 1)
                if normed:
                    need(pe, k_normed, j + 2 if more else j + 1)
                need(pe, pt_lo_ready, j)
                need(pe, pt_hi_ready, j)
                for kt in range(2):
                    for t in range(2):
                        last = pe.transpose(t_ps[:, kt, t * P:(t + 1) * P], probs[:, t, kt * P:(kt + 1) * P],
                                            k.ident[:, :])
                last.then_inc(turned, 1)

            def mix(b, j, next_am=0):
                pe.wait_ge(pt_hi_ready, j + 1)
                pe.wait_ge(pt_lo_ready, j + 1)
                need(pe, z_hi_ready, j)
                need(pe, z_lo_ready, j)
                if not normed and b == 1:
                    need(pe, am_hi_ready, next_am)
                    need(pe, am_lo_ready, next_am)
                for kt in range(2):
                    last = mm3(pe, z_ps, k.keys_hi[:, 2 * b + kt, :], k.keys_lo[:, 2 * b + kt, :], pt_hi[:, kt, :],
                               pt_lo[:, kt, :], kt == 0, kt == 1)
                last.then_inc(z_made, 1)

            def add_y(h, b, j, end=False):
                pe.wait_ge(z_hi_ready, j + 1)
                pe.wait_ge(z_lo_ready, j + 1)
                if b == 0:
                    pe.wait_ge(vo_hi_ready, h + 1)
                    pe.wait_ge(vo_lo_ready, h + 1)
                cols = slice(b % 2 * S, (b % 2 + 1) * S)
                for c in range(CH):
                    w = slice(c * P, (c + 1) * P)
                    last = mm3(pe, y[c][b // 2][:, cols], vo_hi[:, w], vo_lo[:, w], z_hi[:, :], z_lo[:, :], False,
                               end and b % 2 == 1)
                last.then_inc(y_done, 1)

            pe.wait_ge(k.normed, 2)
            for c in range(CH):
                for half in range(2):
                    pe.matmul(y[c][half][:, :], k.zeros[:, 0:P], k.zeros[:, :], start=True, stop=False)
            if not normed:
                make_am(0)
            pe.wait_ge(k.h_hi_ready, 2)
            pe.wait_ge(k.h_lo_ready, 2)
            project(0, 0, 0)
            if normed:
                stats(0)
                key_row(0, 0)

            def body(h, first, last):
                for b in range(STEPS_PER_HEAD):
                    j = h * STEPS_PER_HEAD + b
                    more = not (last and b == 3)
                    next_h, next_b = (h, b + 1) if b < 3 else (h + 1, 0)
                    if more:
                        project(next_h, next_b, j + 1)
                    if b == 2 and not last and not normed:
                        make_am(h + 1)
                    scores(b, j)
                    if not (first and b < 2):
                        add_y(h if b >= 2 else h - 1, (b + 2) % 4, j - 2, last and b >= 2)
                    if b == 1 and not normed:
                        make_vo(h, j + 1)
                    if more and normed:
                        stats(j + 1)
                    if not (first and b == 0):
                        mix((b + 3) % 4, j - 1, 0 if last else h + 2)
                    if more and normed:
                        key_row((b + 1) % 2, j + 1)
                    if b == 1 and normed:
                        make_vo(h, j + 1)
                    turn(j, more)

            over_heads(pe, body)
            add_y(HEADS - 1, 2, steps - 2, True)
            mix(3, steps - 1)
            add_y(HEADS - 1, 3, steps - 1, True)

        @block.scalar
        def _(act):
            def split(h):
                act.wait_ge(raw_loaded, h * 16 + 16)
                if not isinstance(h, int) or h >= 1:
                    act.wait_ge(vo_made, h)
                    if normed:
                        act.wait_ge(q_made, h * STEPS_PER_HEAD)
                    else:
                        act.wait_ge(am_made, h)
                act.activation(w_hi[:, :], raw[:, :], ACT.Copy).then_inc(w_hi_ready, 1)

            def copy_am(h):
                act.wait_ge(am_made, h + 1)
                need(act, q_made, h * STEPS_PER_HEAD)
                act.activation(am_hi[:, :, :], am_ps.rearrange("p (c n) -> p c n", c=CH), ACT.Copy)\
                    .then_inc(am_hi_ready, 1)

            def copy_vo(h):
                act.wait_ge(vo_made, h + 1)
                need(act, y_done, h * STEPS_PER_HEAD)
                act.activation(vo_hi[:, :], q_ps, ACT.Copy).then_inc(vo_hi_ready, 1)

            def squares(j):
                act.wait_ge(q_made, j + 1)
                need(act, stats_ready, j)
                act.activation(k_sq[:, :], k_ps, ACT.Square).then_inc(squares_ready, 1)
                act.activation(q_sq[:, :], q_ps, ACT.Square).then_inc(squares_ready, 1)
                need(act, k_normed, j)
                act.activation(k_raw[:, :], k_ps, ACT.Copy, scale=gains[:, 0:1]).then_inc(k_copied, 1)

            def exps(s, j):
                act.wait_ge(shift_ready, j + 1)
                need(act, probs_ready, j)
                need(act, turned, j)
                for t in range(2):
                    if normed:
                        act.activation(probs[:, t, :], s_ps[:, t, :], ACT.Exp, bias=shift[:, t:t + 1],
                                       scale=rrms[s][:, t:t + 1], accum_out=total[:, t:t + 1]).then_inc(exp_ready, 1)
                    else:
                        act.activation(probs[:, t, :], s_masked[:, t, :], ACT.Exp, bias=shift[:, t:t + 1],
                                       scale=scale, accum_out=total[:, t:t + 1]).then_inc(exp_ready, 1)

            split(0)
            norm_scalar(act, k, 0)
            norm_scalar(act, k, 1)
            if normed:
                act.wait_ge(small_ready, 1)
                squares(0)
            else:
                copy_am(0)

            def body(h, first, last):
                for b in range(STEPS_PER_HEAD):
                    j = h * STEPS_PER_HEAD + b
                    more = not (last and b == 3)
                    if not last and b == 2 and not normed:
                        copy_am(h + 1)
                    exps(b % 2, j)
                    if b == 1 and not normed:
                        copy_vo(h)
                    if more and normed:
                        squares(j + 1)
                    if not (first and b == 0):
                        act.wait_ge(z_made, j)
                        need(act, y_done, j - 1)
                        act.activation(z_hi[:, :], z_ps, ACT.Copy).then_inc(z_hi_ready, 1)
                    act.wait_ge(turned, j + 1)
                    need(act, z_made, j)
                    act.activation(pt_hi[:, :, :], t_ps, ACT.Copy).then_inc(pt_hi_ready, 1)
                    if b == 1 and normed:
                        copy_vo(h)
                    if not last and b == (2 if normed else 1):
                        split(h + 1)

            over_heads(act, body)
            act.wait_ge(z_made, steps)
            act.wait_ge(y_done, steps - 1)
            act.activation(z_hi[:, :], z_ps, ACT.Copy).then_inc(z_hi_ready, 1)

        @block.vector
        def _(dve):
            def copy_q(j):
                dve.wait_ge(q_made, j + 1)
                if normed:
                    dve.wait_ge(squares_ready, 2 * j + 2)
                    dve.wait_ge(k_copied, j + 1)
                need(dve, q_lo_ready, j)
                need(dve, q_hi_ready, j)
                dve.tensor_copy(q32[:, :], q_ps).then_inc(q_copied, 1)

            def key_norm(s, j):
                dve.wait_ge(row_ready, j + 1)
                dve.wait_ge(k_copied, j + 1)
                need(dve, k_lo_ready, j)
                need(dve, k_hi_ready, j)
                dve.tensor_tensor(k32[:, :], k_raw[:, :], row_ps, ALU.mult).then_inc(k_normed, 1)

            def copy_stats(j):
                dve.wait_ge(stats_ready, j + 1)
                need(dve, rrms_ready, j)
                dve.tensor_scalar(rms[:, :], stats_ps, 1e-5, None, ALU.add).then_inc(rms_ready, 1)

            def vo_low(h):
                dve.wait_ge(vo_hi_ready, h + 1)
                dve.tensor_tensor(vo_lo[:, :], q_ps, f32(vo_hi[:, :]), ALU.subtract).then_inc(vo_lo_ready, 1)

            def am_low(h):
                dve.wait_ge(am_hi_ready, h + 1)
                dve.tensor_tensor(am_lo[:, :, :], am_ps.rearrange("p (c n) -> p c n", c=CH), f32(am_hi[:, :, :]),
                                  ALU.subtract).then_inc(am_lo_ready, 1)

            norm_vector(dve, k, 0)
            norm_vector(dve, k, 1)
            if normed:
                dve.wait_ge(small_loaded, 32)
                dve.scalar_tensor_tensor(gains[:, :], gain[:, 0:1], scale, gain[:, 1:2], ALU.mult, ALU.mult)\
                    .then_inc(small_ready, 1)
                copy_q(0)
                copy_stats(0)
                key_norm(0, 0)
            else:
                am_low(0)
                copy_q(0)

            def body(h, first, last):
                for b in range(STEPS_PER_HEAD):
                    j = h * STEPS_PER_HEAD + b
                    s = b % 2
                    more = not (last and b == 3)
                    dve.wait_ge(scores_ready, j + 1)
                    if normed:
                        dve.tensor_reduce(top[:, :], s_ps, AX_X, ALU.max).then_inc(top_ready, 2)
                        dve.wait_ge(top_ready, 2 * j + 2)
                        need(dve, exp_ready, 2 * j)
                        dve.scalar_tensor_tensor(shift[:, :], top[:, :], -1.0, rrms[s][:, 0:2], ALU.mult, ALU.mult)\
                            .then_inc(shift_ready, 1)
                    else:
                        need(dve, exp_ready, 2 * j)
                        dve.memset(unread[:, :], 0.0)
                        for t in range(2):
                            dve.tensor_tensor_reduce(s_masked[:, t, :], s_ps[:, t, :],
                                                     k.mask_bias[:, b * S:(b + 1) * S], 1.0, -3.0e38, ALU.add,
                                                     ALU.max, top[:, t:t + 1]).then_inc(top_ready, 1)
                        dve.wait_ge(top_ready, 2 * j + 2)
                        dve.tensor_scalar(shift[:, :], top[:, :], -scale, None, ALU.mult).then_inc(shift_ready, 1)
                    if more and not normed:
                        copy_q(j + 1)
                    if b == 2 and not last and not normed:
                        am_low(h + 1)
                    dve.wait_ge(exp_ready, 2 * j + 2)
                    dve.reciprocal(rtotal[:, :], total[:, :]).then_inc(rtotal_ready, 1)
                    if masked:
                        dve.wait_ge(rtotal_ready, 2 * j + 1)
                        dve.tensor_scalar(rtotal[:, :], rtotal[:, :], k.any_key[:, b:b + 1], None, ALU.mult)\
                            .then_inc(rtotal_ready, 1)
                        dve.wait_ge(rtotal_ready, 2 * j + 2)
                    else:
                        dve.wait_ge(rtotal_ready, j + 1)
                    dve.tensor_tensor(probs[:, :, :], probs[:, :, :],
                                      rtotal[:, :].unsqueeze(2).to_broadcast([P, 2, S]), ALU.mult)\
                        .then_inc(probs_ready, 1)
                    if b == 1 and not normed:
                        vo_low(h)
                    if more and normed:
                        copy_q(j + 1)
                        copy_stats(j + 1)
                    if not (first and b == 0):
                        dve.wait_ge(z_hi_ready, j)
                        dve.tensor_tensor(z_lo[:, :], z_ps, f32(z_hi[:, :]), ALU.subtract).then_inc(z_lo_ready, 1)
                    if more and normed:
                        key_norm((b + 1) % 2, j + 1)
                    if b == 1 and normed:
                        vo_low(h)
                    dve.wait_ge(pt_hi_ready, j + 1)
                    dve.tensor_tensor(pt_lo[:, :, :], t_ps, f32(pt_hi[:, :, :]), ALU.subtract)\
                        .then_inc(pt_lo_ready, 1)

            over_heads(dve, body)
            dve.wait_ge(z_hi_ready, steps)
            dve.tensor_tensor(z_lo[:, :], z_ps, f32(z_hi[:, :]), ALU.subtract).then_inc(z_lo_ready, 1)
            dve.wait_ge(y_done, steps)
            for c in range(CH):
                for half in range(2):
                    cols = slice(half * HALF, (half + 1) * HALF)
                    dve.scalar_tensor_tensor(k.x[:, c, cols], y[c][half][:, :], k.gates[:, gate:gate + 1],
                                             k.x[:, c, cols], ALU.mult, ALU.add).then_inc(k.x_ready, 1)

        @block.gpsimd
        def _(pool):
            def split(h):
                pool.wait_ge(w_hi_ready, h + 1)
                pool.tensor_tensor(w_lo[:, :], raw[:, :], f32(w_hi[:, :]), ALU.subtract).then_inc(w_lo_ready, 1)

            def parts(hi, lo, source, copied, hi_ready, lo_ready, j):
                pool.wait_ge(copied, j + 1)
                need(pool, scores_ready, j - 1)
                pool.tensor_tensor(hi[:, :], source[:, :], k.one[:, :].to_broadcast([P, S]), ALU.mult)\
                    .then_inc(hi_ready, 1)
                pool.wait_ge(hi_ready, j + 1)
                pool.tensor_tensor(lo[:, :], source[:, :], f32(hi[:, :]), ALU.subtract).then_inc(lo_ready, 1)

            def split_step(s, j):
                if normed:
                    pool.wait_ge(rms_ready, j + 1)
                    pool.tensor_tensor(rrms[s][:, :], rms[:, :], k.minus_half[:, :].to_broadcast([P, 4]), ALU.pow)\
                        .then_inc(rrms_ready, 1)
                parts(q_hi[s], q_lo[s], q32, q_copied, q_hi_ready, q_lo_ready, j)
                if normed:
                    parts(k_hi[s], k_lo[s], k32, k_normed, k_hi_ready, k_lo_ready, j)

            split(0)
            norm_gpsimd(pool, k, 0)
            norm_gpsimd(pool, k, 1)
            split_step(0, 0)

            def body(h, _first, last):
                for b in range(STEPS_PER_HEAD):
                    j = h * STEPS_PER_HEAD + b
                    if not (last and b == 3):
                        split_step((b + 1) % 2, j + 1)
                    if not last and b == (2 if normed else 1):
                        split(h + 1)

            over_heads(pool, body)

    k.at = base



Q_EPS = 1e-6
Q_MAX = 127.0
ROUND = 1.5 * 2.0 ** 23


class Quant:

    def __init__(self, k, name, n, turned, back):
        self.n, self.chunks = n, n // P
        self.turned, self.back = turned, back
        self.top = k.sb(f"{name}_top", [P, TILES], F32)
        self.step = k.sb(f"{name}_step", [P, TILES], F32)
        self.inverse = k.sb(f"{name}_inverse", [P, TILES], F32)
        self.ratio = k.sb(f"{name}_ratio", [P, TILES, n], F32)
        self.rows = k.sb(f"{name}_rows", [P, TILES, n], BF16)
        self.ints = k.sb(f"{name}_ints", [P, self.chunks, TOK], BF16)
        self.scaled_ready = k.sem(f"{name}_scaled_ready")
        self.turned_ready = k.sem(f"{name}_turned_ready")
        self.rows_ready = k.sem(f"{name}_rows_ready")
        self.back_ready = k.sem(f"{name}_back_ready")
        self.ints_ready = k.sem(f"{name}_ints_ready")

    def turn(self, pe, k, scaled):
        pe.wait_ge(self.scaled_ready, 1)
        for t in range(TILES):
            for c in range(self.chunks):
                last = pe.transpose(self.turned[:, t, c * P:(c + 1) * P], scaled[:, c, t * P:(t + 1) * P],
                                    k.ident[:, :])
        last.then_inc(self.turned_ready, 1)

    def round_rows(self, dve, chain):
        dve.wait_ge(self.turned_ready, 1)
        chain.done(dve.tensor_reduce(self.top[:, :], self.turned, AX_X, ALU.max, apply_absolute_value=True))
        chain.done(dve.tensor_scalar(self.step[:, :], self.top[:, :], Q_EPS, 1.0 / Q_MAX, ALU.max, ALU.mult))
        chain.done(dve.reciprocal(self.inverse[:, :], self.step[:, :]))
        chain.done(dve.tensor_tensor(self.ratio[:, :, :], self.turned,
                                     self.inverse[:, :].unsqueeze(2).to_broadcast([P, TILES, self.n]), ALU.mult))
        chain.done(dve.tensor_scalar(self.ratio[:, :, :], self.ratio[:, :, :], Q_MAX, -Q_MAX, ALU.min, ALU.max))
        dve.tensor_scalar(self.rows[:, :, :], self.ratio[:, :, :], ROUND, ROUND, ALU.add, ALU.subtract)\
            .then_inc(self.rows_ready, 1)

    def turn_back(self, pe, k):
        pe.wait_ge(self.rows_ready, 1)
        for t in range(TILES):
            for c in range(self.chunks):
                last = pe.transpose(self.back[:, c, t * P:(t + 1) * P], self.rows[:, t, c * P:(c + 1) * P],
                                    k.ident_bf[:, :])
        last.then_inc(self.back_ready, 1)

    def copy_back(self, act):
        act.wait_ge(self.back_ready, 1)
        act.activation(self.ints[:, :, :], self.back, ACT.Copy).then_inc(self.ints_ready, 1)

    def step_row(self, pe, k, out, ready):
        for t in range(TILES):
            last = pe.transpose(out[:, t * P:(t + 1) * P], self.step[:, t:t + 1].to_broadcast([P, P]), k.ident[:, :])
        last.then_inc(ready, 1)


def quant_phase(k, a):
    nc = k.nc
    base = k.at
    gate = 0
    w1 = k.sb("q_w1", [P, CH, TOK], F32)
    w2 = k.sb("q_w2", [P, 1, TOK], F32)
    act_t = k.sb("q_act", [P, 1, TOK], F32)
    scaled_act = k.sb("q_scaled_act", [P, 1, TOK], F32)
    row = k.sb("q_row", [P, TOK], F32)
    acc = k.sb("q_acc", [P, CH, TOK], F32)
    silu = k.sb("q_silu", [P, TOK], F32)
    half_col = k.sb("q_half", [P, 1], F32)
    tops = [[k.sb(f"q_top{i}{side}", [P, CH, B], F32) for side in "xw"] for i in (1, 2)]
    ratio = [k.sb(f"q_s_squared{i}", [P, CH, B], F32) for i in (1, 2)]
    s = [k.sb(f"q_s{i}", [P, CH, B], F32) for i in (1, 2)]
    rs = [k.sb(f"q_rs{i}", [P, CH, B], F32) for i in (1, 2)]
    out_gain = k.sb("q_out_gain", [P, TILES], F32)

    def tiles_of(first, n):
        return k.psum[:, first * HALF:first * HALF + TILES * n].rearrange("p (t n) -> p t n", n=n)

    def ints_of(first, chunks):
        return k.psum[:, first * HALF:first * HALF + chunks * TOK // 2].bitcast(BF16)\
            .rearrange("p (c n) -> p c n", c=chunks)

    x1 = Quant(k, "q_x1", D, tiles_of(0, D), ints_of(0, CH))
    v1 = Quant(k, "q_v1", D, tiles_of(4, D), ints_of(4, CH))
    x2 = Quant(k, "q_x2", P, tiles_of(0, P), ints_of(4, 1))
    v2 = Quant(k, "q_v2", P, tiles_of(2, P), ints_of(5, 1))
    row1_ps, row2_ps = k.psum[:, 2 * HALF:4 * HALF], k.psum[:, 6 * HALF:8 * HALF]
    acc1_ps = k.psum[:, 4 * HALF:8 * HALF].rearrange("p (c n) -> p c n", c=CH)
    acc2_ps = k.psum[:, 0:4 * HALF].rearrange("p (c n) -> p c n", c=CH)

    w1_loaded, w2_loaded, chain_sem = k.sem("q_w1_loaded"), k.sem("q_w2_loaded"), k.sem("q_chain")
    half_set, ratio_ready, root_ready = k.sem("q_half_set"), k.sem("q_ratio_ready"), k.sem("q_root_ready")
    row_ready, row_copied, acc_ready = k.sem("q_row_ready"), k.sem("q_row_copied"), k.sem("q_acc_ready")
    scaled1, silu_ready, act_ready = k.sem("q_scaled1"), k.sem("q_silu_ready"), k.sem("q_act_ready")

    def per_batch(t, chunks):
        return t.rearrange("p c (b n) -> p (c b) n", b=B)

    with nc.Block() as block:

        @block.sync
        def _(sp):
            sp.dma_start(w1[:, :, :], a["fside"]).then_inc(w1_loaded, 16)
            sp.dma_start(w2[:, 0, :], a["ctx"]).then_inc(w2_loaded, 16)

        @block.gpsimd
        def _(pool):
            pool.memset(half_col[:, :], 0.5).then_inc(half_set, 1)
            pool.wait_ge(half_set, 1)
            norm_gpsimd(pool, k, 0, False)
            norm_gpsimd(pool, k, 1, False)
            for n in range(2):
                pool.wait_ge(ratio_ready, n + 1)
                pool.tensor_tensor(s[n][:, :, :].rearrange("p c b -> p (c b)"),
                                   ratio[n][:, :, :].rearrange("p c b -> p (c b)"),
                                   half_col[:, :].to_broadcast([P, CH * B]), ALU.pow).then_inc(root_ready, 1)

        @block.tensor
        def _(pe):
            norm_tensor(pe, k, 0)
            norm_tensor(pe, k, 1)
            x1.turn(pe, k, k.cen)
            v1.turn(pe, k, w1)
            x1.turn_back(pe, k)
            x1.step_row(pe, k, row1_ps, row_ready)
            v1.turn_back(pe, k)
            pe.wait_ge(x1.ints_ready, 1)
            pe.wait_ge(v1.ints_ready, 1)
            for b in range(B):
                toks = slice(b * S, (b + 1) * S)
                for o in range(CH):
                    for c in range(CH):
                        last = pe.matmul(acc1_ps[:, o, toks], v1.ints[:, c, b * S + o * P:b * S + (o + 1) * P],
                                         x1.ints[:, c, toks], start=(c == 0), stop=(c == CH - 1))
            last.then_inc(acc_ready, 1)
            pe.wait_ge(row_copied, 1)
            v2.turn(pe, k, w2)
            x2.turn(pe, k, scaled_act)
            v2.turn_back(pe, k)
            x2.turn_back(pe, k)
            x2.step_row(pe, k, row2_ps, row_ready)
            pe.wait_ge(x2.ints_ready, 1)
            pe.wait_ge(v2.ints_ready, 1)
            for b in range(B):
                toks = slice(b * S, (b + 1) * S)
                for o in range(CH):
                    last = pe.matmul(acc2_ps[:, o, toks], v2.ints[:, 0, b * S + o * P:b * S + (o + 1) * P],
                                     x2.ints[:, 0, toks], start=True, stop=True)
            last.then_inc(acc_ready, 1)

        @block.scalar
        def _(act):
            norm_scalar(act, k, 0, False)
            norm_scalar(act, k, 1, False)
            x1.copy_back(act)
            act.wait_ge(row_ready, 1)
            act.activation(row[:, :], row1_ps, ACT.Copy).then_inc(row_copied, 1)
            v1.copy_back(act)
            act.wait_ge(scaled1, 1)
            for b in range(B):
                last = act.activation(silu[:, b * S:(b + 1) * S], acc[:, 0, b * S:(b + 1) * S], ACT.Silu,
                                      scale=v1.step[:, 2 * b:2 * b + 1])
            last.then_inc(silu_ready, 1)
            v2.copy_back(act)
            x2.copy_back(act)
            act.wait_ge(row_ready, 2)
            act.wait_ge(scaled1, 1)
            act.activation(row[:, :], row2_ps, ACT.Copy).then_inc(row_copied, 1)

        @block.vector
        def _(dve):
            chain = Chain(dve, chain_sem)

            def smooth(n, values, value_tops, chunks):
                x_top, w_top = (t[:, 0:chunks, :] for t in tops[n])
                chain.done(dve.tensor_reduce(x_top, values.rearrange("p c (b n) -> p c b n", b=B), AX_X, ALU.max,
                                             apply_absolute_value=True))
                chain.done(dve.tensor_scalar(w_top, w_top, Q_EPS, None, ALU.max))
                chain.done(dve.reciprocal(w_top, w_top))
                dve.scalar_tensor_tensor(ratio[n][:, 0:chunks, :].rearrange("p c b -> p (c b)"),
                                         x_top.rearrange("p c b -> p (c b)"), Q_EPS,
                                         w_top.rearrange("p c b -> p (c b)"), ALU.max, ALU.mult)\
                    .then_inc(ratio_ready, 1)
                dve.wait_ge(root_ready, n + 1)
                chain.done(dve.tensor_scalar(s[n][:, :, :], s[n][:, :, :], Q_EPS, None, ALU.max))
                chain.done(dve.reciprocal(rs[n][:, 0:chunks, :], s[n][:, 0:chunks, :]))

            def scale_by(out, values, factor, chunks, side):
                dve.tensor_tensor(per_batch(out, chunks), per_batch(values, chunks),
                                  factor[:, 0:chunks, :].rearrange("p c b -> p (c b)").unsqueeze(2)
                                  .to_broadcast([P, chunks * B, S]), ALU.mult).then_inc(side.scaled_ready, 1)

            chain.done(dve.memset(ratio[1][:, 1, :], 1.0))
            dve.wait_ge(w1_loaded, 16)
            chain.done(dve.tensor_reduce(tops[0][1][:, :, :], w1[:, :, :].rearrange("p c (b n) -> p c b n", b=B), AX_X,
                                         ALU.max, apply_absolute_value=True))
            dve.wait_ge(w2_loaded, 16)
            chain.done(dve.tensor_reduce(tops[1][1][:, 0:1, :], w2[:, :, :].rearrange("p c (b n) -> p c b n", b=B),
                                         AX_X, ALU.max, apply_absolute_value=True))
            norm_vector(dve, k, 0)
            norm_vector(dve, k, 1)
            dve.wait_ge(k.normed, 2)
            smooth(0, k.cen[:, :, :], None, CH)
            scale_by(k.cen[:, :, :], k.cen[:, :, :], rs[0], CH, x1)
            scale_by(w1[:, :, :], w1[:, :, :], s[0], CH, v1)
            x1.round_rows(dve, chain)
            v1.round_rows(dve, chain)
            dve.wait_ge(acc_ready, 1)
            dve.wait_ge(row_copied, 1)
            dve.tensor_tensor(acc[:, :, :], acc1_ps, row[:, :].unsqueeze(1).to_broadcast([P, CH, TOK]), ALU.mult)\
                .then_inc(scaled1, 1)
            dve.wait_ge(scaled1, 1)
            dve.wait_ge(silu_ready, 1)
            for b in range(B):
                toks = slice(b * S, (b + 1) * S)
                last = dve.scalar_tensor_tensor(act_t[:, 0, toks], acc[:, 1, toks], v1.step[:, 2 * b + 1:2 * b + 2],
                                                silu[:, toks], ALU.mult, ALU.mult)
            chain.done(last)
            smooth(1, act_t[:, :, :], None, 1)
            scale_by(w2[:, :, :], w2[:, :, :], s[1], 1, v2)
            scale_by(scaled_act[:, :, :], act_t[:, :, :], rs[1], 1, x2)
            v2.round_rows(dve, chain)
            x2.round_rows(dve, chain)
            chain.done(dve.tensor_scalar(out_gain[:, :], v2.step[:, :], k.gates[:, gate:gate + 1], None, ALU.mult))
            dve.wait_ge(acc_ready, 2)
            dve.wait_ge(row_copied, 2)
            chain.done(dve.tensor_tensor(acc[:, :, :], acc2_ps, row[:, :].unsqueeze(1).to_broadcast([P, CH, TOK]),
                                         ALU.mult))
            for b in range(B):
                toks = slice(b * S, (b + 1) * S)
                for o in range(CH):
                    dve.scalar_tensor_tensor(k.x[:, o, toks], acc[:, o, toks], out_gain[:, 2 * b + o:2 * b + o + 1],
                                             k.x[:, o, toks], ALU.mult, ALU.add).then_inc(k.x_ready, 1)

    k.at = base



SMALL = 8
GROUP = 4
TWO_PI = 6.283185307179586
TWO_PI_HI = 6.28125
PI = 3.1415925


def rope_phase(k, a):
    nc = k.nc
    base = k.at
    gate = 2
    scale = float(SMALL) ** -0.5
    WQ, WQS, WK, WKS, WV, WO, WEND = 0, 512, 1024, 1280, 1536, 1792, 2304
    early = k.at
    raw = k.sb("r_raw", [P, WEND], F32)
    spread_raw = k.sb("r_spread_raw", [P, 16 * P], F32)
    w_hi = k.sb("r_w_hi", [P, WEND], F32R)
    w_lo = k.sb("r_w_lo", [P, WEND], F32R)
    spread = k.sb("r_spread", [P, 16 * P], F32R)
    pos = k.sb("r_pos", [P, TILES, 2], F32)
    angle = k.sb("r_angle", [P, TILES, 2, 2], F32)
    turns = k.sb("r_turns", [P, 2, TILES * 4], F32)
    reduced = k.sb("r_reduced", [P, 2, TILES * 4], F32)
    wave = k.sb("r_wave", [P, 2, TILES * 4], F32)
    wide = k.sb("r_wide", [P, 2, TILES, SMALL], F32)
    full = k.sb("r_full", [P, 2, TILES, P], F32)
    table = k.sb("r_table", [P, 2, TOK], F32)
    part1 = [k.sb(f"r_part1{s}", [P, HALF], F32) for s in range(2)]
    part2 = [k.sb(f"r_part2{s}", [P, HALF], F32) for s in range(2)]
    rotated = [k.sb(f"r_rotated{s}", [P, HALF], F32) for s in range(2)]
    qk_hi = [k.sb(f"r_{n}_hi", [P, CH * TOK], F32R) for n in "qk"]
    qk_lo = [k.sb(f"r_{n}_lo", [P, CH * TOK], F32R) for n in "qk"]
    v_hi = k.sb("r_v_hi", [P, CH * TOK], F32R)
    v_lo = k.sb("r_v_lo", [P, CH * TOK], F32R)
    rows = [k.sb(f"r_rows{s}", [P, 2 * S], F32R) for s in range(2)]
    top = [k.sb(f"r_top{s}", [P, 2], F32) for s in range(2)]
    shift = [k.sb(f"r_shift{s}", [P, 2], F32) for s in range(2)]
    total = k.sb("r_total", [P, 2, 16], F32)
    rtotal = k.sb("r_rtotal", [P, 2, 16], F32)
    probs = [k.sb(f"r_probs{s}", [P, 2, S], F32) for s in range(2)]
    pt_hi = [k.sb(f"r_pt_hi{s}", [P, 2, S], F32R) for s in range(2)]
    pt_lo = [k.sb(f"r_pt_lo{s}", [P, 2, S], F32R) for s in range(2)]
    o32 = k.sb("r_o32", [P, 2, P], F32)
    late, k.at = k.at, early
    o_hi = k.sb("r_o_hi", [P, CH * TOK], F32R)
    o_lo = k.sb("r_o_lo", [P, CH * TOK], F32R)
    k.at = late
    bout = k.sb("r_bout", [P, CH], F32)
    y_sb = k.sb("r_y", [P, HALF], F32)

    def sem(name):
        return k.sem(f"r_{name}")

    loaded, pos_loaded, chain_sem, w_hi_ready, w_lo_ready = (
        sem("loaded"), sem("pos_loaded"), sem("chain"), sem("w_hi_ready"), sem("w_lo_ready"))
    spread_ready, reduced_ready, wave_ready, full_ready = (
        sem("spread_ready"), sem("reduced_ready"), sem("wave_ready"), sem("full_ready"))
    table_turned, table_ready, v_made, v_hi_ready, v_lo_ready = (
        sem("table_turned"), sem("table_ready"), sem("v_made"), sem("v_hi_ready"), sem("v_lo_ready"))
    plain_made, parts_made, rotated_ready, qk_hi_ready, qk_lo_ready = (
        sem("plain_made"), sem("parts_made"), sem("rotated_ready"), sem("qk_hi_ready"), sem("qk_lo_ready"))
    rows_made, rows_ready = sem("rows_made"), sem("rows_ready")
    scores_ready, top_ready, shift_ready, exp_ready = (
        sem("scores_ready"), sem("top_ready"), sem("shift_ready"), sem("exp_ready"))
    turned, pt_hi_ready, pt_lo_ready, mixed = sem("turned"), sem("pt_hi_ready"), sem("pt_lo_ready"), sem("mixed")
    rtotal_ready, o_ready, o_turned, o_hi_ready, o_lo_ready = (
        sem("rtotal_ready"), sem("o_ready"), sem("o_turned"), sem("o_hi_ready"), sem("o_lo_ready"))
    y_made = sem("y_made")

    s_ps = [k.bank[n].rearrange("p (t n) -> p t n", t=2) for n in (0, 1)]
    t_ps = [k.bank[n].rearrange("p (t n) -> p t n", t=2) for n in (2, 3)]
    rows_ps, mix_ps = k.bank[4], k.bank[5][:, 0:S].rearrange("p (t n) -> p t n", t=2)
    turn_ps = k.bank[6][:, 0:S]
    table_ps = k.psum[:, 0:4 * HALF].rearrange("p (w n) -> p w n", w=2)
    v_ps = k.psum[:, 4 * HALF:8 * HALF]
    iterations = CH * B
    units = iterations * 16
    kinds = [(kind, c, half) for kind in range(2) for c in range(CH) for half in range(2)]

    with nc.Block() as block:

        @block.sync
        def _(sp):
            sp.dma_start(pos[:, :, :], a["r_pos"]).then_inc(pos_loaded, 16)
            sp.dma_start(raw[:, :], a["r_w"]).then_inc(loaded, 16)
            sp.dma_start(spread_raw[:, :], a["r_spread"]).then_inc(loaded, 16)
            sp.dma_start(bout[:, :], a["r_bout"]).then_inc(loaded, 16)

        @block.tensor
        def _(pe):
            norm_tensor(pe, k, 0)
            norm_tensor(pe, k, 1)
            pe.wait_ge(k.normed, 2)
            pe.wait_ge(full_ready, 2)
            for w in range(2):
                for t in range(TILES):
                    last = pe.transpose(table_ps[:, w, t * P:(t + 1) * P], full[:, w, t, :], k.ident[:, :])
            last.then_inc(table_turned, 1)
            pe.wait_ge(w_hi_ready, 1)
            pe.wait_ge(w_lo_ready, 1)
            for c in range(CH):
                for t in range(TILES):
                    w = slice(WV + c * P, WV + (c + 1) * P)
                    cols = slice(t * P, (t + 1) * P)
                    last = mm3(pe, v_ps[:, c * TOK + t * P:c * TOK + (t + 1) * P], k.ctx_hi[:, cols],
                               k.ctx_lo[:, cols], w_hi[:, w], w_lo[:, w], True, True)
            last.then_inc(v_made, 1)
            pe.wait_ge(table_ready, 1)
            pe.wait_ge(k.h_hi_ready, 2)
            pe.wait_ge(k.h_lo_ready, 2)
            for n, (kind, c, half) in enumerate(kinds):
                if n >= 2:
                    pe.wait_ge(parts_made, 2 * (n - 1))
                cols = slice(half * HALF, (half + 1) * HALF)
                for swapped in range(2):
                    out = k.bank[2 * (n % 2) + swapped]
                    if kind == 0:
                        for f in range(CH):
                            at = (WQ, WQS)[swapped] + f * D + c * P
                            last = mm3(pe, out, w_hi[:, at:at + P], w_lo[:, at:at + P], k.h_hi[:, f, cols],
                                       k.h_lo[:, f, cols], f == 0, f == CH - 1)
                    else:
                        at = (WK, WKS)[swapped] + c * P
                        last = mm3(pe, out, w_hi[:, at:at + P], w_lo[:, at:at + P], k.ctx_hi[:, cols],
                                   k.ctx_lo[:, cols], True, True)
                last.then_inc(plain_made, 1)

            def make_rows(i, g):
                need(pe, rows_ready, i * 4 + g)
                cols = bass.ds(i * S, S)
                for n in range(2):
                    m = slice((g * 4 + 2 * n) * P, (g * 4 + 2 * n + 1) * P)
                    m2 = slice((g * 4 + 2 * n + 1) * P, (g * 4 + 2 * n + 2) * P)
                    pe.matmul(rows_ps[:, n * S:(n + 1) * S], spread[:, m], qk_hi[n][:, cols], start=True, stop=False)
                    last = pe.matmul(rows_ps[:, n * S:(n + 1) * S], spread[:, m2], qk_lo[n][:, cols], start=False,
                                     stop=True)
                last.then_inc(rows_made, 1)

            def scores(i, u):
                g, s = u // GROUP, u % GROUP
                if s == 0:
                    pe.wait_ge(rows_ready, i * 4 + g + 1)
                need(pe, exp_ready, 2 * (i * 16 + u) - 2)
                r = slice(32 * s, 32 * s + 32)
                for t in range(2):
                    last = pe.matmul(s_ps[u % 2][:, t, :], rows[g % 2][r, t * P:(t + 1) * P], rows[g % 2][r, S:2 * S],
                                     start=True, stop=True)
                last.then_inc(scores_ready, 1)

            def turn(i, u):
                j = i * 16 + u
                pe.wait_ge(exp_ready, 2 * j + 2)
                need(pe, pt_hi_ready, j - 1)
                need(pe, pt_lo_ready, j - 1)
                for kt in range(2):
                    for t in range(2):
                        last = pe.transpose(t_ps[u % 2][:, kt, t * P:(t + 1) * P],
                                            probs[u % 2][:, t, kt * P:(kt + 1) * P], k.ident[:, :])
                last.then_inc(turned, 1)

            def mix(i, u):
                j = i * 16 + u
                pe.wait_ge(pt_hi_ready, j + 1)
                pe.wait_ge(pt_lo_ready, j + 1)
                if u == 0:
                    need(pe, o_ready, i)
                for t in range(2):
                    for kt in range(2):
                        cols = bass.ds(i * S + kt * P + u * SMALL, SMALL)
                        last = mm3(pe, mix_ps[:, t, u * SMALL:(u + 1) * SMALL], pt_hi[u % 2][:, kt, t * P:(t + 1) * P],
                                   pt_lo[u % 2][:, kt, t * P:(t + 1) * P], v_hi[:, cols], v_lo[:, cols], kt == 0,
                                   kt == 1)
                last.then_inc(mixed, 1)

            pe.wait_ge(qk_lo_ready, len(kinds))
            pe.wait_ge(qk_hi_ready, len(kinds))
            pe.wait_ge(spread_ready, 1)
            pe.wait_ge(v_hi_ready, 1)
            pe.wait_ge(v_lo_ready, 1)
            make_rows(0, 0)
            scores(0, 0)

            def body(i, last):
                for u in range(16):
                    if u % 4 == 0 and not (last and u == 12):
                        g = u // 4 + 1
                        make_rows(*((i, g) if g < 4 else (i + 1, 0)))
                    if u < 15:
                        scores(i, u + 1)
                    elif not last:
                        scores(i + 1, 0)
                    turn(i, u)
                    if u > 0:
                        mix(i, u - 1)
                mix(i, 15)
                pe.wait_ge(o_ready, i + 1)
                need(pe, o_lo_ready, i)
                need(pe, o_hi_ready, i)
                for t in range(2):
                    last_turn = pe.transpose(turn_ps[:, t * P:(t + 1) * P], o32[:, t, :], k.ident[:, :])
                last_turn.then_inc(o_turned, 1)

            body(0, False)
            with pe.Fori(1, iterations - 1) as i:
                body(i, False)
            body(iterations - 1, True)
            pe.wait_ge(o_hi_ready, iterations)
            pe.wait_ge(o_lo_ready, iterations)
            for o in range(CH):
                for half in range(2):
                    for c in range(CH):
                        at = WO + c * D + o * P
                        cols = slice(c * TOK + half * HALF, c * TOK + (half + 1) * HALF)
                        last = mm3(pe, k.bank[2 * o + half], w_hi[:, at:at + P], w_lo[:, at:at + P], o_hi[:, cols],
                                   o_lo[:, cols], c == 0, c == CH - 1)
                    last.then_inc(y_made, 1)

        @block.scalar
        def _(act):
            act.wait_ge(loaded, 48)
            act.activation(w_hi[:, :], raw[:, :], ACT.Copy).then_inc(w_hi_ready, 1)
            act.activation(spread[:, :], spread_raw[:, :], ACT.Copy).then_inc(spread_ready, 1)
            act.wait_ge(reduced_ready, 1)
            act.activation(wave[:, :, :], reduced[:, :, :], ACT.Sin).then_inc(wave_ready, 1)
            norm_scalar(act, k, 0)
            norm_scalar(act, k, 1)
            act.wait_ge(table_turned, 1)
            act.activation(table[:, :, :], table_ps, ACT.Copy).then_inc(table_ready, 1)
            act.wait_ge(v_made, 1)
            act.activation(v_hi[:, :], v_ps, ACT.Copy).then_inc(v_hi_ready, 1)
            for n, (kind, c, half) in enumerate(kinds):
                act.wait_ge(rotated_ready, n + 1)
                at = slice(c * TOK + half * HALF, c * TOK + (half + 1) * HALF)
                act.activation(qk_hi[kind][:, at], rotated[n % 2][:, :], ACT.Copy).then_inc(qk_hi_ready, 1)

            def copy_rows(i, g):
                act.wait_ge(rows_made, i * 4 + g + 1)
                need(act, scores_ready, (i * 4 + g - 1) * GROUP)
                act.activation(rows[g % 2][:, :], rows_ps, ACT.Copy).then_inc(rows_ready, 1)

            def exps(i, u):
                j = i * 16 + u
                act.wait_ge(shift_ready, j + 1)
                need(act, turned, j - 1)
                if u == 0:
                    need(act, rtotal_ready, i)
                for t in range(2):
                    act.activation(probs[u % 2][:, t, :], s_ps[u % 2][:, t, :], ACT.Exp,
                                   bias=shift[u % 2][:, t:t + 1], scale=scale, accum_out=total[:, t, u:u + 1])\
                        .then_inc(exp_ready, 1)

            def copy_turned(i, u):
                j = i * 16 + u
                act.wait_ge(turned, j + 1)
                need(act, mixed, j - 1)
                act.activation(pt_hi[u % 2][:, :, :], t_ps[u % 2], ACT.Copy).then_inc(pt_hi_ready, 1)

            copy_rows(0, 0)
            exps(0, 0)

            def body(i, last):
                for u in range(16):
                    if u % 4 == 0 and not (last and u == 12):
                        g = u // 4 + 1
                        copy_rows(*((i, g) if g < 4 else (i + 1, 0)))
                    if u < 15:
                        exps(i, u + 1)
                    elif not last:
                        exps(i + 1, 0)
                    copy_turned(i, u)
                act.wait_ge(o_turned, i + 1)
                act.activation(o_hi[:, bass.ds(i * S, S)], turn_ps, ACT.Copy).then_inc(o_hi_ready, 1)

            body(0, False)
            with act.Fori(1, iterations - 1) as i:
                body(i, False)
            body(iterations - 1, True)

        @block.gpsimd
        def _(pool):
            pool.wait_ge(w_hi_ready, 1)
            pool.tensor_tensor(w_lo[:, :], raw[:, :], f32(w_hi[:, :]), ALU.subtract).then_inc(w_lo_ready, 1)
            norm_gpsimd(pool, k, 0)
            norm_gpsimd(pool, k, 1)
            for n, (kind, c, half) in enumerate(kinds):
                pool.wait_ge(parts_made, 2 * n + 2)
                if n >= 2:
                    pool.wait_ge(qk_hi_ready, n - 1)
                    pool.wait_ge(qk_lo_ready, n - 1)
                pool.tensor_tensor(rotated[n % 2][:, :], part1[n % 2][:, :], part2[n % 2][:, :], ALU.add)\
                    .then_inc(rotated_ready, 1)
                at = slice(c * TOK + half * HALF, c * TOK + (half + 1) * HALF)
                pool.wait_ge(qk_hi_ready, n + 1)
                pool.wait_ge(rotated_ready, n + 1)
                pool.tensor_tensor(qk_lo[kind][:, at], rotated[n % 2][:, :], f32(qk_hi[kind][:, at]), ALU.subtract)\
                    .then_inc(qk_lo_ready, 1)

        @block.vector
        def _(dve):
            chain = Chain(dve, chain_sem)
            dve.wait_ge(pos_loaded, 16)
            dve.tensor_copy(angle[:, :, :, 0], pos[:, :, :])
            chain.done(dve.tensor_scalar(angle[:, :, :, 1], pos[:, :, :], float(k.rope_freq), None, ALU.mult))
            flat = angle[:, :, :, :].rearrange("p t a b -> p (t a b)")
            for w, (quarter, add) in enumerate(((0.25, 0.5 * PI), (0.0, 0.0))):
                chain.done(dve.tensor_scalar(turns[:, w, :], flat, 1.0 / TWO_PI, quarter, ALU.mult, ALU.add))
                chain.done(dve.tensor_scalar(turns[:, w, :], turns[:, w, :], ROUND, ROUND, ALU.add, ALU.subtract))
                chain.done(dve.scalar_tensor_tensor(reduced[:, w, :], turns[:, w, :], -TWO_PI_HI, flat, ALU.mult,
                                                    ALU.add))
                chain.done(dve.scalar_tensor_tensor(reduced[:, w, :], turns[:, w, :], TWO_PI_HI - TWO_PI,
                                                    reduced[:, w, :], ALU.mult, ALU.add))
                chain.done(dve.tensor_scalar(reduced[:, w, :], reduced[:, w, :], (0.5 * 3.141592653589793, 0.0)[w],
                                             None, ALU.add))
            chain.done(dve.tensor_scalar(reduced[:, :, :], reduced[:, :, :], PI, -PI, ALU.min, ALU.max))
            dve.tensor_scalar(reduced[:, :, :], reduced[:, :, :], 1.0, None, ALU.mult).then_inc(reduced_ready, 1)
            dve.wait_ge(wave_ready, 1)
            waves = wave[:, :, :].rearrange("p w (t a) -> p w t a", a=4)
            pairs = wide[:, :, :, :].rearrange("p w t (a i) -> p w t a i", i=2)
            for i in range(2):
                chain.done(dve.tensor_copy(pairs[:, 0, :, :, i], waves[:, 0, :, :]))
            chain.done(dve.tensor_scalar(pairs[:, 1, :, :, 0], waves[:, 1, :, :], -1.0, None, ALU.mult))
            chain.done(dve.tensor_copy(pairs[:, 1, :, :, 1], waves[:, 1, :, :]))
            for w in range(2):
                dve.tensor_copy(full[:, w, :, :].rearrange("p t (h d) -> p t h d", d=SMALL),
                                wide[:, w, :, :].unsqueeze(2).to_broadcast([P, TILES, 16, SMALL]))\
                    .then_inc(full_ready, 1)
            norm_vector(dve, k, 0)
            norm_vector(dve, k, 1)
            dve.wait_ge(v_hi_ready, 1)
            dve.tensor_tensor(v_lo[:, :], v_ps, f32(v_hi[:, :]), ALU.subtract).then_inc(v_lo_ready, 1)
            dve.wait_ge(table_ready, 1)
            for n, (kind, c, half) in enumerate(kinds):
                dve.wait_ge(plain_made, n + 1)
                if n >= 2:
                    dve.wait_ge(rotated_ready, n - 1)
                cols = slice(half * HALF, (half + 1) * HALF)
                for swapped, out in ((0, part1), (1, part2)):
                    dve.tensor_tensor(out[n % 2][:, :], k.bank[2 * (n % 2) + swapped], table[:, swapped, cols],
                                      ALU.mult).then_inc(parts_made, 1)

            def maxima(i, u):
                j = i * 16 + u
                dve.wait_ge(scores_ready, j + 1)
                dve.tensor_reduce(top[u % 2][:, :], s_ps[u % 2], AX_X, ALU.max).then_inc(top_ready, 1)
                dve.wait_ge(top_ready, j + 1)
                dve.tensor_scalar(shift[u % 2][:, :], top[u % 2][:, :], -scale, None, ALU.mult)\
                    .then_inc(shift_ready, 1)

            maxima(0, 0)

            def body(i, last):
                for u in range(16):
                    if u < 15:
                        maxima(i, u + 1)
                    elif not last:
                        maxima(i + 1, 0)
                    j = i * 16 + u
                    if u == 15:
                        dve.wait_ge(exp_ready, 2 * j + 2)
                        dve.reciprocal(rtotal[:, :, :], total[:, :, :]).then_inc(rtotal_ready, 1)
                    dve.wait_ge(pt_hi_ready, j + 1)
                    dve.tensor_tensor(pt_lo[u % 2][:, :, :], t_ps[u % 2], f32(pt_hi[u % 2][:, :, :]), ALU.subtract)\
                        .then_inc(pt_lo_ready, 1)
                dve.wait_ge(rtotal_ready, i + 1)
                dve.wait_ge(mixed, i * 16 + 16)
                need(dve, o_turned, i)
                for t in range(2):
                    ins = dve.tensor_tensor(o32[:, t, :].rearrange("p (h d) -> p h d", d=SMALL),
                                            mix_ps[:, t, :].rearrange("p (h d) -> p h d", d=SMALL),
                                            rtotal[:, t, :].unsqueeze(2).to_broadcast([P, 16, SMALL]), ALU.mult)
                ins.then_inc(o_ready, 1)
                dve.wait_ge(o_hi_ready, i + 1)
                at = bass.ds(i * S, S)
                dve.tensor_tensor(o_lo[:, at], turn_ps, f32(o_hi[:, at]), ALU.subtract).then_inc(o_lo_ready, 1)

            body(0, False)
            with dve.Fori(1, iterations - 1) as i:
                body(i, False)
            body(iterations - 1, True)
            for n, (o, half) in enumerate((o, half) for o in range(CH) for half in range(2)):
                dve.wait_ge(y_made, n + 1)
                cols = slice(half * HALF, (half + 1) * HALF)
                chain.done(dve.tensor_scalar(y_sb[:, :], k.bank[2 * o + half], bout[:, o:o + 1],
                                             k.gates[:, gate:gate + 1], ALU.add, ALU.mult))
                chain.done(dve.tensor_tensor(k.x[:, o, cols], k.x[:, o, cols], y_sb[:, :], ALU.add))

    k.at = base




def lora_phase(k, a):
    nc = k.nc
    base = k.at
    gate = 6
    experts, blocks = 8, 7
    W1, W3, B1, B3, W2, A2, WEND = (D * n for n in range(7))
    A1, A3, B2, SMALL_END = 0, 2 * D, 4 * D, 6 * D
    small_hi = k.sb("l_small_hi", [P, SMALL_END], F32R)
    small_lo = k.sb("l_small_lo", [P, SMALL_END], F32R)
    raw = k.sb("l_raw", [P, WEND], F32)
    w_hi = [k.sb(f"l_w_hi{s}", [P, WEND], F32R) for s in range(2)]
    w_lo = [k.sb(f"l_w_lo{s}", [P, WEND], F32R) for s in range(2)]
    early = k.at
    am_hi = [[k.sb(f"l_am_hi{w}{n}", [P, CH, TOK], F32R) for n in range(2)] for w in range(2)]
    am_lo = [[k.sb(f"l_am_lo{w}{n}", [P, CH, TOK], F32R) for n in range(2)] for w in range(2)]
    late = k.at
    k.at = early
    rw = k.sb("l_rw", [P, CH, experts], F32)
    rw_hi = k.sb("l_rw_hi", [P, CH, experts], F32R)
    rw_lo = k.sb("l_rw_lo", [P, CH, experts], F32R)
    logits, shifted, expd, rank_of = (k.sb(f"l_{n}", [P, TILES, experts], F32)
                                      for n in ("logits", "shifted", "expd", "rank"))
    slot = [k.sb(f"l_slot{n}", [P, TILES, experts], F32) for n in range(2)]
    top, total = k.sb("l_top", [P, TILES], F32), k.sb("l_total", [P, TILES], F32)
    kept = k.sb("l_kept", [P, TILES, experts], F32)
    weight = [k.sb(f"l_weight{n}", [P, TILES, 1], F32) for n in range(2)]
    rest = k.sb("l_rest", [P, TILES, 1], F32)
    parts = k.sb("l_parts", [P, TILES, P], BF16)
    parts_t = k.sb("l_parts_t", [P, TOK], BF16)
    select = k.sb("l_select", [P, 8 * P], BF16)
    k.cmp_gt = k.sb("l_cmp_gt", [P, TILES * 64], F32)
    k.cmp_eq = k.sb("l_cmp_eq", [P, TILES * 64], F32)
    k.at = early
    u_hi = k.sb("l_u_hi", [P, CH, TOK], F32R)
    u_lo = k.sb("l_u_lo", [P, CH, TOK], F32R)
    k.at = late
    weight_row = k.sb("l_weight_row", [P, 2, TOK], F32)
    u = k.sb("l_u", [P, CH, TOK], F32)
    loop = k.at
    act32 = [k.sb(f"l_act32{n}", [P, HALF], F32) for n in range(2)]
    masked = k.sb("l_masked", [P, CH, HALF], F32)
    products = k.at
    x2_hi = [k.sb(f"l_x2_hi{n}", [P, HALF], F32R) for n in range(2)]
    x2_lo = [k.sb(f"l_x2_lo{n}", [P, HALF], F32R) for n in range(2)]
    k.at = loop
    small_raw = k.sb("l_small_raw", [P, SMALL_END], F32)
    k.at = loop
    row_hi = k.sb("l_row_hi", [P, HALF], F32R)
    row_lo = k.sb("l_row_lo", [P, HALF], F32R)
    k.at = products
    diff = k.sb("l_diff", [P, CH, TOK], F32)
    mask = [k.cen, k.sq]

    def sem(name):
        return k.sem(f"l_{name}")

    small_loaded, raw_loaded, chain_sem, zeroed = sem("small_loaded"), sem("raw_loaded"), sem("chain"), sem("zeroed")
    small_hi_ready, small_lo_ready, router_hi, router_lo = (
        sem("small_hi_ready"), sem("small_lo_ready"), sem("router_hi"), sem("router_lo"))
    logits_ready, shifted_ready, expd_ready, parts_ready = (
        sem("logits_ready"), sem("shifted_ready"), sem("expd_ready"), sem("parts_ready"))
    turned, parts_t_ready, table_made, table_copied = (
        sem("turned"), sem("parts_t_ready"), sem("table_made"), sem("table_copied"))
    row_made, row_hi_ready, row_lo_ready, am_ready = (
        sem("row_made"), sem("row_hi_ready"), sem("row_lo_ready"), sem("am_ready"))
    w_hi_ready, w_lo_ready = sem("w_hi_ready"), sem("w_lo_ready")
    x1_made, x3_made, silu_ready, gated_ready = sem("x1_made"), sem("x3_made"), sem("silu_ready"), sem("gated_ready")
    weighted_ready, x2_hi_ready, x2_lo_ready = sem("weighted_ready"), sem("x2_hi_ready"), sem("x2_lo_ready")
    y_done, a2_masked, a2_added = sem("y_done"), sem("a2_masked"), sem("a2_added")
    u_hi_ready, u_lo_ready, y_whole = sem("u_hi_ready"), sem("u_lo_ready"), sem("y_whole")

    y = [[k.bank[2 * c + half] for half in range(2)] for c in range(CH)]
    x1_ps, x3_ps = k.bank[4], k.bank[5]
    a2_ps = k.psum[:, 6 * HALF:8 * HALF].rearrange("p (c n) -> p c n", c=CH)
    logits_ps = k.bank[7][:, 0:TILES * experts].rearrange("p (t e) -> p t e", e=experts)
    tables = [mask[0][:, 0, :], mask[0][:, 1, :], mask[1][:, 0, :], mask[1][:, 1, :], diff[:, 0, :], diff[:, 1, :],
              weight_row[:, 0, :], weight_row[:, 1, :]]
    rows = [(w, c, half) for w in range(2) for c in range(CH) for half in range(2)]
    units = blocks * 4
    loop_to = (blocks - 1) // 2

    def static(b):
        return isinstance(b, int)

    def over_blocks(eng, body):
        body(0, 0, True)
        body(1, 1, True)
        with eng.Fori(1, loop_to) as pair:
            body(pair * 2, 0, True)
            body(pair * 2 + 1, 1, True)
        for b in range(2 * loop_to, blocks):
            body(b, b % 2, b + 1 < blocks)

    with nc.Block() as block:

        @block.sync
        def _(sp):
            sp.dma_start(rw[:, :, :], a["l_router"]).then_inc(small_loaded, 16)
            sp.dma_start(small_raw[:, :], a["l_small"]).then_inc(small_loaded, 16)
            sp.dma_start(select[:, :], a["l_select"]).then_inc(small_loaded, 16)
            sp.dma_start(raw[:, :], a["l_w"][0, :, :]).then_inc(raw_loaded, 16)
            with sp.Fori(1, blocks) as b:
                sp.wait_ge(w_hi_ready, b)
                sp.wait_ge(w_lo_ready, b)
                sp.dma_start(raw[:, :], a["l_w"][bass.ds(b, 1), :, :].rearrange("b p n -> p (b n)"))\
                    .then_inc(raw_loaded, 16)

        @block.tensor
        def _(pe):
            norm_tensor(pe, k, 0)
            norm_tensor(pe, k, 1)
            pe.wait_ge(k.h_hi_ready, 2)
            pe.wait_ge(k.h_lo_ready, 2)
            pe.wait_ge(router_hi, 1)
            pe.wait_ge(router_lo, 1)
            for t in range(TILES):
                cols = slice(t * P, (t + 1) * P)
                for c in range(CH):
                    last = mm3(pe, logits_ps[:, t, :], k.h_hi[:, c, cols], k.h_lo[:, c, cols], rw_hi[:, c, :],
                               rw_lo[:, c, :], c == 0, c == CH - 1)
            last.then_inc(logits_ready, 1)
            pe.wait_ge(parts_ready, 1)
            turned_ps = k.bank[6].bitcast(BF16)
            for t in range(TILES):
                last = pe.transpose(turned_ps[:, t * P:(t + 1) * P], parts[:, t, :], k.ident_bf[:, :])
            last.then_inc(turned, 1)
            pe.wait_ge(parts_t_ready, 1)
            for n in range(len(tables)):
                if n >= 2:
                    pe.wait_ge(table_copied, n - 1)
                for half in range(2):
                    last = pe.matmul(k.bank[2 * (n % 2) + half], select[:, n * P:(n + 1) * P],
                                     parts_t[:, half * HALF:(half + 1) * HALF], start=True, stop=True)
                last.then_inc(table_made, 1)
            pe.wait_ge(small_hi_ready, 1)
            pe.wait_ge(small_lo_ready, 1)
            for n, (w, c, half) in enumerate(rows):
                if n >= 2:
                    pe.wait_ge(row_lo_ready, n - 1)
                cols = slice(half * HALF, (half + 1) * HALF)
                for f in range(CH):
                    at = (A1, A3)[w] + f * D + c * P
                    last = mm3(pe, k.bank[4 + n % 2], small_hi[:, at:at + P], small_lo[:, at:at + P],
                               k.h_hi[:, f, cols], k.h_lo[:, f, cols], f == 0, f == CH - 1)
                last.then_inc(row_made, 1)
            pe.wait_ge(table_copied, len(tables))
            for c in range(CH):
                for half in range(2):
                    pe.matmul(y[c][half], k.zeros[:, 0:P], k.zeros[:, :], start=True, stop=False)
            pe.wait_ge(row_lo_ready, len(rows))
            pe.wait_ge(am_ready, 4 * len(rows))

            def add_y(j, half, n, s):
                pe.wait_ge(x2_hi_ready, j + 1)
                pe.wait_ge(x2_lo_ready, j + 1)
                for c in range(CH):
                    at = W2 + c * P
                    mm3(pe, y[c][half], w_hi[s][:, at:at + P], w_lo[s][:, at:at + P], x2_hi[n][:, :], x2_lo[n][:, :],
                        False, False)
                need(pe, a2_masked, j)
                for c in range(CH):
                    at = A2 + c * P
                    last = mm3(pe, a2_ps[:, c, :], w_hi[s][:, at:at + P], w_lo[s][:, at:at + P], x2_hi[n][:, :],
                               x2_lo[n][:, :], True, True)
                last.then_inc(y_done, 1)

            def body(b, s, _more):
                pe.wait_ge(w_hi_ready, b + 1)
                pe.wait_ge(w_lo_ready, b + 1)
                for half in range(2):
                    cols = slice(half * HALF, (half + 1) * HALF)
                    for n in range(2):
                        j = b * 4 + half * 2 + n
                        for w, (out, big, low, made, free) in enumerate(((x1_ps, W1, B1, x1_made, silu_ready),
                                                                         (x3_ps, W3, B3, x3_made, gated_ready))):
                            need(pe, free, j)
                            if n == 0:
                                for c in range(CH):
                                    at = big + c * P
                                    mm3(pe, out, w_hi[s][:, at:at + P], w_lo[s][:, at:at + P], k.h_hi[:, c, cols],
                                        k.h_lo[:, c, cols], c == 0, False)
                            for c in range(CH):
                                at = low + c * P
                                stop = c == CH - 1
                                lhs_hi, lhs_lo = w_hi[s][:, at:at + P], w_lo[s][:, at:at + P]
                                rhs_hi, rhs_lo = am_hi[w][n][:, c, cols], am_lo[w][n][:, c, cols]
                                again = n == 1
                                pe.matmul(out, lhs_hi, rhs_hi, start=False, stop=False, skip_group_check=again)
                                pe.matmul(out, lhs_lo, rhs_hi, start=False, stop=False, skip_group_check=again)
                                last = pe.matmul(out, lhs_hi, rhs_lo, start=False, stop=stop, skip_group_check=again)
                            last.then_inc(made, 1)
                        if not (static(b) and j == 0):
                            if n == 1:
                                add_y(j - 1, half, 0, s)
                            elif half == 1:
                                add_y(j - 1, 0, 1, s)
                            else:
                                add_y(j - 1, 1, 1, 1 - s)

            over_blocks(pe, body)
            add_y(units - 1, 1, 1, (blocks - 1) % 2)
            for half in range(2):
                cols = slice(half * HALF, (half + 1) * HALF)
                pe.wait_ge(u_hi_ready, half + 1)
                pe.wait_ge(u_lo_ready, half + 1)
                for o in range(CH):
                    for c in range(CH):
                        at = B2 + c * D + o * P
                        last = mm3(pe, y[o][half], small_hi[:, at:at + P], small_lo[:, at:at + P], u_hi[:, c, cols],
                                   u_lo[:, c, cols], False, c == CH - 1)
                last.then_inc(y_whole, 1)

        @block.scalar
        def _(act):
            def split(b, s):
                act.wait_ge(raw_loaded, b * 16 + 16)
                if not static(b) or b >= 2:
                    act.wait_ge(y_done, b * 4 - 4)
                act.activation(w_hi[s][:, :], raw[:, :], ACT.Copy).then_inc(w_hi_ready, 1)

            act.wait_ge(small_loaded, 48)
            act.activation(rw_hi[:, :, :], rw[:, :, :], ACT.Copy).then_inc(router_hi, 1)
            act.activation(small_hi[:, :], small_raw[:, :], ACT.Copy).then_inc(small_hi_ready, 1)
            norm_scalar(act, k, 0)
            norm_scalar(act, k, 1)
            split(0, 0)
            act.wait_ge(shifted_ready, 1)
            act.activation(expd[:, :, :], shifted[:, :, :], ACT.Exp).then_inc(expd_ready, 1)
            act.wait_ge(k.normed, 2)
            act.wait_ge(k.h_lo_ready, 2)
            for n, table in enumerate(tables):
                act.wait_ge(table_made, n + 1)
                act.activation(table, k.psum[:, 2 * (n % 2) * HALF:(2 * (n % 2) + 2) * HALF], ACT.Copy)\
                    .then_inc(table_copied, 1)
            for n in range(len(rows)):
                act.wait_ge(row_made, n + 1)
                need(act, am_ready, 4 * n)
                act.activation(row_hi[:, :], k.bank[4 + n % 2], ACT.Copy).then_inc(row_hi_ready, 1)

            def body(b, s, more):
                for half in range(2):
                    for n in range(2):
                        j = b * 4 + half * 2 + n
                        act.wait_ge(x1_made, j + 1)
                        need(act, x2_lo_ready, j - 1)
                        act.activation(act32[n][:, :], x1_ps, ACT.Silu).then_inc(silu_ready, 1)
                        act.wait_ge(weighted_ready, j + 1)
                        need(act, y_done, j - 1)
                        act.activation(x2_hi[n][:, :], act32[n][:, :], ACT.Copy).then_inc(x2_hi_ready, 1)
                        if half == 0 and n == 0 and more:
                            split(b + 1, 1 - s)

            over_blocks(act, body)
            for half in range(2):
                cols = slice(half * HALF, (half + 1) * HALF)
                act.wait_ge(a2_added, units - 1 + half)
                act.wait_ge(y_done, units)
                act.activation(u_hi[:, :, cols], u[:, :, cols], ACT.Copy).then_inc(u_hi_ready, 1)

        @block.gpsimd
        def _(pool):
            def split(b, s):
                pool.wait_ge(w_hi_ready, b + 1)
                pool.tensor_tensor(w_lo[s][:, :], raw[:, :], f32(w_hi[s][:, :]), ALU.subtract).then_inc(w_lo_ready, 1)

            pool.memset(parts[:, :, :], 0.0).then_inc(zeroed, 1)
            pool.memset(u[:, :, :], 0.0).then_inc(zeroed, 1)
            pool.wait_ge(router_hi, 1)
            pool.tensor_tensor(rw_lo[:, :, :], rw[:, :, :], f32(rw_hi[:, :, :]), ALU.subtract).then_inc(router_lo, 1)
            norm_gpsimd(pool, k, 0)
            norm_gpsimd(pool, k, 1)
            pool.wait_ge(small_hi_ready, 1)
            pool.tensor_tensor(small_lo[:, :], small_raw[:, :], f32(small_hi[:, :]), ALU.subtract)\
                .then_inc(small_lo_ready, 1)
            split(0, 0)
            pool.wait_ge(table_copied, len(tables))
            for n, (w, c, half) in enumerate(rows):
                cols = slice(half * HALF, (half + 1) * HALF)
                pool.wait_ge(row_hi_ready, n + 1)
                pool.tensor_tensor(am_hi[w][1][:, c, cols], f32(row_hi[:, :]), diff[:, c, cols], ALU.mult)\
                    .then_inc(am_ready, 1)
                pool.wait_ge(row_lo_ready, n + 1)
                pool.tensor_tensor(am_lo[w][1][:, c, cols], f32(row_lo[:, :]), diff[:, c, cols], ALU.mult)\
                    .then_inc(am_ready, 1)

            def add_masked(j, half):
                pool.wait_ge(a2_masked, j + 1)
                need(pool, a2_added, j)
                cols = slice(half * HALF, (half + 1) * HALF)
                pool.tensor_tensor(u[:, :, cols], u[:, :, cols], masked[:, :, :], ALU.add).then_inc(a2_added, 1)

            def body(b, s, more):
                for half in range(2):
                    for n in range(2):
                        j = b * 4 + half * 2 + n
                        if not (static(b) and j == 0):
                            add_masked(j - 1, half if n == 1 else 1 - half)
                        if half == 0 and n == 0 and more:
                            split(b + 1, 1 - s)

            over_blocks(pool, body)
            add_masked(units - 1, 1)

        @block.vector
        def _(dve):
            chain = Chain(dve, chain_sem)
            norm_vector(dve, k, 0)
            norm_vector(dve, k, 1)
            dve.wait_ge(logits_ready, 1)
            chain.done(dve.tensor_copy(logits[:, :, :], logits_ps))
            chain.done(dve.tensor_reduce(top[:, :], logits[:, :, :], AX_X, ALU.max))
            dve.tensor_tensor(shifted[:, :, :], logits[:, :, :], top[:, :].unsqueeze(2)
                              .to_broadcast([P, TILES, experts]), ALU.subtract).then_inc(shifted_ready, 1)
            rank(dve, chain, k, rank_of[:, :, :], logits[:, :, :], experts)
            dve.wait_ge(expd_ready, 1)
            for n in range(2):
                chain.done(dve.tensor_scalar(slot[n][:, :, :], rank_of[:, :, :], float(n), None, ALU.is_equal))
                chain.done(dve.tensor_tensor(kept[:, :, :], slot[n][:, :, :], expd[:, :, :], ALU.mult))
                chain.done(dve.tensor_reduce(weight[n][:, :, 0], kept[:, :, :], AX_X, ALU.add))
            chain.done(dve.tensor_tensor(total[:, :], weight[0][:, :, 0], weight[1][:, :, 0], ALU.add))
            chain.done(dve.reciprocal(total[:, :], total[:, :]))
            dve.wait_ge(zeroed, 2)
            for n in range(2):
                chain.done(dve.tensor_tensor(weight[n][:, :, 0], weight[n][:, :, 0], total[:, :], ALU.mult))
                chain.done(dve.tensor_copy(parts[:, :, 8 * n:8 * n + 8], slot[n][:, :, :]))
                at = 16 + 3 * n
                chain.done(dve.tensor_copy(parts[:, :, at:at + 1], weight[n][:, :, :]))
                chain.done(dve.tensor_tensor(rest[:, :, :], weight[n][:, :, :], parts[:, :, at:at + 1], ALU.subtract))
                chain.done(dve.tensor_copy(parts[:, :, at + 1:at + 2], rest[:, :, :]))
                chain.done(dve.tensor_tensor(rest[:, :, :], rest[:, :, :], parts[:, :, at + 1:at + 2], ALU.subtract))
                last = dve.tensor_copy(parts[:, :, at + 2:at + 3], rest[:, :, :])
                if n == 0:
                    chain.done(last)
            last.then_inc(parts_ready, 1)
            dve.wait_ge(turned, 1)
            dve.tensor_copy(parts_t[:, :], k.bank[6].bitcast(BF16)).then_inc(parts_t_ready, 1)
            dve.wait_ge(table_copied, len(tables))
            for n, (w, c, half) in enumerate(rows):
                cols = slice(half * HALF, (half + 1) * HALF)
                dve.wait_ge(row_hi_ready, n + 1)
                need(dve, am_ready, 4 * n)
                dve.tensor_tensor(row_lo[:, :], k.bank[4 + n % 2], f32(row_hi[:, :]), ALU.subtract)\
                    .then_inc(row_lo_ready, 1)
                dve.tensor_tensor(am_hi[w][0][:, c, cols], f32(row_hi[:, :]), mask[0][:, c, cols], ALU.mult)\
                    .then_inc(am_ready, 1)
                dve.wait_ge(row_lo_ready, n + 1)
                dve.tensor_tensor(am_lo[w][0][:, c, cols], f32(row_lo[:, :]), mask[0][:, c, cols], ALU.mult)\
                    .then_inc(am_ready, 1)

            def mask_rows(j, half, n):
                dve.wait_ge(y_done, j + 1)
                need(dve, a2_added, j)
                cols = slice(half * HALF, (half + 1) * HALF)
                dve.tensor_tensor(masked[:, :, :], a2_ps, mask[n][:, :, cols], ALU.mult).then_inc(a2_masked, 1)

            def body(b, s, _more):
                for half in range(2):
                    cols = slice(half * HALF, (half + 1) * HALF)
                    for n in range(2):
                        j = b * 4 + half * 2 + n
                        dve.wait_ge(silu_ready, j + 1)
                        dve.wait_ge(x3_made, j + 1)
                        dve.tensor_tensor(act32[n][:, :], act32[n][:, :], x3_ps, ALU.mult).then_inc(gated_ready, 1)
                        dve.wait_ge(gated_ready, j + 1)
                        dve.tensor_tensor(act32[n][:, :], act32[n][:, :], weight_row[:, n, cols], ALU.mult)\
                            .then_inc(weighted_ready, 1)
                        dve.wait_ge(x2_hi_ready, j + 1)
                        dve.tensor_tensor(x2_lo[n][:, :], act32[n][:, :], f32(x2_hi[n][:, :]), ALU.subtract)\
                            .then_inc(x2_lo_ready, 1)
                        if not (static(b) and j == 0):
                            mask_rows(j - 1, half if n == 1 else 1 - half, 1 - n)

            over_blocks(dve, body)
            mask_rows(units - 1, 1, 1)
            for half in range(2):
                cols = slice(half * HALF, (half + 1) * HALF)
                dve.wait_ge(u_hi_ready, half + 1)
                dve.tensor_tensor(u_lo[:, :, cols], u[:, :, cols], f32(u_hi[:, :, cols]), ALU.subtract)\
                    .then_inc(u_lo_ready, 1)
            for half in range(2):
                cols = slice(half * HALF, (half + 1) * HALF)
                dve.wait_ge(y_whole, half + 1)
                for c in range(CH):
                    dve.scalar_tensor_tensor(k.x[:, c, cols], y[c][half], k.gates[:, gate:gate + 1], k.x[:, c, cols],
                                             ALU.mult, ALU.add).then_inc(k.x_ready, 1)

    k.at = base




def flamingo(nc, a, out):
    with ExitStack() as ctx:
        k = Core(nc, ctx)
        k.x = k.sb("x", [P, CH, TOK], F32)
        k.cen = k.sb("cen", [P, CH, TOK], F32)
        k.sq = k.sb("sq", [P, CH, TOK], F32)
        k.h_hi = k.sb("h_hi", [P, CH, TOK], F32R)
        k.h_lo = k.sb("h_lo", [P, CH, TOK], F32R)
        k.mean_w = k.sb("mean_w", [P, P], F32)
        k.ident = k.sb("ident", [P, P], F32)
        k.ident_bf = k.sb("ident_bf", [P, P], BF16)
        k.zeros = k.sb("zeros", [P, HALF], BF16)
        k.ctx_hi = k.sb("ctx_hi", [P, TOK], F32R)
        k.ctx_lo = k.sb("ctx_lo", [P, TOK], F32R)
        k.keys_hi = k.sb("keys_hi", [P, TILES, CD], F32R)
        k.keys_lo = k.sb("keys_lo", [P, TILES, CD], F32R)
        k.mask_bias = k.sb("mask_bias", [P, TOK], F32)
        k.any_key = k.sb("any_key", [P, B], F32)
        k.head_w = k.sb("head_w", [P, 1], F32)
        k.minus_half = k.sb("minus_half", [P, 1], F32)
        k.one = k.sb("one", [P, 1], F32)
        k.var = k.sb("var", [P, TILES], F32)
        k.rstd = k.sb("rstd", [P, TILES], F32)
        k.gates = k.sb("gates", [P, 8], F32)
        k.before = k.sb("before", [P, 256], F32)
        k.psum = ctx.enter_context(nc.psum_tensor("psum", [P, 8 * HALF], F32))
        k.bank = [k.psum[:, i * HALF:(i + 1) * HALF] for i in range(8)]

        base = k.at
        mask = k.sb("mask", [P, TOK], U8)
        ctx_raw = k.sb("ctx_raw", [P, TOK], F32)
        keys_raw = k.sb("keys_raw", [P, TILES, CD], F32)
        k.at = base
        ctx_loaded, parts_ready, mask_ready = k.sem("ctx_loaded"), k.sem("parts_ready"), k.sem("mask_ready")
        k.rope_freq = 0.01
        x_loaded, consts_loaded, const_set, stored = (k.sem(n) for n in (
            "x_loaded", "consts_loaded", "const_set", "stored"))
        with nc.Block() as block:

            @block.sync
            def _(sp):
                sp.dma_start(k.x[:, :, :], a["x"]).then_inc(x_loaded, 16)
                sp.dma_start(k.ident[:, :], a["ident"]).then_inc(consts_loaded, 16)
                sp.dma_start(k.before[:, :], a["before"].partition_broadcast(P)).then_inc(consts_loaded, 16)
                sp.dma_start(k.gates[:, 0:4], a["g_xattn"].partition_broadcast(P)).then_inc(consts_loaded, 16)
                sp.dma_start(k.gates[:, 4:8], a["g_ffn"].partition_broadcast(P)).then_inc(consts_loaded, 16)
                sp.dma_start(ctx_raw[:, :], a["ctx"]).then_inc(ctx_loaded, 16)
                sp.dma_start(keys_raw[:, :, :], a["keys"]).then_inc(ctx_loaded, 16)
                sp.dma_start(mask[:, :], a["mask"].partition_broadcast(P)).then_inc(ctx_loaded, 16)

            @block.gpsimd
            def _(pool):
                pool.memset(k.mean_w[:, :], 1.0 / D).then_inc(const_set, 1)
                pool.memset(k.zeros[:, :], 0.0).then_inc(const_set, 1)
                pool.memset(k.one[:, :], 1.0).then_inc(const_set, 1)
                pool.memset(k.minus_half[:, :], -0.5).then_inc(const_set, 1)
                pool.memset(k.head_w[:, :], 1.0 / HD).then_inc(const_set, 1)

            @block.scalar
            def _(act):
                act.wait_ge(consts_loaded, 64)
                act.activation(k.gates[:, :], k.gates[:, :], ACT.Tanh).then_inc(const_set, 1)
                act.activation(k.ident_bf[:, :], k.ident[:, :], ACT.Copy).then_inc(const_set, 1)
                act.wait_ge(ctx_loaded, 48)
                act.activation(k.ctx_hi[:, :], ctx_raw[:, :], ACT.Copy).then_inc(parts_ready, 1)
                act.activation(k.keys_hi[:, :, :], keys_raw[:, :, :], ACT.Copy).then_inc(parts_ready, 1)

            @block.vector
            def _(dve):
                dve.wait_ge(ctx_loaded, 48)
                dve.tensor_scalar(k.mask_bias[:, :], mask[:, :], 1.0e30, -1.0e30, ALU.mult, ALU.add)\
                    .then_inc(mask_ready, 1)
                dve.tensor_reduce(k.any_key[:, :], mask[:, :].rearrange("p (b n) -> p b n", b=B), AX_X, ALU.max)\
                    .then_inc(mask_ready, 1)
                dve.wait_ge(parts_ready, 2)
                dve.tensor_tensor(k.ctx_lo[:, :], ctx_raw[:, :], f32(k.ctx_hi[:, :]), ALU.subtract)\
                    .then_inc(parts_ready, 1)
                dve.tensor_tensor(k.keys_lo[:, :, :], keys_raw[:, :, :], f32(k.keys_hi[:, :, :]), ALU.subtract)\
                    .then_inc(parts_ready, 1)
                dve.wait_ge(const_set, 7)
                dve.wait_ge(x_loaded, 16)

        for step in STEPS:
            with nc.cleanup_on_exit():
                k.phase_sems()
                step(k, a)

        with nc.Block() as block:

            @block.sync
            def _(sp):
                sp.dma_start(out, k.x[:, :, :]).then_inc(stored, 16)
                sp.wait_ge(stored, 16)


def l0_ffn(k, a):
    ffn_phase(k, "f0", "sigmoid_top4", 16, True, 17, 4, a["f0_w"], a["f0_router"], a["f0_sel"], a["f0_bias"])


def l1_ffn(k, a):
    ffn_phase(k, "f1", "softmax_top2", 8, False, 32, 5, a["f1_w"], a["f1_router"], a["f1_sel"], None)


def l3_ffn(k, a):
    ffn_phase(k, "f3", "group_top4", 16, True, 25, 7, a["f3_w"], a["f3_router"], a["f3_sel"], None)


def l1_xattn(k, a):
    xattn_phase(k, "x1", True, 1, a["x1_w"], a["x1_gq"], a["x1_gk"], False)


def l3_xattn(k, a):
    xattn_phase(k, "x3", False, 3, a["x3_w"], None, None, True)


STEPS = (quant_phase, l0_ffn, l1_xattn, l1_ffn, rope_phase, lora_phase, l3_xattn, l3_ffn)




def _feature_major(w):
    return w.reshape(-1, P, w.shape[-1]).transpose(1, 0, 2)


def _ffn_blocks(np, gates, ups, downs):
    blocks = -(-gates.shape[0] // P)
    out = np.zeros((blocks, P, BLOCK), np.float32)
    for at, w in ((0, gates), (D, ups)):
        full = np.zeros((blocks * P, D), np.float32)
        full[:w.shape[0]] = w
        out[:, :, at:at + D] = full.reshape(blocks, P, CH, P).transpose(0, 3, 2, 1).reshape(blocks, P, D)
    full = np.zeros((blocks * P, D), np.float32)
    full[:downs.shape[1]] = downs.T
    out[:, :, 2 * D:] = full.reshape(blocks, P, D)
    return out


def _bf16(np, table):
    return (table.view(np.uint32) >> 16).astype(np.uint16)


def _select(np, widths, blocks):
    expert = np.repeat(np.arange(len(widths)), widths)
    sel = np.zeros((P, blocks * P), np.float32)
    for part in range(3):
        sel[32 * part + expert, np.arange(len(expert))] = 1.0
    return _bf16(np, sel)


def _heads(np, parts):
    return np.concatenate(parts, 2)


def _by_head(w):
    return w.reshape(w.shape[0], -1, HD).transpose(1, 0, 2)


def _columns(w):
    return w.reshape(CH, P, -1, P).transpose(2, 1, 0, 3).reshape(-1, P, CH * P)


def _slots(np):
    out = np.zeros((P, 8, P), np.float32)
    for c in range(CH):
        for row in range(P):
            expert = 4 * c + row // 32
            out[expert, c, row] = 1.0
            out[8 + expert, 2 + c, row] = 1.0
            out[8 + expert, 4 + c, row] = 1.0
            out[expert, 4 + c, row] = -1.0
    out[16:19, 6, :] = 1.0
    out[19:22, 7, :] = 1.0
    return out.reshape(P, 8 * P)


def _spread(np):
    out = np.zeros((P, 16, P), np.float32)
    for g in range(4):
        for s in range(GROUP):
            for d in range(SMALL):
                row = (GROUP * g + s) * SMALL + d
                for n, places in enumerate(((0, 16), (8, 24), (0, 8), (16, 24))):
                    for place in places:
                        out[row, 4 * g + n, 32 * s + place + d] = 1.0
    return out.reshape(P, 16 * P)


def _arrays(np, i):
    cat = np.concatenate
    flat = lambda w: w.reshape(-1, w.shape[-1])
    side = lambda w: w.transpose(1, 0, 2).reshape(w.shape[1], -1)
    a = {
        "x": _feature_major(i["x"].reshape(TOK, D).T),
        "g_xattn": i["g_xattn"], "g_ffn": i["g_ffn"],
        "ident": np.eye(P, dtype=np.float32),
        "before": np.tril(np.ones((16, 16), np.float32), -1).reshape(256),
        "fside": i["fside_BxS2xS2_0"].transpose(2, 0, 1).reshape(CH, P, TOK).transpose(1, 0, 2),
        "ctx": i["ctx_1024"].reshape(TOK, CD).T,
        "keys": i["ctx_1024"].reshape(TILES, P, CD).transpose(1, 0, 2),
        "mask": i["mask_BxS2_bf1"].reshape(TOK).view(np.uint8),
        "x1_w": _heads(np, [
            _by_head(i["L1_xattn_Wq"]).reshape(HEADS, CH, P, HD).transpose(0, 2, 1, 3).reshape(HEADS, P, D),
            _by_head(i["L1_xattn_Wk"]), _by_head(i["L1_xattn_Wv"]).transpose(0, 2, 1),
            i["L1_xattn_Wo"].reshape(HEADS, HD, D)]),
        "x1_gq": i["L1_xattn_gq"], "x1_gk": i["L1_xattn_gk"],
        "x3_w": _heads(np, [
            _by_head(i["L3_xattn_Wq"]).transpose(0, 2, 1),
            _by_head(i["L3_xattn_Wk"]).transpose(0, 2, 1)[np.arange(HEADS) // 2],
            _by_head(i["L3_xattn_Wv"]).transpose(0, 2, 1)[np.arange(HEADS) // 2],
            i["L3_xattn_Wo"].reshape(HEADS, HD, D)]),
        "r_pos": i["fside_BxSx2_0"].reshape(TILES, P, 2).transpose(1, 0, 2),
        "r_w": cat([_feature_major(i["L2_xattn_Wq"]).reshape(P, 512),
                    _feature_major(i["L2_xattn_Wq"][:, np.arange(D) ^ 1]).reshape(P, 512),
                    i["L2_xattn_Wkv"][:, :D], i["L2_xattn_Wkv"][:, np.arange(D) ^ 1], i["L2_xattn_Wkv"][:, D:],
                    _feature_major(i["L2_xattn_Wout"]).reshape(P, 512)], 1),
        "r_spread": _spread(np), "r_bout": i["L2_xattn_bout"].reshape(CH, P).T,
        "l_router": _feature_major(i["L2_ffn_Wg"].T),
        "l_small": cat([_feature_major(flat(i["L2_ffn_A1"]).T).reshape(P, 512),
                        _feature_major(flat(i["L2_ffn_A3"]).T).reshape(P, 512),
                        _feature_major(i["L2_ffn_B2"].transpose(0, 2, 1).reshape(D, D)).reshape(P, 512)], 1),
        "l_w": cat([_columns(i["L2_ffn_W1"].T), _columns(i["L2_ffn_W3"].T),
                    _columns(i["L2_ffn_B1"].transpose(0, 2, 1).reshape(D, -1)),
                    _columns(i["L2_ffn_B3"].transpose(0, 2, 1).reshape(D, -1)),
                    i["L2_ffn_W2"].T.reshape(-1, P, D), flat(i["L2_ffn_A2"]).T.reshape(-1, P, D)], 2),
        "l_select": _bf16(np, _slots(np)),
        "f0_w": _ffn_blocks(np, cat([flat(i["L0_ffn_expert_gate_w"]), i["L0_ffn_shared_gate_w"]]),
                            cat([flat(i["L0_ffn_expert_up_w"]), i["L0_ffn_shared_up_w"]]),
                            cat([side(i["L0_ffn_expert_down_w"]), i["L0_ffn_shared_down_w"]], 1)),
        "f0_router": _feature_major(i["L0_ffn_router_w"].T), "f0_bias": i["L0_ffn_router_bias"],
        "f0_sel": _select(np, [128] * 17, 17),
        "f1_w": _ffn_blocks(np, flat(i["L1_ffn_w0_kernel"].transpose(0, 2, 1)),
                            flat(i["L1_ffn_w1_kernel"].transpose(0, 2, 1)), flat(i["L1_ffn_wo_kernel"]).T),
        "f1_router": _feature_major(i["L1_ffn_gate_kernel"]), "f1_sel": _select(np, [512] * 8, 32),
        "f3_w": _ffn_blocks(np, cat([flat(i["L3_ffn_W1"]), i["L3_ffn_Ws1"]]),
                            cat([flat(i["L3_ffn_W3"]), i["L3_ffn_Ws3"]]),
                            cat([side(i["L3_ffn_W2"]), i["L3_ffn_Ws2"]], 1)),
        "f3_router": _feature_major(i["L3_ffn_gate_w"].T), "f3_sel": _select(np, [176] * 16 + [352], 25),
    }
    return a


def kernel(**inputs):
    import numpy as np
    import concourse.bacc as bacc
    from concourse.bass_utils import run_bass_kernel_spmd

    nc = bacc.Bacc("TRN2", target_bir_lowering=False, num_devices=1)
    arrays, args = {}, {}
    for name, value in _arrays(np, {n: np.asarray(v) for n, v in inputs.items()}).items():
        value = np.ascontiguousarray(value)
        arrays[f"in_{name}"] = value
        args[name] = nc.dram_tensor(f"in_{name}", value.shape, mybir.dt.from_np(value.dtype),
                                    kind="ExternalInput").ap()
    out = nc.dram_tensor("out", (P, CH, TOK), F32, kind="ExternalOutput").ap()
    for name in ("l_select", "f0_sel", "f1_sel", "f3_sel"):
        args[name] = args[name].bitcast(BF16)
    flamingo(nc, args, out)
    got = run_bass_kernel_spmd(nc, [arrays], core_ids=[0]).results[0]["out"]
    return got.transpose(2, 1, 0).reshape(B, S, D)
```

```python
from contextlib import ExitStack

import concourse.bass as bass
from concourse import mybir

ALU = mybir.AluOpType
ACT = mybir.ActivationFunctionType
AX_X = mybir.AxisListType.X
F32 = mybir.dt.float32
F32R = mybir.dt.float32r
BF16 = mybir.dt.bfloat16
U8 = mybir.dt.uint8

P = 128
B = 4
S = 256
TOK = B * S
D = 256
CH = D // P
CD = 128
HALF = TOK // 2
TILES = TOK // P
BLOCK = 3 * D


class Core:

    def __init__(self, nc, ctx):
        self.nc = nc
        self.ctx = ctx
        self.at = 17 * 1024
        self.phase = 0

    def sem(self, name):
        if self.phase:
            return self.nc.alloc_semaphore(name=name)
        return self.ctx.enter_context(self.nc.semaphore(name))

    def phase_sems(self):
        self.phase += 1
        names = ("mean_ready", "squared", "var_ready", "rstd_ready", "rstd_row_ready", "centred", "var_copied",
                 "normed", "h_hi_ready", "h_lo_ready", "x_ready")
        (self.mean_ready, self.squared, self.var_ready, self.rstd_ready, self.rstd_row_ready, self.centred,
         self.var_copied, self.normed, self.h_hi_ready, self.h_lo_ready, self.x_ready) = (
            self.sem(f"{name}{self.phase}") for name in names)

    def sb(self, name, shape, dt):
        size = 2 if dt == BF16 else 1 if dt == U8 else 4
        for n in shape[1:]:
            size *= n
        self.at = (self.at + 31) // 32 * 32
        t = self.nc.alloc_sbuf_tensor_at(name, shape, dt, offset=self.at)
        self.at += size
        return t


def f32(ap):
    return ap.bitcast(F32)


def mm3(pe, out, w_hi, w_lo, v_hi, v_lo, first, last):
    pe.matmul(out, w_hi, v_hi, start=first, stop=False)
    pe.matmul(out, w_lo, v_hi, start=False, stop=False)
    return pe.matmul(out, w_hi, v_lo, start=False, stop=last)


class Chain:

    def __init__(self, eng, sem, count=0):
        self.eng, self.sem, self.count = eng, sem, count

    def done(self, ins):
        self.count += 1
        ins.then_inc(self.sem, 1)
        self.eng.wait_ge(self.sem, self.count)




def norm_tensor(pe, k):
    for half in range(2):
        cols = slice(half * HALF, (half + 1) * HALF)
        for c in range(CH):
            last = pe.matmul(k.bank[half][:, :], k.mean_w[:, :], k.x[:, c, cols], start=(c == 0), stop=(c == CH - 1))
        last.then_inc(k.mean_ready, 1)
    for half in range(2):
        pe.wait_ge(k.squared, half + 1)
        for t in range(half * 4, half * 4 + 4):
            for c in range(CH):
                last = pe.matmul(k.bank[7][:, 504 + t:505 + t], k.sq[:, c, t * P:(t + 1) * P], k.mean_w[:, 0:1],
                                 start=(c == 0), stop=(c == CH - 1))
    last.then_inc(k.var_ready, 1)
    pe.wait_ge(k.rstd_ready, 1)
    for half in range(2):
        for t in range(4):
            last = pe.transpose(k.bank[2 + half][:, t * P:(t + 1) * P],
                                k.rstd[:, half * 4 + t:half * 4 + t + 1].to_broadcast([P, P]), k.ident[:, :])
        last.then_inc(k.rstd_row_ready, 1)


def norm_scalar(act, k, parts=True):
    for half in range(2):
        cols = slice(half * HALF, (half + 1) * HALF)
        act.wait_ge(k.centred, half + 1)
        act.activation(k.sq[:, :, cols], k.cen[:, :, cols], ACT.Square).then_inc(k.squared, 1)
    if parts:
        for half in range(2):
            cols = slice(half * HALF, (half + 1) * HALF)
            act.wait_ge(k.normed, half + 1)
            act.activation(k.h_hi[:, :, cols], k.cen[:, :, cols], ACT.Copy).then_inc(k.h_hi_ready, 1)


def norm_vector(dve, k, parts=True):
    for half in range(2):
        cols = slice(half * HALF, (half + 1) * HALF)
        dve.wait_ge(k.mean_ready, half + 1)
        dve.tensor_tensor(k.cen[:, :, cols], k.x[:, :, cols],
                          k.bank[half][:, :].unsqueeze(1).to_broadcast([P, CH, HALF]), ALU.subtract)\
            .then_inc(k.centred, 1)
    dve.wait_ge(k.var_ready, 1)
    dve.tensor_scalar(k.var[:, :], k.bank[7][:, 504:512], 1e-5, None, ALU.add).then_inc(k.var_copied, 1)
    for half in range(2):
        cols = slice(half * HALF, (half + 1) * HALF)
        dve.wait_ge(k.squared, half + 1)
        dve.wait_ge(k.rstd_row_ready, half + 1)
        dve.tensor_tensor(k.cen[:, :, cols], k.cen[:, :, cols],
                          k.bank[2 + half][:, :].unsqueeze(1).to_broadcast([P, CH, HALF]), ALU.mult)\
            .then_inc(k.normed, 1)
    if parts:
        dve.wait_ge(k.h_hi_ready, 2)
        dve.tensor_tensor(k.h_lo[:, :, cols], k.cen[:, :, cols], f32(k.h_hi[:, :, cols]), ALU.subtract)\
            .then_inc(k.h_lo_ready, 1)


def norm_gpsimd(pool, k, parts=True):
    pool.wait_ge(k.var_copied, 1)
    pool.tensor_tensor(k.rstd[:, :], k.var[:, :], k.minus_half[:, :].to_broadcast([P, TILES]), ALU.pow)\
        .then_inc(k.rstd_ready, 1)
    if parts:
        pool.wait_ge(k.h_hi_ready, 1)
        pool.tensor_tensor(k.h_lo[:, :, 0:HALF], k.cen[:, :, 0:HALF], f32(k.h_hi[:, :, 0:HALF]), ALU.subtract)\
            .then_inc(k.h_lo_ready, 1)




def rank(dve, chain, k, out, values, n, tiles=TILES):
    gt = k.cmp_gt[:, 0:tiles * n * n].rearrange("p (t i j) -> p t i j", t=tiles, i=n)
    eq = k.cmp_eq[:, 0:tiles * n * n].rearrange("p (t i j) -> p t i j", t=tiles, i=n)
    before = k.before[:, :].rearrange("p (i j) -> p i j", i=16)[:, 0:n, 0:n]
    vj = values.unsqueeze(2).to_broadcast([P, tiles, n, n])
    vi = values.unsqueeze(3).to_broadcast([P, tiles, n, n])
    dve.tensor_tensor(gt, vj, vi, ALU.is_gt)
    chain.done(dve.tensor_tensor(eq, vj, vi, ALU.is_equal))
    chain.done(dve.tensor_tensor(eq, eq, before.unsqueeze(1).to_broadcast([P, tiles, n, n]), ALU.mult))
    chain.done(dve.tensor_tensor(gt, gt, eq, ALU.add))
    chain.done(dve.tensor_reduce(out, gt, AX_X, ALU.add))


def route_vector(dve, chain, k, f):
    n = f.experts
    if f.kind == "sigmoid_top4":
        dve.wait_ge(f.score_ready, 1)
        chain.done(dve.tensor_tensor(f.choice[:, :, :], f.score[:, :, :],
                                     f.bias[:, :].unsqueeze(1).to_broadcast([P, TILES, n]), ALU.add))
        rank(dve, chain, k, f.rank[:, :, :], f.choice[:, :, :], n)
        keep = 4
    elif f.kind == "group_top4":
        dve.wait_ge(f.score_ready, 1)
        groups = n // 4
        chain.done(dve.tensor_reduce(f.group[:, :, :], f.score[:, :, :].rearrange("p t (g e) -> p t g e", e=4),
                                     AX_X, ALU.max))
        rank(dve, chain, k, f.group_rank[:, :, :], f.group[:, :, :], groups)
        chain.done(dve.tensor_scalar(f.group[:, :, :], f.group_rank[:, :, :], 2.0, None, ALU.is_lt))
        chain.done(dve.tensor_tensor(f.choice[:, :, :].rearrange("p t (g e) -> p (t g) e", e=4),
                                     f.score[:, :, :].rearrange("p t (g e) -> p (t g) e", e=4),
                                     f.group[:, :, :].rearrange("p t g -> p (t g)").unsqueeze(2)
                                     .to_broadcast([P, TILES * groups, 4]), ALU.mult))
        rank(dve, chain, k, f.rank[:, :, :], f.choice[:, :, :], n)
        keep = 4
    else:
        dve.wait_ge(f.logits_ready, 1)
        chain.done(dve.tensor_copy(f.choice[:, :, :], f.logits))
        chain.done(dve.tensor_reduce(f.top[:, :], f.choice[:, :, :], AX_X, ALU.max))
        dve.tensor_tensor(f.shifted[:, :, :], f.choice[:, :, :],
                          f.top[:, :].unsqueeze(2).to_broadcast([P, TILES, n]), ALU.subtract)\
            .then_inc(f.shifted_ready, 1)
        rank(dve, chain, k, f.rank[:, :, :], f.choice[:, :, :], n)
        dve.wait_ge(f.score_ready, 1)
        keep = 2
    chain.done(dve.scalar_tensor_tensor(f.chosen[:, :, :], f.rank[:, :, :], float(keep), f.score[:, :, :],
                                        ALU.is_lt, ALU.mult))
    chain.done(dve.tensor_reduce(f.total[:, :], f.chosen[:, :, :], AX_X, ALU.add))
    if f.kind == "sigmoid_top4":
        chain.done(dve.tensor_scalar(f.total[:, :], f.total[:, :], 1e-20, None, ALU.add))
    chain.done(dve.reciprocal(f.total[:, :], f.total[:, :]))
    chain.done(dve.tensor_tensor(f.comb[:, :, 0:n], f.chosen[:, :, :],
                                 f.total[:, :].unsqueeze(2).to_broadcast([P, TILES, n]), ALU.mult))


def three_parts(dve, chain, parts, values, rest, n):
    chain.done(dve.tensor_copy(parts[:, :, 0:n], values))
    chain.done(dve.tensor_tensor(rest, values, parts[:, :, 0:n], ALU.subtract))
    chain.done(dve.tensor_copy(parts[:, :, 32:32 + n], rest))
    chain.done(dve.tensor_tensor(rest, rest, parts[:, :, 32:32 + n], ALU.subtract))
    return dve.tensor_copy(parts[:, :, 64:64 + n], rest)


class Ffn:
    pass


def ffn_phase(k, tag, kind, experts, shared, blocks, gate, weights, router, select, bias):
    nc = k.nc
    f = Ffn()
    f.kind, f.experts = kind, experts
    base = k.at
    rows = experts + (1 if shared else 0)
    raw = [k.sb(f"{tag}_raw{s}", [P, BLOCK], F32) for s in range(2)]
    w_hi = [k.sb(f"{tag}_w_hi{s}", [P, BLOCK], F32R) for s in range(2)]
    w_lo = [k.sb(f"{tag}_w_lo{s}", [P, BLOCK], F32R) for s in range(2)]
    silu = [k.sb(f"{tag}_silu{s}", [P, HALF], F32) for s in range(2)]
    gated = [k.sb(f"{tag}_gated{s}", [P, HALF], F32) for s in range(2)]
    act32 = [k.sb(f"{tag}_act32{s}", [P, HALF], F32) for s in range(2)]
    a_hi = [k.sb(f"{tag}_a_hi{s}", [P, HALF], F32R) for s in range(2)]
    a_lo = [k.sb(f"{tag}_a_lo{s}", [P, HALF], F32R) for s in range(2)]
    sel = k.sb(f"{tag}_sel", [P, blocks * P], BF16)
    rw = k.sb(f"{tag}_rw", [P, CH, experts], F32)
    rw_hi = k.sb(f"{tag}_rw_hi", [P, CH, experts], F32R)
    rw_lo = k.sb(f"{tag}_rw_lo", [P, CH, experts], F32R)
    if bias is not None:
        f.bias = k.sb(f"{tag}_bias", [P, experts], F32)
    f.score, f.choice, f.shifted, f.rank, f.chosen = (
        k.sb(f"{tag}_{name}", [P, TILES, experts], F32) for name in ("score", "choice", "shifted", "rank", "chosen"))
    k.cmp_gt = k.sb(f"{tag}_cmp_gt", [P, TILES * 256], BF16)
    k.cmp_eq = k.sb(f"{tag}_cmp_eq", [P, TILES * 256], BF16)
    f.group = k.sb(f"{tag}_group", [P, TILES, 4], F32)
    f.group_rank = k.sb(f"{tag}_group_rank", [P, TILES, 4], F32)
    f.top = k.sb(f"{tag}_top", [P, TILES], F32)
    f.total = k.sb(f"{tag}_total", [P, TILES], F32)
    f.comb = k.sb(f"{tag}_comb", [P, TILES, rows], F32)
    rest = k.sb(f"{tag}_rest", [P, TILES, rows], F32)
    parts = k.sb(f"{tag}_parts", [P, TILES, P], BF16)
    comb_t = k.sb(f"{tag}_comb_t", [P, TOK], BF16)

    names = ("small_loaded", "router_hi", "router_lo", "zeroed", "logits_ready", "shifted_ready", "score_ready",
             "chain", "parts_ready", "turned", "comb_t_ready", "w_hi_ready", "w_lo_ready", "g_ready", "u_ready",
             "cb_ready", "silu_ready", "gated_ready", "act_ready", "a_hi_ready", "a_lo_ready", "y_done")
    sem = {name: k.sem(f"{tag}_{name}") for name in names}
    raw_loaded = [k.sem(f"{tag}_raw_loaded{s}") for s in range(2)]
    f.logits_ready, f.shifted_ready, f.score_ready = sem["logits_ready"], sem["shifted_ready"], sem["score_ready"]
    small_loaded, chain_sem, y_done = sem["small_loaded"], sem["chain"], sem["y_done"]
    w_hi_ready, w_lo_ready = sem["w_hi_ready"], sem["w_lo_ready"]
    g_ready, u_ready, cb_ready = sem["g_ready"], sem["u_ready"], sem["cb_ready"]
    silu_ready, gated_ready, act_ready = sem["silu_ready"], sem["gated_ready"], sem["act_ready"]
    a_hi_ready, a_lo_ready = sem["a_hi_ready"], sem["a_lo_ready"]

    y = [[k.bank[2 * c + half] for half in range(2)] for c in range(CH)]
    g_ps, u_ps, cb_ps = k.bank[4], k.bank[5], k.bank[6]
    f.logits = k.bank[7][:, 0:TILES * experts].rearrange("p (t e) -> p t e", e=experts)
    turned = k.bank[7][:, :].bitcast(BF16)
    small_loads = 2 + (1 if bias is not None else 0)

    loop_to = (blocks - 1) // 2

    def over_blocks(eng, body):
        body(0, 0, True)
        body(1, 1, True)
        with eng.Fori(1, loop_to) as pair:
            body(pair * 2, 0, True)
            body(pair * 2 + 1, 1, True)
        for b in range(2 * loop_to, blocks):
            body(b, b % 2, b + 1 < blocks)

    def static(b):
        return isinstance(b, int)

    with nc.Block() as block:

        @block.sync
        def _(sp):
            sp.dma_start(raw[0][:, :], weights[0, :, :]).then_inc(raw_loaded[0], 16)
            sp.dma_start(rw[:, :, :], router).then_inc(small_loaded, 16)
            sp.dma_start(sel[:, :], select).then_inc(small_loaded, 16)
            if bias is not None:
                sp.dma_start(f.bias[:, :], bias.partition_broadcast(P)).then_inc(small_loaded, 16)
            sp.dma_start(raw[1][:, :], weights[1, :, :]).then_inc(raw_loaded[1], 16)

            def load(b, s):
                sp.wait_ge(w_hi_ready, b - 1)
                sp.wait_ge(w_lo_ready, b - 1)
                sp.dma_start(raw[s][:, :], weights[bass.ds(b, 1), :, :].rearrange("b p n -> p (b n)"))\
                    .then_inc(raw_loaded[s], 16)

            with sp.Fori(1, loop_to) as pair:
                load(pair * 2, 0)
                load(pair * 2 + 1, 1)
            for b in range(2 * loop_to, blocks):
                load(b, b % 2)

        @block.tensor
        def _(pe):
            norm_tensor(pe, k)
            pe.wait_ge(k.h_hi_ready, 2)
            pe.wait_ge(k.h_lo_ready, 2)
            pe.wait_ge(sem["router_hi"], 1)
            pe.wait_ge(sem["router_lo"], 1)
            for t in range(TILES):
                cols = slice(t * P, (t + 1) * P)
                for c in range(CH):
                    last = mm3(pe, f.logits[:, t, :], k.h_hi[:, c, cols], k.h_lo[:, c, cols], rw_hi[:, c, :],
                               rw_lo[:, c, :], c == 0, c == CH - 1)
            last.then_inc(f.logits_ready, 1)
            pe.wait_ge(sem["zeroed"], 1)
            for c in range(CH):
                for half in range(2):
                    pe.matmul(y[c][half][:, :], k.zeros[:, 0:P], k.zeros[:, :], start=True, stop=False)

            def add_y(j, half, s, last_block=False):
                pe.wait_ge(a_hi_ready, j + 1)
                pe.wait_ge(a_lo_ready, j + 1)
                for c in range(CH):
                    w = slice(2 * D + c * P, 2 * D + (c + 1) * P)
                    last = mm3(pe, y[c][half][:, :], w_hi[s][:, w], w_lo[s][:, w], a_hi[half][:, :],
                               a_lo[half][:, :], False, last_block)
                last.then_inc(y_done, 1)

            def body(b, s, _more):
                pe.wait_ge(w_hi_ready, b + 1)
                pe.wait_ge(w_lo_ready, b + 1)
                for half in range(2):
                    j = b * 2 + half
                    cols = slice(half * HALF, (half + 1) * HALF)
                    first = static(b) and j == 0
                    for out, at, ready, free in ((g_ps, 0, g_ready, silu_ready), (u_ps, D, u_ready, gated_ready)):
                        if not first:
                            pe.wait_ge(free, j)
                        for c in range(CH):
                            w = slice(at + c * P, at + (c + 1) * P)
                            last = mm3(pe, out[:, :], w_hi[s][:, w], w_lo[s][:, w], k.h_hi[:, c, cols],
                                       k.h_lo[:, c, cols], c == 0, c == CH - 1)
                        last.then_inc(ready, 1)
                    if first:
                        for t in range(TILES):
                            if t == 0:
                                pe.wait_ge(sem["parts_ready"], 1)
                            last = pe.transpose(turned[:, t * P:(t + 1) * P], parts[:, t, :], k.ident_bf[:, :])
                        last.then_inc(sem["turned"], 1)
                        pe.wait_ge(sem["comb_t_ready"], 1)
                    else:
                        pe.wait_ge(act_ready, j)
                    sel_b = sel[:, bass.ds(b * P, P)]
                    pe.matmul(cb_ps[:, :], sel_b, comb_t[:, cols], start=True, stop=True).then_inc(cb_ready, 1)
                    if not first:
                        add_y(j - 1, 1 - half, 1 - s if half == 0 else s,
                              static(b) and b == blocks - 1 and half == 1)

            over_blocks(pe, body)
            add_y(2 * blocks - 1, 1, (blocks - 1) % 2, True)

        @block.scalar
        def _(act):
            def split(b, s):
                act.wait_ge(raw_loaded[s], (b // 2) * 16 + 16 if static(b) else b * 8 + (16 - 8 * s))
                if not static(b) or b >= 2:
                    act.wait_ge(y_done, b * 2 - 2)
                act.activation(w_hi[s][:, :], raw[s][:, :], ACT.Copy).then_inc(w_hi_ready, 1)

            split(0, 0)
            act.wait_ge(small_loaded, 16 * small_loads)
            act.activation(rw_hi[:, :, :], rw[:, :, :], ACT.Copy).then_inc(sem["router_hi"], 1)
            norm_scalar(act, k)
            if kind == "softmax_top2":
                act.wait_ge(f.shifted_ready, 1)
                act.activation(f.score[:, :, :], f.shifted[:, :, :], ACT.Exp).then_inc(f.score_ready, 1)
            else:
                act.wait_ge(f.logits_ready, 1)
                act.activation(f.score[:, :, :], f.logits, ACT.Sigmoid).then_inc(f.score_ready, 1)

            def body(b, s, more):
                for half in range(2):
                    j = b * 2 + half
                    act.wait_ge(g_ready, j + 1)
                    if not static(b) or j >= 2:
                        act.wait_ge(gated_ready, j - 1)
                    act.activation(silu[half][:, :], g_ps[:, :], ACT.Silu).then_inc(silu_ready, 1)
                    act.wait_ge(act_ready, j + 1)
                    if not static(b) or j >= 2:
                        act.wait_ge(y_done, j - 1)
                    act.activation(a_hi[half][:, :], act32[half][:, :], ACT.Copy).then_inc(a_hi_ready, 1)
                    if half == 0 and more:
                        split(b + 1, 1 - s)

            over_blocks(act, body)

        @block.gpsimd
        def _(pool):
            pool.memset(parts[:, :, :], 0.0).then_inc(sem["zeroed"], 1)

            def split(b, s):
                pool.wait_ge(w_hi_ready, b + 1)
                pool.tensor_tensor(w_lo[s][:, :], raw[s][:, :], f32(w_hi[s][:, :]), ALU.subtract)\
                    .then_inc(w_lo_ready, 1)

            split(0, 0)
            pool.wait_ge(sem["router_hi"], 1)
            pool.tensor_tensor(rw_lo[:, :, :], rw[:, :, :], f32(rw_hi[:, :, :]), ALU.subtract)\
                .then_inc(sem["router_lo"], 1)
            norm_gpsimd(pool, k)
            split(1, 1)
            with pool.Fori(1, loop_to) as pair:
                split(pair * 2, 0)
                split(pair * 2 + 1, 1)
            for b in range(2 * loop_to, blocks):
                split(b, b % 2)

        @block.vector
        def _(dve):
            chain = Chain(dve, chain_sem)
            norm_vector(dve, k)
            dve.wait_ge(sem["zeroed"], 1)
            dve.wait_ge(small_loaded, 16 * small_loads)
            route_vector(dve, chain, k, f)
            if shared:
                chain.done(dve.memset(f.comb[:, :, experts:experts + 1], 1.0))
            three_parts(dve, chain, parts, f.comb[:, :, :], rest[:, :, :], rows).then_inc(sem["parts_ready"], 1)
            dve.wait_ge(sem["turned"], 1)
            dve.tensor_copy(comb_t[:, :], turned).then_inc(sem["comb_t_ready"], 1)

            def body(b, _s, _more):
                for half in range(2):
                    j = b * 2 + half
                    dve.wait_ge(silu_ready, j + 1)
                    dve.wait_ge(u_ready, j + 1)
                    dve.tensor_tensor(gated[half][:, :], silu[half][:, :], u_ps[:, :], ALU.mult)\
                        .then_inc(gated_ready, 1)
                    dve.wait_ge(gated_ready, j + 1)
                    dve.wait_ge(cb_ready, j + 1)
                    dve.tensor_tensor(act32[half][:, :], gated[half][:, :], cb_ps[:, :], ALU.mult)\
                        .then_inc(act_ready, 1)
                    dve.wait_ge(a_hi_ready, j + 1)
                    dve.tensor_tensor(a_lo[half][:, :], act32[half][:, :], f32(a_hi[half][:, :]), ALU.subtract)\
                        .then_inc(a_lo_ready, 1)

            over_blocks(dve, body)
            for half in range(2):
                cols = slice(half * HALF, (half + 1) * HALF)
                dve.wait_ge(y_done, 2 * blocks - 1 + half)
                for c in range(CH):
                    dve.scalar_tensor_tensor(k.x[:, c, cols], y[c][half][:, :], k.gates[:, gate:gate + 1],
                                             k.x[:, c, cols], ALU.mult, ALU.add).then_inc(k.x_ready, 1)

    k.at = base



HEADS = 16
HD = 128
STEPS_PER_HEAD = B


def need(eng, sem, value):
    if not isinstance(value, int) or value > 0:
        eng.wait_ge(sem, value)


def over_heads(eng, body):
    body(0, 0, True, False, False)
    body(1, 1, False, False, False)
    with eng.Fori(1, HEADS // 2 - 1) as pair:
        body(pair * 2, 0, False, False, False)
        body(pair * 2 + 1, 1, False, False, False)
    body(HEADS - 2, 0, False, True, False)
    body(HEADS - 1, 1, False, True, True)


def xattn_phase(k, tag, normed, gate, weights, gq, gk, masked):
    nc = k.nc
    base = k.at
    scale = float(HD) ** -0.5
    raw = k.sb(f"{tag}_raw", [P, BLOCK], F32)
    w_his = [k.sb(f"{tag}_w_hi{s}", [P, BLOCK], F32R) for s in range(2)]
    w_los = [k.sb(f"{tag}_w_lo{s}", [P, BLOCK], F32R) for s in range(2)]
    vo_hi = k.sb(f"{tag}_vo_hi", [P, D], F32R)
    vo_lo = k.sb(f"{tag}_vo_lo", [P, D], F32R)
    q_hi = [k.sb(f"{tag}_q_hi{s}", [P, S], F32R) for s in range(2)]
    q_lo = [k.sb(f"{tag}_q_lo{s}", [P, S], F32R) for s in range(2)]
    if normed:
        q_sq = k.sb(f"{tag}_q_sq", [P, S], F32)
        k_sq = k.sb(f"{tag}_k_sq", [P, S], F32)
        k_raw = [k.sb(f"{tag}_k_raw{s}", [P, S], F32) for s in range(2)]
        k32 = k.sb(f"{tag}_k32", [P, S], F32)
        k_hi = [k.sb(f"{tag}_k_hi{s}", [P, S], F32R) for s in range(2)]
        k_lo = [k.sb(f"{tag}_k_lo{s}", [P, S], F32R) for s in range(2)]
        rms = k.sb(f"{tag}_rms", [P, 4], F32)
        rrms = [k.sb(f"{tag}_rrms{s}", [P, 4], F32) for s in range(2)]
        gain = k.sb(f"{tag}_gain", [P, 2], F32)
        gains = k.sb(f"{tag}_gains", [P, 1], F32)
    else:
        am_his = [k.sb(f"{tag}_am_hi{s}", [P, CH, CD], F32R) for s in range(2)]
        am_los = [k.sb(f"{tag}_am_lo{s}", [P, CH, CD], F32R) for s in range(2)]
        s_masked = k.sb(f"{tag}_s_masked", [P, 2, S], F32)
        unread = k.sb(f"{tag}_unread", [P, 1], F32)
    probs = k.sb(f"{tag}_probs", [P, 2, S], F32)
    top = k.sb(f"{tag}_top", [P, 2], F32)
    shift = k.sb(f"{tag}_shift", [P, 2], F32)
    total = k.sb(f"{tag}_total", [P, 2], F32)
    rtotal = k.sb(f"{tag}_rtotal", [P, 2], F32)
    pt_hi = k.sb(f"{tag}_pt_hi", [P, 2, S], F32R)
    pt_lo = k.sb(f"{tag}_pt_lo", [P, 2, S], F32R)
    z_hi = k.sb(f"{tag}_z_hi", [P, S], F32R)
    z_lo = k.sb(f"{tag}_z_lo", [P, S], F32R)

    def sem(name):
        return k.sem(f"{tag}_{name}")

    raw_loaded, small_loaded, small_ready = sem("raw_loaded"), sem("small_loaded"), sem("small_ready")
    w_hi_ready, w_lo_ready = sem("w_hi_ready"), sem("w_lo_ready")
    vo_made, vo_hi_ready, vo_lo_ready = sem("vo_made"), sem("vo_hi_ready"), sem("vo_lo_ready")
    am_made, am_hi_ready, am_lo_ready = sem("am_made"), sem("am_hi_ready"), sem("am_lo_ready")
    q_made, q_hi_ready, q_lo_ready = sem("q_made"), sem("q_hi_ready"), sem("q_lo_ready")
    k_copied, squares_ready, stats_ready, rms_ready = (
        sem("k_copied"), sem("squares_ready"), sem("stats_ready"), sem("rms_ready"))
    rrms_ready, row_ready, k_normed = sem("rrms_ready"), sem("row_ready"), sem("k_normed")
    k_hi_ready, k_lo_ready = sem("k_hi_ready"), sem("k_lo_ready")
    scores_ready, top_ready, shift_ready = sem("scores_ready"), sem("top_ready"), sem("shift_ready")
    exp_ready, rtotal_ready, probs_ready = sem("exp_ready"), sem("rtotal_ready"), sem("probs_ready")
    turned, pt_hi_ready, pt_lo_ready = sem("turned"), sem("pt_hi_ready"), sem("pt_lo_ready")
    z_made, z_hi_ready, z_lo_ready, y_done = sem("z_made"), sem("z_hi_ready"), sem("z_lo_ready"), sem("y_done")

    y = [[k.bank[2 * c + half] for half in range(2)] for c in range(CH)]
    q_ps, k_ps = k.bank[4][:, 0:S], k.bank[4][:, S:2 * S]
    s_ps = k.bank[5][:, :].rearrange("p (t n) -> p t n", t=2)
    t_ps = k.bank[6][:, :].rearrange("p (t n) -> p t n", t=2)
    z_ps, am_ps = k.bank[7][:, 0:S], k.bank[7][:, S:2 * S]
    row_ps, stats_ps = k.bank[6][:, 0:S], k.bank[7][:, S:S + 4]
    steps = HEADS * STEPS_PER_HEAD

    with nc.Block() as block:

        @block.sync
        def _(sp):
            sp.dma_start(raw[:, :], weights[0, :, :]).then_inc(raw_loaded, 16)
            if normed:
                sp.dma_start(gain[:, 0:1], gq.unsqueeze(1)).then_inc(small_loaded, 16)
                sp.dma_start(gain[:, 1:2], gk.unsqueeze(1)).then_inc(small_loaded, 16)
            with sp.Fori(1, HEADS) as h:
                sp.wait_ge(w_hi_ready, h)
                sp.wait_ge(w_lo_ready, h)
                sp.dma_start(raw[:, :], weights[bass.ds(h, 1), :, :].rearrange("h p n -> p (h n)"))\
                    .then_inc(raw_loaded, 16)

        @block.tensor
        def _(pe):
            norm_tensor(pe, k)

            def make_am(h, s):
                w_hi, w_lo = w_his[s], w_los[s]
                pe.wait_ge(w_hi_ready, h + 1)
                pe.wait_ge(w_lo_ready, h + 1)
                need(pe, z_hi_ready, (h - 1) * STEPS_PER_HEAD)
                need(pe, z_lo_ready, (h - 1) * STEPS_PER_HEAD)
                for c in range(CH):
                    w = slice(c * P, (c + 1) * P)
                    last = mm3(pe, am_ps[:, c * CD:(c + 1) * CD], w_hi[:, w], w_lo[:, w], w_hi[:, D:D + CD],
                               w_lo[:, D:D + CD], True, True)
                last.then_inc(am_made, 1)

            def bank_left(j):
                need(pe, q_hi_ready, j)
                need(pe, q_lo_ready, j)
                if normed:
                    need(pe, squares_ready, 2 * j)
                    need(pe, k_copied, j)

            def make_vo(s, j):
                w_hi, w_lo = w_his[s], w_los[s]
                bank_left(j + 1)
                w = slice(D + CD, 2 * D)
                mm3(pe, q_ps, w_hi[:, w], w_lo[:, w], w_hi[:, 2 * D:], w_lo[:, 2 * D:], True, True)\
                    .then_inc(vo_made, 1)

            def project(h, s, b, j):
                w_hi, w_lo = w_his[s], w_los[s]
                if b == 0:
                    if normed:
                        pe.wait_ge(w_hi_ready, h + 1)
                        pe.wait_ge(w_lo_ready, h + 1)
                    else:
                        pe.wait_ge(am_hi_ready, h + 1)
                        pe.wait_ge(am_lo_ready, h + 1)
                if b == 0:
                    need(pe, vo_hi_ready, h)
                    need(pe, vo_lo_ready, h)
                bank_left(j)
                cols = slice(b * S, (b + 1) * S)
                for c in range(CH):
                    if normed:
                        part_hi, part_lo = w_hi[:, c * P:(c + 1) * P], w_lo[:, c * P:(c + 1) * P]
                    else:
                        part_hi, part_lo = am_his[s][:, c, :], am_los[s][:, c, :]
                    last = mm3(pe, q_ps, part_hi, part_lo, k.h_hi[:, c, cols], k.h_lo[:, c, cols], c == 0,
                               c == CH - 1)
                if normed:
                    last = mm3(pe, k_ps, w_hi[:, D:D + CD], w_lo[:, D:D + CD], k.ctx_hi[:, cols], k.ctx_lo[:, cols],
                               True, True)
                last.then_inc(q_made, 1)

            def stats(j):
                pe.wait_ge(squares_ready, 2 * j + 2)
                need(pe, rms_ready, j)
                need(pe, z_hi_ready, j - 3)
                need(pe, z_lo_ready, j - 3)
                for n, sq in enumerate((q_sq, k_sq)):
                    for t in range(2):
                        last = pe.matmul(stats_ps[:, 2 * n + t:2 * n + t + 1], sq[:, t * P:(t + 1) * P],
                                         k.head_w[:, :], start=True, stop=True)
                last.then_inc(stats_ready, 1)

            def key_row(s, j):
                pe.wait_ge(rrms_ready, j + 1)
                need(pe, pt_hi_ready, j - 1)
                need(pe, pt_lo_ready, j - 1)
                for t in range(2):
                    last = pe.transpose(row_ps[:, t * P:(t + 1) * P], rrms[s][:, 2 + t:3 + t].to_broadcast([P, P]),
                                        k.ident[:, :])
                last.then_inc(row_ready, 1)

            def scores(b, j):
                s = b % 2
                cols = slice(b * S, (b + 1) * S)
                pe.wait_ge(q_hi_ready, j + 1)
                pe.wait_ge(q_lo_ready, j + 1)
                if normed:
                    pe.wait_ge(k_hi_ready, j + 1)
                    pe.wait_ge(k_lo_ready, j + 1)
                    need(pe, exp_ready, 2 * j)
                    right_hi, right_lo = k_hi[s][:, :], k_lo[s][:, :]
                else:
                    need(pe, top_ready, 2 * j)
                    right_hi, right_lo = k.ctx_hi[:, cols], k.ctx_lo[:, cols]
                for t in range(2):
                    rows = slice(t * P, (t + 1) * P)
                    last = mm3(pe, s_ps[:, t, :], q_hi[s][:, rows], q_lo[s][:, rows], right_hi, right_lo, True, True)
                last.then_inc(scores_ready, 1)

            def turn(j, end=False):
                pe.wait_ge(probs_ready, j + 1)
                if normed:
                    pe.wait_ge(k_normed, steps if end else j + 2)
                need(pe, pt_lo_ready, j)
                need(pe, pt_hi_ready, j)
                for kt in range(2):
                    for t in range(2):
                        last = pe.transpose(t_ps[:, kt, t * P:(t + 1) * P], probs[:, t, kt * P:(kt + 1) * P],
                                            k.ident[:, :])
                last.then_inc(turned, 1)

            def mix(b, j, next_am=0, ending=False):
                if normed and ending:
                    pe.wait_ge(rms_ready, steps)
                pe.wait_ge(pt_hi_ready, j + 1)
                pe.wait_ge(pt_lo_ready, j + 1)
                need(pe, z_hi_ready, j)
                need(pe, z_lo_ready, j)
                if not normed and b == 0:
                    need(pe, am_hi_ready, next_am)
                    need(pe, am_lo_ready, next_am)
                for kt in range(2):
                    last = mm3(pe, z_ps, k.keys_hi[:, 2 * b + kt, :], k.keys_lo[:, 2 * b + kt, :], pt_hi[:, kt, :],
                               pt_lo[:, kt, :], kt == 0, kt == 1)
                last.then_inc(z_made, 1)

            def add_y(h, b, j, end=False):
                pe.wait_ge(z_hi_ready, j + 1)
                pe.wait_ge(z_lo_ready, j + 1)
                if b == 0:
                    pe.wait_ge(vo_hi_ready, h + 1)
                    pe.wait_ge(vo_lo_ready, h + 1)
                cols = slice(b % 2 * S, (b % 2 + 1) * S)
                for c in range(CH):
                    w = slice(c * P, (c + 1) * P)
                    last = mm3(pe, y[c][b // 2][:, cols], vo_hi[:, w], vo_lo[:, w], z_hi[:, :], z_lo[:, :], False,
                               end and b % 2 == 1)
                last.then_inc(y_done, 1)

            pe.wait_ge(k.normed, 2)
            for c in range(CH):
                for half in range(2):
                    pe.matmul(y[c][half][:, :], k.zeros[:, 0:P], k.zeros[:, :], start=True, stop=False)
            if not normed:
                make_am(0, 0)
            pe.wait_ge(k.h_hi_ready, 2)
            pe.wait_ge(k.h_lo_ready, 2)
            for j in range(2):
                project(0, 0, j, j)
                if normed:
                    stats(j)
                if normed and j == 0:
                    key_row(j, j)

            def body(h, slot, first, ending, last):
                for b in range(STEPS_PER_HEAD):
                    j = h * STEPS_PER_HEAD + b
                    more = not (last and b >= 2)
                    next_key = normed and not (last and b == 3)
                    scores(b, j)
                    if not (first and b == 0):
                        turn(j - 1)
                    if more:
                        if b < 2:
                            project(h, slot, b + 2, j + 2)
                        else:
                            project(h + 1, 1 - slot, b - 2, j + 2)
                    if b == 1 and not last and not normed:
                        make_am(h + 1, 1 - slot)
                    if not (first and b < 2):
                        add_y(h if b >= 2 else h - 1, (b + 2) % 4, j - 2, last and b >= 2)
                    if next_key:
                        key_row((b + 1) % 2, j + 1)
                    if more and normed:
                        stats(j + 2)
                    if not (first and b == 0):
                        mix((b + 3) % 4, j - 1, 0 if last else h + 2, not more)
                    if b == 1:
                        make_vo(slot, j + 2)

            over_heads(pe, body)
            turn(steps - 1, True)
            add_y(HEADS - 1, 2, steps - 2, True)
            mix(3, steps - 1, 0, True)
            add_y(HEADS - 1, 3, steps - 1, True)

        @block.scalar
        def _(act):
            def split(h, s):
                act.wait_ge(raw_loaded, h * 16 + 16)
                need(act, vo_made, h - 1)
                if normed:
                    need(act, q_made, (h - 1) * STEPS_PER_HEAD)
                else:
                    need(act, am_made, h - 1)
                act.activation(w_his[s][:, :], raw[:, :], ACT.Copy).then_inc(w_hi_ready, 1)

            def copy_am(h, s):
                act.wait_ge(am_made, h + 1)
                need(act, q_made, (h - 1) * STEPS_PER_HEAD)
                act.activation(am_his[s][:, :, :], am_ps.rearrange("p (c n) -> p c n", c=CH), ACT.Copy)\
                    .then_inc(am_hi_ready, 1)

            def copy_vo(h):
                act.wait_ge(vo_made, h + 1)
                need(act, y_done, h * STEPS_PER_HEAD)
                act.activation(vo_hi[:, :], q_ps, ACT.Copy).then_inc(vo_hi_ready, 1)

            def copy_q(s, j):
                act.wait_ge(q_made, j + 1)
                need(act, scores_ready, j - 1)
                act.activation(q_hi[s][:, :], q_ps, ACT.Copy).then_inc(q_hi_ready, 1)

            def squares(s, j):
                act.wait_ge(q_made, j + 1)
                need(act, stats_ready, j)
                act.activation(k_sq[:, :], k_ps, ACT.Square).then_inc(squares_ready, 1)
                act.activation(q_sq[:, :], q_ps, ACT.Square).then_inc(squares_ready, 1)
                need(act, k_normed, j - 1)
                act.activation(k_raw[s][:, :], k_ps, ACT.Copy, scale=gains[:, 0:1]).then_inc(k_copied, 1)

            def exps(s, j):
                act.wait_ge(shift_ready, j + 1)
                need(act, probs_ready, j)
                need(act, turned, j)
                for t in range(2):
                    if normed:
                        act.activation(probs[:, t, :], s_ps[:, t, :], ACT.Exp, bias=shift[:, t:t + 1],
                                       scale=rrms[s][:, t:t + 1], accum_out=total[:, t:t + 1]).then_inc(exp_ready, 1)
                    else:
                        act.activation(probs[:, t, :], s_masked[:, t, :], ACT.Exp, bias=shift[:, t:t + 1],
                                       scale=scale, accum_out=total[:, t:t + 1]).then_inc(exp_ready, 1)

            def copy_turned(j):
                act.wait_ge(turned, j + 1)
                need(act, z_made, j)
                act.activation(pt_hi[:, :, :], t_ps, ACT.Copy).then_inc(pt_hi_ready, 1)

            split(0, 0)
            norm_scalar(act, k)
            if normed:
                act.wait_ge(small_ready, 1)
            else:
                copy_am(0, 0)
            for j in range(2):
                if normed:
                    squares(j, j)
                copy_q(j, j)
            split(1, 1)

            def body(h, slot, first, ending, last):
                for b in range(STEPS_PER_HEAD):
                    j = h * STEPS_PER_HEAD + b
                    more = not (last and b >= 2)
                    if not (first and b == 0):
                        copy_turned(j - 1)
                    exps(b % 2, j)
                    if b == 1 and not last and not normed:
                        copy_am(h + 1, 1 - slot)
                    if more:
                        if normed:
                            squares(b % 2, j + 2)
                        copy_q(b % 2, j + 2)
                    if not (first and b == 0):
                        act.wait_ge(z_made, j)
                        need(act, y_done, j - 1)
                        act.activation(z_hi[:, :], z_ps, ACT.Copy).then_inc(z_hi_ready, 1)
                    if b == 1:
                        copy_vo(h)
                    if b == 2 and not ending:
                        split(h + 2, slot)

            over_heads(act, body)
            copy_turned(steps - 1)
            act.wait_ge(z_made, steps)
            act.wait_ge(y_done, steps - 1)
            act.activation(z_hi[:, :], z_ps, ACT.Copy).then_inc(z_hi_ready, 1)

        @block.vector
        def _(dve):
            def low_q(s, j):
                dve.wait_ge(q_hi_ready, j + 1)
                if normed:
                    dve.wait_ge(squares_ready, 2 * j + 2)
                    dve.wait_ge(k_copied, j + 1)
                need(dve, scores_ready, j - 1)
                dve.tensor_tensor(q_lo[s][:, :], q_ps, f32(q_hi[s][:, :]), ALU.subtract).then_inc(q_lo_ready, 1)

            def key_norm(s, j):
                dve.wait_ge(row_ready, j + 1)
                dve.wait_ge(k_copied, j + 1)
                need(dve, k_lo_ready, j)
                need(dve, k_hi_ready, j)
                dve.tensor_tensor(k32[:, :], k_raw[s][:, :], row_ps, ALU.mult).then_inc(k_normed, 1)

            def copy_stats(j):
                dve.wait_ge(stats_ready, j + 1)
                need(dve, z_made, j - 2)
                need(dve, z_hi_ready, j - 2)
                need(dve, rrms_ready, j)
                dve.tensor_scalar(rms[:, :], stats_ps, 1e-5, None, ALU.add).then_inc(rms_ready, 1)

            def vo_low(h):
                dve.wait_ge(vo_hi_ready, h + 1)
                dve.tensor_tensor(vo_lo[:, :], q_ps, f32(vo_hi[:, :]), ALU.subtract).then_inc(vo_lo_ready, 1)

            def am_low(h, s):
                dve.wait_ge(am_hi_ready, h + 1)
                dve.tensor_tensor(am_los[s][:, :, :], am_ps.rearrange("p (c n) -> p c n", c=CH),
                                  f32(am_his[s][:, :, :]),
                                  ALU.subtract).then_inc(am_lo_ready, 1)

            norm_vector(dve, k)
            if normed:
                dve.wait_ge(small_loaded, 32)
                dve.scalar_tensor_tensor(gains[:, :], gain[:, 0:1], scale, gain[:, 1:2], ALU.mult, ALU.mult)\
                    .then_inc(small_ready, 1)
            else:
                am_low(0, 0)
            for j in range(2):
                low_q(j, j)
                if normed:
                    copy_stats(j)
                if normed and j == 0:
                    key_norm(j, j)

            def low_turned(j):
                dve.wait_ge(pt_hi_ready, j + 1)
                dve.tensor_tensor(pt_lo[:, :, :], t_ps, f32(pt_hi[:, :, :]), ALU.subtract).then_inc(pt_lo_ready, 1)

            def body(h, slot, first, _ending, last):
                for b in range(STEPS_PER_HEAD):
                    j = h * STEPS_PER_HEAD + b
                    s = b % 2
                    more = not (last and b >= 2)
                    next_key = normed and not (last and b == 3)
                    dve.wait_ge(scores_ready, j + 1)
                    if normed:
                        dve.tensor_reduce(top[:, :], s_ps, AX_X, ALU.max).then_inc(top_ready, 2)
                        dve.wait_ge(top_ready, 2 * j + 2)
                        need(dve, exp_ready, 2 * j)
                        dve.scalar_tensor_tensor(shift[:, :], top[:, :], -1.0, rrms[s][:, 0:2], ALU.mult, ALU.mult)\
                            .then_inc(shift_ready, 1)
                    else:
                        need(dve, exp_ready, 2 * j)
                        dve.memset(unread[:, :], 0.0)
                        for t in range(2):
                            dve.tensor_tensor_reduce(s_masked[:, t, :], s_ps[:, t, :],
                                                     k.mask_bias[:, b * S:(b + 1) * S], 1.0, -3.0e38, ALU.add,
                                                     ALU.max, top[:, t:t + 1]).then_inc(top_ready, 1)
                        dve.wait_ge(top_ready, 2 * j + 2)
                        dve.tensor_scalar(shift[:, :], top[:, :], -scale, None, ALU.mult).then_inc(shift_ready, 1)
                    if not (first and b == 0):
                        low_turned(j - 1)
                    if next_key:
                        key_norm(1 - s, j + 1)
                    if b == 1 and not last and not normed:
                        am_low(h + 1, 1 - slot)
                    dve.wait_ge(exp_ready, 2 * j + 2)
                    dve.reciprocal(rtotal[:, :], total[:, :]).then_inc(rtotal_ready, 1)
                    if masked:
                        dve.wait_ge(rtotal_ready, 2 * j + 1)
                        dve.tensor_scalar(rtotal[:, :], rtotal[:, :], k.any_key[:, b:b + 1], None, ALU.mult)\
                            .then_inc(rtotal_ready, 1)
                        dve.wait_ge(rtotal_ready, 2 * j + 2)
                    else:
                        dve.wait_ge(rtotal_ready, j + 1)
                    dve.tensor_tensor(probs[:, :, :], probs[:, :, :],
                                      rtotal[:, :].unsqueeze(2).to_broadcast([P, 2, S]), ALU.mult)\
                        .then_inc(probs_ready, 1)
                    if more:
                        low_q(s, j + 2)
                    if not (first and b == 0):
                        dve.wait_ge(z_hi_ready, j)
                        dve.tensor_tensor(z_lo[:, :], z_ps, f32(z_hi[:, :]), ALU.subtract).then_inc(z_lo_ready, 1)
                    if more and normed:
                        copy_stats(j + 2)
                    if b == 1:
                        vo_low(h)

            over_heads(dve, body)
            low_turned(steps - 1)
            dve.wait_ge(z_hi_ready, steps)
            dve.tensor_tensor(z_lo[:, :], z_ps, f32(z_hi[:, :]), ALU.subtract).then_inc(z_lo_ready, 1)
            for half in range(2):
                cols = slice(half * HALF, (half + 1) * HALF)
                dve.wait_ge(y_done, steps - 2 + 2 * half)
                for c in range(CH):
                    dve.scalar_tensor_tensor(k.x[:, c, cols], y[c][half][:, :], k.gates[:, gate:gate + 1],
                                             k.x[:, c, cols], ALU.mult, ALU.add).then_inc(k.x_ready, 1)

        @block.gpsimd
        def _(pool):
            def split(h, s):
                pool.wait_ge(w_hi_ready, h + 1)
                pool.tensor_tensor(w_los[s][:, :], raw[:, :], f32(w_his[s][:, :]), ALU.subtract)\
                    .then_inc(w_lo_ready, 1)

            def reciprocal_rms(s, j):
                pool.wait_ge(rms_ready, j + 1)
                pool.tensor_tensor(rrms[s][:, :], rms[:, :], k.minus_half[:, :].to_broadcast([P, 4]), ALU.pow)\
                    .then_inc(rrms_ready, 1)

            def key_parts(s, j):
                pool.wait_ge(k_normed, j + 1)
                need(pool, scores_ready, j - 1)
                pool.tensor_tensor(k_hi[s][:, :], k32[:, :], k.one[:, :].to_broadcast([P, S]), ALU.mult)\
                    .then_inc(k_hi_ready, 1)
                pool.wait_ge(k_hi_ready, j + 1)
                pool.tensor_tensor(k_lo[s][:, :], k32[:, :], f32(k_hi[s][:, :]), ALU.subtract).then_inc(k_lo_ready, 1)

            split(0, 0)
            norm_gpsimd(pool, k)
            if normed:
                reciprocal_rms(0, 0)
                key_parts(0, 0)
                reciprocal_rms(1, 1)
            split(1, 1)

            def body(h, slot, _first, ending, last):
                for b in range(STEPS_PER_HEAD):
                    j = h * STEPS_PER_HEAD + b
                    if normed and not (last and b == 3):
                        key_parts((b + 1) % 2, j + 1)
                    if normed and not (last and b >= 2):
                        reciprocal_rms(b % 2, j + 2)
                    if b == 2 and not ending:
                        split(h + 2, slot)

            over_heads(pool, body)

    k.at = base



Q_EPS = 1e-6
Q_MAX = 127.0
ROUND = 1.5 * 2.0 ** 23


class Quant:

    def __init__(self, k, name, n, turned, back):
        self.n, self.chunks = n, n // P
        self.turned, self.back = turned, back
        self.top = k.sb(f"{name}_top", [P, TILES], F32)
        self.step = k.sb(f"{name}_step", [P, TILES], F32)
        self.inverse = k.sb(f"{name}_inverse", [P, TILES], F32)
        self.ratio = k.sb(f"{name}_ratio", [P, TILES, n], F32)
        self.rows = k.sb(f"{name}_rows", [P, TILES, n], BF16)
        self.ints = k.sb(f"{name}_ints", [P, self.chunks, TOK], BF16)
        self.scaled_ready = k.sem(f"{name}_scaled_ready")
        self.turned_ready = k.sem(f"{name}_turned_ready")
        self.rows_ready = k.sem(f"{name}_rows_ready")
        self.back_ready = k.sem(f"{name}_back_ready")
        self.ints_ready = k.sem(f"{name}_ints_ready")

    def turn(self, pe, k, scaled):
        pe.wait_ge(self.scaled_ready, 1)
        for t in range(TILES):
            for c in range(self.chunks):
                last = pe.transpose(self.turned[:, t, c * P:(c + 1) * P], scaled[:, c, t * P:(t + 1) * P],
                                    k.ident[:, :])
        last.then_inc(self.turned_ready, 1)

    def round_rows(self, dve, chain):
        dve.wait_ge(self.turned_ready, 1)
        chain.done(dve.tensor_reduce(self.top[:, :], self.turned, AX_X, ALU.max, apply_absolute_value=True))
        chain.done(dve.tensor_scalar(self.step[:, :], self.top[:, :], Q_EPS, 1.0 / Q_MAX, ALU.max, ALU.mult))
        chain.done(dve.reciprocal(self.inverse[:, :], self.step[:, :]))
        chain.done(dve.tensor_tensor(self.ratio[:, :, :], self.turned,
                                     self.inverse[:, :].unsqueeze(2).to_broadcast([P, TILES, self.n]), ALU.mult))
        chain.done(dve.tensor_scalar(self.ratio[:, :, :], self.ratio[:, :, :], Q_MAX, -Q_MAX, ALU.min, ALU.max))
        dve.tensor_scalar(self.rows[:, :, :], self.ratio[:, :, :], ROUND, ROUND, ALU.add, ALU.subtract)\
            .then_inc(self.rows_ready, 1)

    def turn_back(self, pe, k):
        pe.wait_ge(self.rows_ready, 1)
        for t in range(TILES):
            for c in range(self.chunks):
                last = pe.transpose(self.back[:, c, t * P:(t + 1) * P], self.rows[:, t, c * P:(c + 1) * P],
                                    k.ident_bf[:, :])
        last.then_inc(self.back_ready, 1)

    def copy_back(self, act):
        act.wait_ge(self.back_ready, 1)
        act.activation(self.ints[:, :, :], self.back, ACT.Copy).then_inc(self.ints_ready, 1)

    def step_row(self, pe, k, out, ready):
        for t in range(TILES):
            last = pe.transpose(out[:, t * P:(t + 1) * P], self.step[:, t:t + 1].to_broadcast([P, P]), k.ident[:, :])
        last.then_inc(ready, 1)


def quant_phase(k, a):
    nc = k.nc
    base = k.at
    gate = 0
    w1 = k.sb("q_w1", [P, CH, TOK], F32)
    w2 = k.sb("q_w2", [P, 1, TOK], F32)
    act_t = k.sb("q_act", [P, 1, TOK], F32)
    scaled_act = k.sb("q_scaled_act", [P, 1, TOK], F32)
    row = k.sb("q_row", [P, TOK], F32)
    acc = k.sb("q_acc", [P, CH, TOK], F32)
    silu = k.sb("q_silu", [P, TOK], F32)
    half_col = k.sb("q_half", [P, 1], F32)
    tops = [[k.sb(f"q_top{i}{side}", [P, CH, B], F32) for side in "xw"] for i in (1, 2)]
    ratio = [k.sb(f"q_s_squared{i}", [P, CH, B], F32) for i in (1, 2)]
    s = [k.sb(f"q_s{i}", [P, CH, B], F32) for i in (1, 2)]
    rs = [k.sb(f"q_rs{i}", [P, CH, B], F32) for i in (1, 2)]
    out_gain = k.sb("q_out_gain", [P, TILES], F32)

    def tiles_of(first, n):
        return k.psum[:, first * HALF:first * HALF + TILES * n].rearrange("p (t n) -> p t n", n=n)

    def ints_of(first, chunks):
        return k.psum[:, first * HALF:first * HALF + chunks * TOK // 2].bitcast(BF16)\
            .rearrange("p (c n) -> p c n", c=chunks)

    x1 = Quant(k, "q_x1", D, tiles_of(0, D), ints_of(0, CH))
    v1 = Quant(k, "q_v1", D, tiles_of(4, D), ints_of(4, CH))
    x2 = Quant(k, "q_x2", P, tiles_of(0, P), ints_of(4, 1))
    v2 = Quant(k, "q_v2", P, tiles_of(2, P), ints_of(5, 1))
    row1_ps, row2_ps = k.psum[:, 2 * HALF:4 * HALF], k.psum[:, 6 * HALF:8 * HALF]
    acc1_ps = k.psum[:, 4 * HALF:8 * HALF].rearrange("p (c n) -> p c n", c=CH)
    acc2_ps = k.psum[:, 0:4 * HALF].rearrange("p (c n) -> p c n", c=CH)

    w1_loaded, w2_loaded, chain_sem = k.sem("q_w1_loaded"), k.sem("q_w2_loaded"), k.sem("q_chain")
    half_set, ratio_ready, root_ready = k.sem("q_half_set"), k.sem("q_ratio_ready"), k.sem("q_root_ready")
    row_ready, row_copied, acc_ready = k.sem("q_row_ready"), k.sem("q_row_copied"), k.sem("q_acc_ready")
    scaled1, silu_ready, act_ready = k.sem("q_scaled1"), k.sem("q_silu_ready"), k.sem("q_act_ready")

    def per_batch(t, chunks):
        return t.rearrange("p c (b n) -> p (c b) n", b=B)

    with nc.Block() as block:

        @block.sync
        def _(sp):
            sp.dma_start(w1[:, :, :], a["fside"]).then_inc(w1_loaded, 16)
            sp.dma_start(w2[:, 0, :], a["ctx"]).then_inc(w2_loaded, 16)

        @block.gpsimd
        def _(pool):
            pool.memset(half_col[:, :], 0.5).then_inc(half_set, 1)
            pool.wait_ge(half_set, 1)
            norm_gpsimd(pool, k, False)
            for n in range(2):
                pool.wait_ge(ratio_ready, n + 1)
                pool.tensor_tensor(s[n][:, :, :].rearrange("p c b -> p (c b)"),
                                   ratio[n][:, :, :].rearrange("p c b -> p (c b)"),
                                   half_col[:, :].to_broadcast([P, CH * B]), ALU.pow).then_inc(root_ready, 1)

        @block.tensor
        def _(pe):
            norm_tensor(pe, k)
            x1.turn(pe, k, k.cen)
            v1.turn(pe, k, w1)
            x1.turn_back(pe, k)
            x1.step_row(pe, k, row1_ps, row_ready)
            v1.turn_back(pe, k)
            pe.wait_ge(x1.ints_ready, 1)
            pe.wait_ge(v1.ints_ready, 1)
            for b in range(B):
                toks = slice(b * S, (b + 1) * S)
                for o in range(CH):
                    for c in range(CH):
                        last = pe.matmul(acc1_ps[:, o, toks], v1.ints[:, c, b * S + o * P:b * S + (o + 1) * P],
                                         x1.ints[:, c, toks], start=(c == 0), stop=(c == CH - 1))
            last.then_inc(acc_ready, 1)
            pe.wait_ge(row_copied, 1)
            v2.turn(pe, k, w2)
            x2.turn(pe, k, scaled_act)
            v2.turn_back(pe, k)
            x2.turn_back(pe, k)
            x2.step_row(pe, k, row2_ps, row_ready)
            pe.wait_ge(x2.ints_ready, 1)
            pe.wait_ge(v2.ints_ready, 1)
            for b in range(B):
                toks = slice(b * S, (b + 1) * S)
                for o in range(CH):
                    last = pe.matmul(acc2_ps[:, o, toks], v2.ints[:, 0, b * S + o * P:b * S + (o + 1) * P],
                                     x2.ints[:, 0, toks], start=True, stop=True)
            last.then_inc(acc_ready, 1)

        @block.scalar
        def _(act):
            norm_scalar(act, k, False)
            x1.copy_back(act)
            act.wait_ge(row_ready, 1)
            act.activation(row[:, :], row1_ps, ACT.Copy).then_inc(row_copied, 1)
            v1.copy_back(act)
            act.wait_ge(scaled1, 1)
            for b in range(B):
                last = act.activation(silu[:, b * S:(b + 1) * S], acc[:, 0, b * S:(b + 1) * S], ACT.Silu,
                                      scale=v1.step[:, 2 * b:2 * b + 1])
            last.then_inc(silu_ready, 1)
            v2.copy_back(act)
            x2.copy_back(act)
            act.wait_ge(row_ready, 2)
            act.wait_ge(scaled1, 1)
            act.activation(row[:, :], row2_ps, ACT.Copy).then_inc(row_copied, 1)

        @block.vector
        def _(dve):
            chain = Chain(dve, chain_sem)

            def smooth(n, values, value_tops, chunks):
                x_top, w_top = (t[:, 0:chunks, :] for t in tops[n])
                chain.done(dve.tensor_reduce(x_top, values.rearrange("p c (b n) -> p c b n", b=B), AX_X, ALU.max,
                                             apply_absolute_value=True))
                chain.done(dve.tensor_scalar(w_top, w_top, Q_EPS, None, ALU.max))
                chain.done(dve.reciprocal(w_top, w_top))
                dve.scalar_tensor_tensor(ratio[n][:, 0:chunks, :].rearrange("p c b -> p (c b)"),
                                         x_top.rearrange("p c b -> p (c b)"), Q_EPS,
                                         w_top.rearrange("p c b -> p (c b)"), ALU.max, ALU.mult)\
                    .then_inc(ratio_ready, 1)
                dve.wait_ge(root_ready, n + 1)
                chain.done(dve.tensor_scalar(s[n][:, :, :], s[n][:, :, :], Q_EPS, None, ALU.max))
                chain.done(dve.reciprocal(rs[n][:, 0:chunks, :], s[n][:, 0:chunks, :]))

            def scale_by(out, values, factor, chunks, side):
                dve.tensor_tensor(per_batch(out, chunks), per_batch(values, chunks),
                                  factor[:, 0:chunks, :].rearrange("p c b -> p (c b)").unsqueeze(2)
                                  .to_broadcast([P, chunks * B, S]), ALU.mult).then_inc(side.scaled_ready, 1)

            chain.done(dve.memset(ratio[1][:, 1, :], 1.0))
            dve.wait_ge(w1_loaded, 16)
            chain.done(dve.tensor_reduce(tops[0][1][:, :, :], w1[:, :, :].rearrange("p c (b n) -> p c b n", b=B), AX_X,
                                         ALU.max, apply_absolute_value=True))
            dve.wait_ge(w2_loaded, 16)
            chain.done(dve.tensor_reduce(tops[1][1][:, 0:1, :], w2[:, :, :].rearrange("p c (b n) -> p c b n", b=B),
                                         AX_X, ALU.max, apply_absolute_value=True))
            norm_vector(dve, k, False)
            dve.wait_ge(k.normed, 2)
            smooth(0, k.cen[:, :, :], None, CH)
            scale_by(k.cen[:, :, :], k.cen[:, :, :], rs[0], CH, x1)
            scale_by(w1[:, :, :], w1[:, :, :], s[0], CH, v1)
            x1.round_rows(dve, chain)
            v1.round_rows(dve, chain)
            dve.wait_ge(acc_ready, 1)
            dve.wait_ge(row_copied, 1)
            dve.tensor_tensor(acc[:, :, :], acc1_ps, row[:, :].unsqueeze(1).to_broadcast([P, CH, TOK]), ALU.mult)\
                .then_inc(scaled1, 1)
            dve.wait_ge(scaled1, 1)
            dve.wait_ge(silu_ready, 1)
            for b in range(B):
                toks = slice(b * S, (b + 1) * S)
                last = dve.scalar_tensor_tensor(act_t[:, 0, toks], acc[:, 1, toks], v1.step[:, 2 * b + 1:2 * b + 2],
                                                silu[:, toks], ALU.mult, ALU.mult)
            chain.done(last)
            smooth(1, act_t[:, :, :], None, 1)
            scale_by(w2[:, :, :], w2[:, :, :], s[1], 1, v2)
            scale_by(scaled_act[:, :, :], act_t[:, :, :], rs[1], 1, x2)
            v2.round_rows(dve, chain)
            x2.round_rows(dve, chain)
            chain.done(dve.tensor_scalar(out_gain[:, :], v2.step[:, :], k.gates[:, gate:gate + 1], None, ALU.mult))
            dve.wait_ge(acc_ready, 2)
            dve.wait_ge(row_copied, 2)
            chain.done(dve.tensor_tensor(acc[:, :, :], acc2_ps, row[:, :].unsqueeze(1).to_broadcast([P, CH, TOK]),
                                         ALU.mult))
            for b in range(B):
                toks = slice(b * S, (b + 1) * S)
                for o in range(CH):
                    dve.scalar_tensor_tensor(k.x[:, o, toks], acc[:, o, toks], out_gain[:, 2 * b + o:2 * b + o + 1],
                                             k.x[:, o, toks], ALU.mult, ALU.add).then_inc(k.x_ready, 1)

    k.at = base



SMALL = 8
GROUP = 4
TWO_PI = 6.283185307179586
TWO_PI_HI = 6.28125
PI = 3.1415925
PAD = P - SMALL


def rope_phase(k, a):
    nc = k.nc
    base = k.at
    gate = 2
    scale = float(SMALL) ** -0.5
    WQ, WQS, WK, WKS, WV, WO, WEND = 0, 512, 1024, 1280, 1536, 1792, 2304
    early = k.at
    raw = k.sb("r_raw", [P, WEND], F32)
    spread_raw = k.sb("r_spread_raw", [P, 16 * P], F32)
    w_hi = k.sb("r_w_hi", [P, WEND], F32R)
    w_lo = k.sb("r_w_lo", [P, WEND], F32R)
    spread = k.sb("r_spread", [P, 16 * P], F32R)
    pos = k.sb("r_pos", [P, TILES, 2], F32)
    angle = k.sb("r_angle", [P, TILES, 2, 2], F32)
    turns = k.sb("r_turns", [P, 2, TILES * 4], F32)
    reduced = k.sb("r_reduced", [P, 2, TILES * 4], F32)
    wave = k.sb("r_wave", [P, 2, TILES * 4], F32)
    wide = k.sb("r_wide", [P, 2, TILES, SMALL], F32)
    shared = k.at
    full = k.sb("r_full", [P, 2, TILES, P], F32)
    table = k.sb("r_table", [P, 2, TOK], F32)
    part1 = [k.sb(f"r_part1{s}", [P, HALF], F32) for s in range(2)]
    part2 = [k.sb(f"r_part2{s}", [P, HALF], F32) for s in range(2)]
    rotated = [k.sb(f"r_rotated{s}", [P, HALF], F32) for s in range(2)]
    qk_hi = [k.sb(f"r_{n}_hi", [P, CH * TOK], F32R) for n in "qk"]
    qk_lo = [k.sb(f"r_{n}_lo", [P, CH * TOK], F32R) for n in "qk"]
    v_parts = k.sb("r_v_parts", [P, 2, CH * TOK], F32R)
    head_v = [k.sb(f"r_head_v{s}", [P, 2, 2, PAD + SMALL + PAD], F32R) for s in range(4)]
    rows = [k.sb(f"r_rows{s}", [P, 2 * S], F32R) for s in range(2)]
    top = [k.sb(f"r_top{s}", [P, 2], F32) for s in range(2)]
    shift = [k.sb(f"r_shift{s}", [P, 2], F32) for s in range(2)]
    total = k.sb("r_total", [P, 2, 16], F32)
    rtotal = k.sb("r_rtotal", [P, 2, 16], F32)
    spread_total = k.sb("r_spread_total", [P, 2, 16, SMALL], F32)
    row = k.sb("r_row", [P, S], F32)
    o32 = k.sb("r_o32", [P, S], F32)
    late, k.at = k.at, shared
    probs = [k.sb(f"r_probs{s}", [P, 2, S], F32) for s in range(2)]
    pt_hi = [k.sb(f"r_pt_hi{s}", [P, 2, S], F32R) for s in range(2)]
    pt_lo = [k.sb(f"r_pt_lo{s}", [P, 2, S], F32R) for s in range(2)]
    y_sb = k.sb("r_y", [P, HALF], F32)
    k.at = early
    o_hi = k.sb("r_o_hi", [P, CH * TOK], F32R)
    o_lo = k.sb("r_o_lo", [P, CH * TOK], F32R)
    k.at = late
    bout = k.sb("r_bout", [P, CH], F32)

    def sem(name):
        return k.sem(f"r_{name}")

    loaded, pos_loaded, chain_sem, w_hi_ready, w_lo_ready = (
        sem("loaded"), sem("pos_loaded"), sem("chain"), sem("w_hi_ready"), sem("w_lo_ready"))
    spread_ready, reduced_ready, wave_ready, full_ready = (
        sem("spread_ready"), sem("reduced_ready"), sem("wave_ready"), sem("full_ready"))
    table_turned, table_ready, v_made, v_hi_ready, v_lo_ready = (
        sem("table_turned"), sem("table_ready"), sem("v_made"), sem("v_hi_ready"), sem("v_lo_ready"))
    plain_made, parts_made, rotated_ready, qk_hi_ready, qk_lo_ready = (
        sem("plain_made"), sem("parts_made"), sem("rotated_ready"), sem("qk_hi_ready"), sem("qk_lo_ready"))
    rows_made, rows_ready = sem("rows_made"), sem("rows_ready")
    scores_ready, top_ready, shift_ready, exp_ready = (
        sem("scores_ready"), sem("top_ready"), sem("shift_ready"), sem("exp_ready"))
    turned, pt_hi_ready, pt_lo_ready, mixed = sem("turned"), sem("pt_hi_ready"), sem("pt_lo_ready"), sem("mixed")
    rtotal_ready, spread_done, row_made, row_ready, o_ready, o_hi_ready, o_lo_ready = (
        sem("rtotal_ready"), sem("spread_done"), sem("row_made"), sem("row_ready"), sem("o_ready"),
        sem("o_hi_ready"), sem("o_lo_ready"))
    pads_zero, head_v_ready = sem("pads_zero"), sem("head_v_ready")
    y_made = sem("y_made")

    s_ps = [k.bank[n].rearrange("p (t n) -> p t n", t=2) for n in (0, 1)]
    t_ps = [k.bank[n].rearrange("p (t n) -> p t n", t=2) for n in (2, 3)]
    rows_ps, mix_ps = k.bank[4], k.bank[5][:, 0:S]
    turn_ps = k.bank[6][:, 0:S]
    table_ps = k.psum[:, 0:4 * HALF].rearrange("p (w n) -> p w n", w=2)
    v_ps = k.psum[:, 4 * HALF:8 * HALF]
    iterations = CH * B
    units = iterations * 16
    kinds = [(kind, c, half) for kind in range(2) for c in range(CH) for half in range(2)]

    with nc.Block() as block:

        @block.sync
        def _(sp):
            sp.dma_start(pos[:, :, :], a["r_pos"]).then_inc(pos_loaded, 16)
            sp.dma_start(raw[:, :], a["r_w"]).then_inc(loaded, 16)
            sp.dma_start(spread_raw[:, :], a["r_spread"]).then_inc(loaded, 16)
            sp.dma_start(bout[:, :], a["r_bout"]).then_inc(loaded, 16)

        @block.tensor
        def _(pe):
            norm_tensor(pe, k)
            pe.wait_ge(k.normed, 2)
            pe.wait_ge(full_ready, 2)
            for w in range(2):
                for t in range(TILES):
                    last = pe.transpose(table_ps[:, w, t * P:(t + 1) * P], full[:, w, t, :], k.ident[:, :])
            last.then_inc(table_turned, 1)
            pe.wait_ge(w_hi_ready, 1)
            pe.wait_ge(w_lo_ready, 1)
            for c in range(CH):
                for t in range(TILES):
                    w = slice(WV + c * P, WV + (c + 1) * P)
                    cols = slice(t * P, (t + 1) * P)
                    last = mm3(pe, v_ps[:, c * TOK + t * P:c * TOK + (t + 1) * P], k.ctx_hi[:, cols],
                               k.ctx_lo[:, cols], w_hi[:, w], w_lo[:, w], True, True)
            last.then_inc(v_made, 1)
            pe.wait_ge(table_ready, 1)
            pe.wait_ge(k.h_hi_ready, 2)
            pe.wait_ge(k.h_lo_ready, 2)
            for n, (kind, c, half) in enumerate(kinds):
                if n >= 2:
                    pe.wait_ge(parts_made, 2 * (n - 1))
                cols = slice(half * HALF, (half + 1) * HALF)
                for swapped in range(2):
                    out = k.bank[2 * (n % 2) + swapped]
                    if kind == 0:
                        for f in range(CH):
                            at = (WQ, WQS)[swapped] + f * D + c * P
                            last = mm3(pe, out, w_hi[:, at:at + P], w_lo[:, at:at + P], k.h_hi[:, f, cols],
                                       k.h_lo[:, f, cols], f == 0, f == CH - 1)
                    else:
                        at = (WK, WKS)[swapped] + c * P
                        last = mm3(pe, out, w_hi[:, at:at + P], w_lo[:, at:at + P], k.ctx_hi[:, cols],
                                   k.ctx_lo[:, cols], True, True)
                last.then_inc(plain_made, 1)

            def make_rows(i, g):
                need(pe, rows_ready, i * 4 + g)
                cols = bass.ds(i * S, S)
                for n in range(2):
                    m = slice((g * 4 + 2 * n) * P, (g * 4 + 2 * n + 1) * P)
                    m2 = slice((g * 4 + 2 * n + 1) * P, (g * 4 + 2 * n + 2) * P)
                    pe.matmul(rows_ps[:, n * S:(n + 1) * S], spread[:, m], qk_hi[n][:, cols], start=True, stop=False)
                    last = pe.matmul(rows_ps[:, n * S:(n + 1) * S], spread[:, m2], qk_lo[n][:, cols], start=False,
                                     stop=True)
                last.then_inc(rows_made, 1)

            def scores(i, u):
                g, s = u // GROUP, u % GROUP
                if s == 0:
                    pe.wait_ge(rows_ready, i * 4 + g + 1)
                need(pe, exp_ready, 2 * (i * 16 + u) - 2)
                r = slice(32 * s, 32 * s + 32)
                for t in range(2):
                    last = pe.matmul(s_ps[u % 2][:, t, :], rows[g % 2][r, t * P:(t + 1) * P], rows[g % 2][r, S:2 * S],
                                     start=True, stop=True)
                last.then_inc(scores_ready, 1)

            def turn(i, u):
                j = i * 16 + u
                pe.wait_ge(exp_ready, 2 * j + 2)
                need(pe, pt_hi_ready, j - 1)
                need(pe, pt_lo_ready, j - 1)
                for kt in range(2):
                    for t in range(2):
                        last = pe.transpose(t_ps[u % 2][:, kt, t * P:(t + 1) * P],
                                            probs[u % 2][:, t, kt * P:(kt + 1) * P], k.ident[:, :])
                last.then_inc(turned, 1)

            def mix(i, u):
                j = i * 16 + u
                pe.wait_ge(pt_hi_ready, j + 1)
                pe.wait_ge(pt_lo_ready, j + 1)
                pe.wait_ge(head_v_ready, j + 1)
                if u == 0:
                    need(pe, o_ready, i)
                window = slice(PAD - SMALL * u, PAD - SMALL * u + P)
                for kt in range(2):
                    last = mm3(pe, mix_ps, head_v[u % 4][:, 0, kt, window], head_v[u % 4][:, 1, kt, window],
                               pt_hi[u % 2][:, kt, :], pt_lo[u % 2][:, kt, :], u == 0 and kt == 0,
                               u == 15 and kt == 1)
                last.then_inc(mixed, 1)

            pe.wait_ge(qk_lo_ready, len(kinds))
            pe.wait_ge(qk_hi_ready, len(kinds))
            pe.wait_ge(spread_ready, 1)
            make_rows(0, 0)
            scores(0, 0)
            scores(0, 1)

            def turn_totals(i):
                pe.wait_ge(spread_done, i + 1)
                need(pe, row_ready, i)
                for t in range(2):
                    last_turn = pe.transpose(turn_ps[:, t * P:(t + 1) * P],
                                             spread_total[:, t, :, :].rearrange("p h d -> p (h d)"), k.ident[:, :])
                last_turn.then_inc(row_made, 1)

            def body(i, first, last):
                for u in range(16):
                    if u % 4 == 0 and not (last and u == 12):
                        g = u // 4 + 1
                        make_rows(*((i, g) if g < 4 else (i + 1, 0)))
                    if u < 14:
                        scores(i, u + 2)
                    elif not last:
                        scores(i + 1, u - 14)
                    turn(i, u)
                    if u > 0:
                        mix(i, u - 1)
                    elif not first:
                        mix(i - 1, 15)
                    if u == 0 and not first:
                        turn_totals(i - 1)

            body(0, True, False)
            with pe.Fori(1, iterations - 1) as i:
                body(i, False, False)
            body(iterations - 1, False, True)
            mix(iterations - 1, 15)
            turn_totals(iterations - 1)
            pe.wait_ge(o_hi_ready, iterations)
            pe.wait_ge(o_lo_ready, iterations)
            for o in range(CH):
                for half in range(2):
                    for c in range(CH):
                        at = WO + c * D + o * P
                        cols = slice(c * TOK + half * HALF, c * TOK + (half + 1) * HALF)
                        last = mm3(pe, k.bank[2 * o + half], w_hi[:, at:at + P], w_lo[:, at:at + P], o_hi[:, cols],
                                   o_lo[:, cols], c == 0, c == CH - 1)
                    last.then_inc(y_made, 1)

        @block.scalar
        def _(act):
            act.wait_ge(reduced_ready, 1)
            act.activation(wave[:, :, :], reduced[:, :, :], ACT.Sin).then_inc(wave_ready, 1)
            act.wait_ge(loaded, 48)
            act.activation(w_hi[:, :], raw[:, :], ACT.Copy).then_inc(w_hi_ready, 1)
            act.activation(spread[:, :], spread_raw[:, :], ACT.Copy).then_inc(spread_ready, 1)
            norm_scalar(act, k)
            act.wait_ge(table_turned, 1)
            act.activation(table[:, :, :], table_ps, ACT.Copy).then_inc(table_ready, 1)
            act.wait_ge(v_made, 1)
            act.activation(v_parts[:, 0, :], v_ps, ACT.Copy).then_inc(v_hi_ready, 1)
            for n, (kind, c, half) in enumerate(kinds):
                act.wait_ge(rotated_ready, n + 1)
                at = slice(c * TOK + half * HALF, c * TOK + (half + 1) * HALF)
                act.activation(qk_hi[kind][:, at], rotated[n % 2][:, :], ACT.Copy).then_inc(qk_hi_ready, 1)

            def copy_rows(i, g):
                act.wait_ge(rows_made, i * 4 + g + 1)
                need(act, scores_ready, (i * 4 + g - 1) * GROUP)
                act.activation(rows[g % 2][:, :], rows_ps, ACT.Copy).then_inc(rows_ready, 1)

            def exps(i, u):
                j = i * 16 + u
                act.wait_ge(shift_ready, j + 1)
                need(act, turned, j - 1)
                if u == 0:
                    need(act, rtotal_ready, i)
                for t in range(2):
                    act.activation(probs[u % 2][:, t, :], s_ps[u % 2][:, t, :], ACT.Exp,
                                   bias=shift[u % 2][:, t:t + 1], scale=scale, accum_out=total[:, t, u:u + 1])\
                        .then_inc(exp_ready, 1)

            def copy_turned(i, u):
                j = i * 16 + u
                act.wait_ge(turned, j + 1)
                need(act, mixed, j - 1)
                act.activation(pt_hi[u % 2][:, :, :], t_ps[u % 2], ACT.Copy).then_inc(pt_hi_ready, 1)

            copy_rows(0, 0)
            exps(0, 0)

            def copy_o(i):
                act.wait_ge(o_ready, i + 1)
                act.activation(o_hi[:, bass.ds(i * S, S)], o32[:, :], ACT.Copy).then_inc(o_hi_ready, 1)

            def body(i, first, last):
                for u in range(16):
                    if u % 4 == 0 and not (last and u == 12):
                        g = u // 4 + 1
                        copy_rows(*((i, g) if g < 4 else (i + 1, 0)))
                    if u < 15:
                        exps(i, u + 1)
                    elif not last:
                        exps(i + 1, 0)
                    copy_turned(i, u)
                    if u == 1 and not first:
                        copy_o(i - 1)

            body(0, True, False)
            with act.Fori(1, iterations - 1) as i:
                body(i, False, False)
            body(iterations - 1, False, True)
            copy_o(iterations - 1)

        @block.gpsimd
        def _(pool):
            for slot in head_v:
                for n in range(2):
                    pool.tensor_tensor(slot[:, n, :, :], k.zeros[:, 0:1].unsqueeze(2).to_broadcast(
                        [P, 2, PAD + SMALL + PAD]), k.zeros[:, 0:1].unsqueeze(2).to_broadcast(
                        [P, 2, PAD + SMALL + PAD]), ALU.mult).then_inc(pads_zero, 1)
            pool.wait_ge(w_hi_ready, 1)
            pool.tensor_tensor(w_lo[:, :], raw[:, :], f32(w_hi[:, :]), ALU.subtract).then_inc(w_lo_ready, 1)
            norm_gpsimd(pool, k)
            for n, (kind, c, half) in enumerate(kinds):
                at = slice(c * TOK + half * HALF, c * TOK + (half + 1) * HALF)
                pool.wait_ge(qk_hi_ready, n + 1)
                pool.wait_ge(rotated_ready, n + 1)
                pool.tensor_tensor(qk_lo[kind][:, at], rotated[n % 2][:, :], f32(qk_hi[kind][:, at]), ALU.subtract)\
                    .then_inc(qk_lo_ready, 1)

            def place_values(i, u):
                j = i * 16 + u
                need(pool, mixed, j - 3)
                values = v_parts[:, :, bass.ds(i * S, S)].rearrange("p n (t m) -> p n t m", t=2)
                pool.tensor_tensor(head_v[u % 4][:, :, :, PAD:PAD + SMALL],
                                   f32(values[:, :, :, u * SMALL:(u + 1) * SMALL]),
                                   k.one[:, :].unsqueeze(2).unsqueeze(3).to_broadcast([P, 2, 2, SMALL]), ALU.mult)\
                    .then_inc(head_v_ready, 1)

            pool.wait_ge(v_hi_ready, 1)
            pool.wait_ge(v_lo_ready, 1)
            pool.wait_ge(pads_zero, 2 * len(head_v))

            def body(i):
                for u in range(16):
                    place_values(i, u)

            body(0)
            with pool.Fori(1, iterations) as i:
                body(i)

        @block.vector
        def _(dve):
            chain = Chain(dve, chain_sem)
            dve.wait_ge(pos_loaded, 16)
            dve.tensor_copy(angle[:, :, :, 0], pos[:, :, :])
            chain.done(dve.tensor_scalar(angle[:, :, :, 1], pos[:, :, :], float(k.rope_freq), None, ALU.mult))
            flat = angle[:, :, :, :].rearrange("p t a b -> p (t a b)")
            for w, (quarter, add) in enumerate(((0.25, 0.5 * PI), (0.0, 0.0))):
                chain.done(dve.tensor_scalar(turns[:, w, :], flat, 1.0 / TWO_PI, quarter, ALU.mult, ALU.add))
                chain.done(dve.tensor_scalar(turns[:, w, :], turns[:, w, :], ROUND, ROUND, ALU.add, ALU.subtract))
                chain.done(dve.scalar_tensor_tensor(reduced[:, w, :], turns[:, w, :], -TWO_PI_HI, flat, ALU.mult,
                                                    ALU.add))
                chain.done(dve.scalar_tensor_tensor(reduced[:, w, :], turns[:, w, :], TWO_PI_HI - TWO_PI,
                                                    reduced[:, w, :], ALU.mult, ALU.add))
                chain.done(dve.tensor_scalar(reduced[:, w, :], reduced[:, w, :], (0.5 * 3.141592653589793, 0.0)[w],
                                             None, ALU.add))
            chain.done(dve.tensor_scalar(reduced[:, :, :], reduced[:, :, :], PI, -PI, ALU.min, ALU.max))
            dve.tensor_scalar(reduced[:, :, :], reduced[:, :, :], 1.0, None, ALU.mult).then_inc(reduced_ready, 1)
            dve.wait_ge(wave_ready, 1)
            waves = wave[:, :, :].rearrange("p w (t a) -> p w t a", a=4)
            pairs = wide[:, :, :, :].rearrange("p w t (a i) -> p w t a i", i=2)
            for i in range(2):
                chain.done(dve.tensor_copy(pairs[:, 0, :, :, i], waves[:, 0, :, :]))
            chain.done(dve.tensor_scalar(pairs[:, 1, :, :, 0], waves[:, 1, :, :], -1.0, None, ALU.mult))
            chain.done(dve.tensor_copy(pairs[:, 1, :, :, 1], waves[:, 1, :, :]))
            for w in range(2):
                dve.tensor_copy(full[:, w, :, :].rearrange("p t (h d) -> p t h d", d=SMALL),
                                wide[:, w, :, :].unsqueeze(2).to_broadcast([P, TILES, 16, SMALL]))\
                    .then_inc(full_ready, 1)
            norm_vector(dve, k)
            dve.wait_ge(v_hi_ready, 1)
            dve.tensor_tensor(v_parts[:, 1, :], v_ps, f32(v_parts[:, 0, :]), ALU.subtract).then_inc(v_lo_ready, 1)
            dve.wait_ge(table_ready, 1)
            for n, (kind, c, half) in enumerate(kinds):
                dve.wait_ge(plain_made, n + 1)
                cols = slice(half * HALF, (half + 1) * HALF)
                for swapped, out in ((0, part1), (1, part2)):
                    dve.tensor_tensor(out[n % 2][:, :], k.bank[2 * (n % 2) + swapped], table[:, swapped, cols],
                                      ALU.mult).then_inc(parts_made, 1)
                dve.wait_ge(parts_made, 2 * n + 2)
                if n >= 2:
                    dve.wait_ge(qk_hi_ready, n - 1)
                    dve.wait_ge(qk_lo_ready, n - 1)
                dve.tensor_tensor(rotated[n % 2][:, :], part1[n % 2][:, :], part2[n % 2][:, :], ALU.add)\
                    .then_inc(rotated_ready, 1)

            def maxima(i, u):
                j = i * 16 + u
                dve.wait_ge(scores_ready, j + 1)
                dve.tensor_reduce(top[u % 2][:, :], s_ps[u % 2], AX_X, ALU.max).then_inc(top_ready, 1)
                dve.wait_ge(top_ready, j + 1)
                dve.tensor_scalar(shift[u % 2][:, :], top[u % 2][:, :], -scale, None, ALU.mult)\
                    .then_inc(shift_ready, 1)

            def divide(i):
                dve.wait_ge(row_made, i + 1)
                dve.tensor_copy(row[:, :], turn_ps).then_inc(row_ready, 1)
                dve.wait_ge(row_ready, i + 1)
                dve.wait_ge(mixed, i * 16 + 16)
                need(dve, o_hi_ready, i)
                need(dve, o_lo_ready, i)
                dve.tensor_tensor(o32[:, :], mix_ps, row[:, :], ALU.mult).then_inc(o_ready, 1)

            def low_o(i):
                dve.wait_ge(o_hi_ready, i + 1)
                at = bass.ds(i * S, S)
                dve.tensor_tensor(o_lo[:, at], o32[:, :], f32(o_hi[:, at]), ALU.subtract).then_inc(o_lo_ready, 1)

            maxima(0, 0)
            maxima(0, 1)

            def body(i, first, last):
                for u in range(16):
                    if u < 14:
                        maxima(i, u + 2)
                    elif not last:
                        maxima(i + 1, u - 14)
                    j = i * 16 + u
                    if u == 0 and not first:
                        divide(i - 1)
                    if u == 15:
                        dve.wait_ge(exp_ready, 2 * j + 2)
                        dve.reciprocal(rtotal[:, :, :], total[:, :, :]).then_inc(rtotal_ready, 1)
                        dve.wait_ge(rtotal_ready, i + 1)
                        need(dve, row_made, i)
                        dve.tensor_copy(spread_total[:, :, :, :],
                                        rtotal[:, :, :].unsqueeze(3).to_broadcast([P, 2, 16, SMALL]))\
                            .then_inc(spread_done, 1)
                    dve.wait_ge(pt_hi_ready, j + 1)
                    dve.tensor_tensor(pt_lo[u % 2][:, :, :], t_ps[u % 2], f32(pt_hi[u % 2][:, :, :]), ALU.subtract)\
                        .then_inc(pt_lo_ready, 1)
                    if u == 2 and not first:
                        low_o(i - 1)

            body(0, True, False)
            with dve.Fori(1, iterations - 1) as i:
                body(i, False, False)
            body(iterations - 1, False, True)
            divide(iterations - 1)
            low_o(iterations - 1)
            for n, (o, half) in enumerate((o, half) for o in range(CH) for half in range(2)):
                dve.wait_ge(y_made, n + 1)
                cols = slice(half * HALF, (half + 1) * HALF)
                chain.done(dve.tensor_scalar(y_sb[:, :], k.bank[2 * o + half], bout[:, o:o + 1],
                                             k.gates[:, gate:gate + 1], ALU.add, ALU.mult))
                chain.done(dve.tensor_tensor(k.x[:, o, cols], k.x[:, o, cols], y_sb[:, :], ALU.add))

    k.at = base




def lora_phase(k, a):
    nc = k.nc
    base = k.at
    gate = 6
    experts, blocks = 8, 7
    W1, W3, B1, B3, W2, A2, WEND = (D * n for n in range(7))
    A1, A3, B2, SMALL_END = 0, 2 * D, 4 * D, 6 * D
    small_hi = k.sb("l_small_hi", [P, SMALL_END], F32R)
    small_lo = k.sb("l_small_lo", [P, SMALL_END], F32R)
    raw = k.sb("l_raw", [P, WEND], F32)
    w_hi = [k.sb(f"l_w_hi{s}", [P, WEND], F32R) for s in range(2)]
    w_lo = [k.sb(f"l_w_lo{s}", [P, WEND], F32R) for s in range(2)]
    early = k.at
    am_hi = [[k.sb(f"l_am_hi{w}{n}", [P, CH, TOK], F32R) for n in range(2)] for w in range(2)]
    am_lo = [[k.sb(f"l_am_lo{w}{n}", [P, CH, TOK], F32R) for n in range(2)] for w in range(2)]
    late = k.at
    k.at = early
    rw = k.sb("l_rw", [P, CH, experts], F32)
    rw_hi = k.sb("l_rw_hi", [P, CH, experts], F32R)
    rw_lo = k.sb("l_rw_lo", [P, CH, experts], F32R)
    logits, shifted, expd, rank_of = (k.sb(f"l_{n}", [P, TILES, experts], F32)
                                      for n in ("logits", "shifted", "expd", "rank"))
    slot = [k.sb(f"l_slot{n}", [P, TILES, experts], F32) for n in range(2)]
    top, total = k.sb("l_top", [P, TILES], F32), k.sb("l_total", [P, TILES], F32)
    kept = k.sb("l_kept", [P, TILES, experts], F32)
    weight = [k.sb(f"l_weight{n}", [P, TILES, 1], F32) for n in range(2)]
    rest = k.sb("l_rest", [P, TILES, 1], F32)
    parts = k.sb("l_parts", [P, TILES, P], BF16)
    parts_t = k.sb("l_parts_t", [P, TOK], BF16)
    select = k.sb("l_select", [P, 8 * P], BF16)
    k.cmp_gt = k.sb("l_cmp_gt", [P, TILES * 64], BF16)
    k.cmp_eq = k.sb("l_cmp_eq", [P, TILES * 64], BF16)
    k.at = early
    u_hi = k.sb("l_u_hi", [P, CH, TOK], F32R)
    u_lo = k.sb("l_u_lo", [P, CH, TOK], F32R)
    k.at = late
    weight_row = k.sb("l_weight_row", [P, 2, TOK], F32)
    u = k.sb("l_u", [P, CH, TOK], F32)
    loop = k.at
    act32 = [k.sb(f"l_act32{n}", [P, HALF], F32) for n in range(2)]
    masked = k.sb("l_masked", [P, CH, HALF], F32)
    products = k.at
    x2_hi = [k.sb(f"l_x2_hi{n}", [P, HALF], F32R) for n in range(2)]
    x2_lo = [k.sb(f"l_x2_lo{n}", [P, HALF], F32R) for n in range(2)]
    k.at = loop
    small_raw = k.sb("l_small_raw", [P, SMALL_END], F32)
    k.at = loop
    row_hi = k.sb("l_row_hi", [P, HALF], F32R)
    row_lo = k.sb("l_row_lo", [P, HALF], F32R)
    k.at = products
    diff = k.sb("l_diff", [P, CH, TOK], F32)
    mask = [k.cen, k.sq]

    def sem(name):
        return k.sem(f"l_{name}")

    small_loaded, raw_loaded, chain_sem, zeroed = sem("small_loaded"), sem("raw_loaded"), sem("chain"), sem("zeroed")
    small_hi_ready, small_lo_ready, router_hi, router_lo = (
        sem("small_hi_ready"), sem("small_lo_ready"), sem("router_hi"), sem("router_lo"))
    logits_ready, shifted_ready, expd_ready, parts_ready = (
        sem("logits_ready"), sem("shifted_ready"), sem("expd_ready"), sem("parts_ready"))
    turned, parts_t_ready, table_made, table_copied = (
        sem("turned"), sem("parts_t_ready"), sem("table_made"), sem("table_copied"))
    row_made, row_hi_ready, row_lo_ready, am_ready = (
        sem("row_made"), sem("row_hi_ready"), sem("row_lo_ready"), sem("am_ready"))
    w_hi_ready, w_lo_ready = sem("w_hi_ready"), sem("w_lo_ready")
    x1_made, x3_made, silu_ready, gated_ready = sem("x1_made"), sem("x3_made"), sem("silu_ready"), sem("gated_ready")
    weighted_ready, x2_hi_ready, x2_lo_ready = sem("weighted_ready"), sem("x2_hi_ready"), sem("x2_lo_ready")
    y_done, a2_masked, a2_added = sem("y_done"), sem("a2_masked"), sem("a2_added")
    u_hi_ready, u_lo_ready, y_whole = sem("u_hi_ready"), sem("u_lo_ready"), sem("y_whole")

    y = [[k.bank[2 * c + half] for half in range(2)] for c in range(CH)]
    x1_ps, x3_ps = k.bank[4], k.bank[5]
    a2_ps = k.psum[:, 6 * HALF:8 * HALF].rearrange("p (c n) -> p c n", c=CH)
    logits_ps = k.bank[7][:, 0:TILES * experts].rearrange("p (t e) -> p t e", e=experts)
    tables = [mask[0][:, 0, :], mask[0][:, 1, :], mask[1][:, 0, :], mask[1][:, 1, :], diff[:, 0, :], diff[:, 1, :],
              weight_row[:, 0, :], weight_row[:, 1, :]]
    rows = [(w, c, half) for w in range(2) for c in range(CH) for half in range(2)]
    units = blocks * 4
    loop_to = (blocks - 1) // 2

    def static(b):
        return isinstance(b, int)

    def over_blocks(eng, body):
        body(0, 0, True)
        body(1, 1, True)
        with eng.Fori(1, loop_to) as pair:
            body(pair * 2, 0, True)
            body(pair * 2 + 1, 1, True)
        for b in range(2 * loop_to, blocks):
            body(b, b % 2, b + 1 < blocks)

    with nc.Block() as block:

        @block.sync
        def _(sp):
            sp.dma_start(rw[:, :, :], a["l_router"]).then_inc(small_loaded, 16)
            sp.dma_start(small_raw[:, :], a["l_small"]).then_inc(small_loaded, 16)
            sp.dma_start(select[:, :], a["l_select"]).then_inc(small_loaded, 16)
            sp.dma_start(raw[:, :], a["l_w"][0, :, :]).then_inc(raw_loaded, 16)
            with sp.Fori(1, blocks) as b:
                sp.wait_ge(w_hi_ready, b)
                sp.wait_ge(w_lo_ready, b)
                sp.dma_start(raw[:, :], a["l_w"][bass.ds(b, 1), :, :].rearrange("b p n -> p (b n)"))\
                    .then_inc(raw_loaded, 16)

        @block.tensor
        def _(pe):
            norm_tensor(pe, k)
            pe.wait_ge(k.h_hi_ready, 2)
            pe.wait_ge(k.h_lo_ready, 2)
            pe.wait_ge(router_hi, 1)
            pe.wait_ge(router_lo, 1)
            for t in range(TILES):
                cols = slice(t * P, (t + 1) * P)
                for c in range(CH):
                    last = mm3(pe, logits_ps[:, t, :], k.h_hi[:, c, cols], k.h_lo[:, c, cols], rw_hi[:, c, :],
                               rw_lo[:, c, :], c == 0, c == CH - 1)
            last.then_inc(logits_ready, 1)
            pe.wait_ge(parts_ready, 1)
            turned_ps = k.bank[6].bitcast(BF16)
            for t in range(TILES):
                last = pe.transpose(turned_ps[:, t * P:(t + 1) * P], parts[:, t, :], k.ident_bf[:, :])
            last.then_inc(turned, 1)
            pe.wait_ge(parts_t_ready, 1)
            for n in range(len(tables)):
                if n >= 2:
                    pe.wait_ge(table_copied, n - 1)
                for half in range(2):
                    last = pe.matmul(k.bank[2 * (n % 2) + half], select[:, n * P:(n + 1) * P],
                                     parts_t[:, half * HALF:(half + 1) * HALF], start=True, stop=True)
                last.then_inc(table_made, 1)
            pe.wait_ge(small_hi_ready, 1)
            pe.wait_ge(small_lo_ready, 1)
            for n, (w, c, half) in enumerate(rows):
                if n >= 2:
                    pe.wait_ge(row_lo_ready, n - 1)
                cols = slice(half * HALF, (half + 1) * HALF)
                for f in range(CH):
                    at = (A1, A3)[w] + f * D + c * P
                    last = mm3(pe, k.bank[4 + n % 2], small_hi[:, at:at + P], small_lo[:, at:at + P],
                               k.h_hi[:, f, cols], k.h_lo[:, f, cols], f == 0, f == CH - 1)
                last.then_inc(row_made, 1)
            pe.wait_ge(table_copied, len(tables))
            for c in range(CH):
                for half in range(2):
                    pe.matmul(y[c][half], k.zeros[:, 0:P], k.zeros[:, :], start=True, stop=False)
            pe.wait_ge(row_lo_ready, len(rows))
            pe.wait_ge(am_ready, 4 * len(rows))

            def add_y(j, half, n, s):
                pe.wait_ge(x2_hi_ready, j + 1)
                pe.wait_ge(x2_lo_ready, j + 1)
                for c in range(CH):
                    at = W2 + c * P
                    mm3(pe, y[c][half], w_hi[s][:, at:at + P], w_lo[s][:, at:at + P], x2_hi[n][:, :], x2_lo[n][:, :],
                        False, False)
                need(pe, a2_masked, j)
                for c in range(CH):
                    at = A2 + c * P
                    last = mm3(pe, a2_ps[:, c, :], w_hi[s][:, at:at + P], w_lo[s][:, at:at + P], x2_hi[n][:, :],
                               x2_lo[n][:, :], True, True)
                last.then_inc(y_done, 1)

            def body(b, s, _more):
                pe.wait_ge(w_hi_ready, b + 1)
                pe.wait_ge(w_lo_ready, b + 1)
                for half in range(2):
                    cols = slice(half * HALF, (half + 1) * HALF)
                    for n in range(2):
                        j = b * 4 + half * 2 + n
                        for w, (out, big, low, made, free) in enumerate(((x1_ps, W1, B1, x1_made, silu_ready),
                                                                         (x3_ps, W3, B3, x3_made, gated_ready))):
                            need(pe, free, j)
                            if n == 0:
                                for c in range(CH):
                                    at = big + c * P
                                    mm3(pe, out, w_hi[s][:, at:at + P], w_lo[s][:, at:at + P], k.h_hi[:, c, cols],
                                        k.h_lo[:, c, cols], c == 0, False)
                            for c in range(CH):
                                at = low + c * P
                                stop = c == CH - 1
                                lhs_hi, lhs_lo = w_hi[s][:, at:at + P], w_lo[s][:, at:at + P]
                                rhs_hi, rhs_lo = am_hi[w][n][:, c, cols], am_lo[w][n][:, c, cols]
                                again = n == 1
                                pe.matmul(out, lhs_hi, rhs_hi, start=False, stop=False, skip_group_check=again)
                                pe.matmul(out, lhs_lo, rhs_hi, start=False, stop=False, skip_group_check=again)
                                last = pe.matmul(out, lhs_hi, rhs_lo, start=False, stop=stop, skip_group_check=again)
                            last.then_inc(made, 1)
                        if not (static(b) and j == 0):
                            if n == 1:
                                add_y(j - 1, half, 0, s)
                            elif half == 1:
                                add_y(j - 1, 0, 1, s)
                            else:
                                add_y(j - 1, 1, 1, 1 - s)

            over_blocks(pe, body)
            add_y(units - 1, 1, 1, (blocks - 1) % 2)
            for half in range(2):
                cols = slice(half * HALF, (half + 1) * HALF)
                pe.wait_ge(u_hi_ready, half + 1)
                pe.wait_ge(u_lo_ready, half + 1)
                for o in range(CH):
                    for c in range(CH):
                        at = B2 + c * D + o * P
                        last = mm3(pe, y[o][half], small_hi[:, at:at + P], small_lo[:, at:at + P], u_hi[:, c, cols],
                                   u_lo[:, c, cols], False, c == CH - 1)
                last.then_inc(y_whole, 1)

        @block.scalar
        def _(act):
            def split(b, s):
                act.wait_ge(raw_loaded, b * 16 + 16)
                if not static(b) or b >= 2:
                    act.wait_ge(y_done, b * 4 - 4)
                act.activation(w_hi[s][:, :], raw[:, :], ACT.Copy).then_inc(w_hi_ready, 1)

            act.wait_ge(small_loaded, 48)
            act.activation(rw_hi[:, :, :], rw[:, :, :], ACT.Copy).then_inc(router_hi, 1)
            act.activation(small_hi[:, :], small_raw[:, :], ACT.Copy).then_inc(small_hi_ready, 1)
            norm_scalar(act, k)
            split(0, 0)
            act.wait_ge(shifted_ready, 1)
            act.activation(expd[:, :, :], shifted[:, :, :], ACT.Exp).then_inc(expd_ready, 1)
            act.wait_ge(k.normed, 2)
            act.wait_ge(k.h_lo_ready, 2)
            for n, table in enumerate(tables):
                act.wait_ge(table_made, n + 1)
                act.activation(table, k.psum[:, 2 * (n % 2) * HALF:(2 * (n % 2) + 2) * HALF], ACT.Copy)\
                    .then_inc(table_copied, 1)
            for n in range(len(rows)):
                act.wait_ge(row_made, n + 1)
                need(act, am_ready, 4 * n)
                act.activation(row_hi[:, :], k.bank[4 + n % 2], ACT.Copy).then_inc(row_hi_ready, 1)

            def body(b, s, more):
                for half in range(2):
                    for n in range(2):
                        j = b * 4 + half * 2 + n
                        act.wait_ge(x1_made, j + 1)
                        need(act, x2_lo_ready, j - 1)
                        act.activation(act32[n][:, :], x1_ps, ACT.Silu).then_inc(silu_ready, 1)
                        act.wait_ge(weighted_ready, j + 1)
                        need(act, y_done, j - 1)
                        act.activation(x2_hi[n][:, :], act32[n][:, :], ACT.Copy).then_inc(x2_hi_ready, 1)
                        if half == 0 and n == 0 and more:
                            split(b + 1, 1 - s)

            over_blocks(act, body)
            for half in range(2):
                cols = slice(half * HALF, (half + 1) * HALF)
                act.wait_ge(a2_added, units - 1 + half)
                act.wait_ge(y_done, units)
                act.activation(u_hi[:, :, cols], u[:, :, cols], ACT.Copy).then_inc(u_hi_ready, 1)

        @block.gpsimd
        def _(pool):
            def split(b, s):
                pool.wait_ge(w_hi_ready, b + 1)
                pool.tensor_tensor(w_lo[s][:, :], raw[:, :], f32(w_hi[s][:, :]), ALU.subtract).then_inc(w_lo_ready, 1)

            pool.memset(parts[:, :, :], 0.0).then_inc(zeroed, 1)
            pool.memset(u[:, :, :], 0.0).then_inc(zeroed, 1)
            pool.wait_ge(router_hi, 1)
            pool.tensor_tensor(rw_lo[:, :, :], rw[:, :, :], f32(rw_hi[:, :, :]), ALU.subtract).then_inc(router_lo, 1)
            norm_gpsimd(pool, k)
            pool.wait_ge(small_hi_ready, 1)
            pool.tensor_tensor(small_lo[:, :], small_raw[:, :], f32(small_hi[:, :]), ALU.subtract)\
                .then_inc(small_lo_ready, 1)
            split(0, 0)
            pool.wait_ge(table_copied, len(tables))
            for n, (w, c, half) in enumerate(rows):
                cols = slice(half * HALF, (half + 1) * HALF)
                pool.wait_ge(row_hi_ready, n + 1)
                pool.tensor_tensor(am_hi[w][1][:, c, cols], f32(row_hi[:, :]), diff[:, c, cols], ALU.mult)\
                    .then_inc(am_ready, 1)
                pool.wait_ge(row_lo_ready, n + 1)
                pool.tensor_tensor(am_lo[w][1][:, c, cols], f32(row_lo[:, :]), diff[:, c, cols], ALU.mult)\
                    .then_inc(am_ready, 1)

            def add_masked(j, half):
                pool.wait_ge(a2_masked, j + 1)
                need(pool, a2_added, j)
                cols = slice(half * HALF, (half + 1) * HALF)
                pool.tensor_tensor(u[:, :, cols], u[:, :, cols], masked[:, :, :], ALU.add).then_inc(a2_added, 1)

            def body(b, s, more):
                for half in range(2):
                    for n in range(2):
                        j = b * 4 + half * 2 + n
                        if not (static(b) and j == 0):
                            add_masked(j - 1, half if n == 1 else 1 - half)
                        if half == 0 and n == 0 and more:
                            split(b + 1, 1 - s)

            over_blocks(pool, body)
            add_masked(units - 1, 1)

        @block.vector
        def _(dve):
            chain = Chain(dve, chain_sem)
            norm_vector(dve, k)
            dve.wait_ge(logits_ready, 1)
            chain.done(dve.tensor_copy(logits[:, :, :], logits_ps))
            chain.done(dve.tensor_reduce(top[:, :], logits[:, :, :], AX_X, ALU.max))
            dve.tensor_tensor(shifted[:, :, :], logits[:, :, :], top[:, :].unsqueeze(2)
                              .to_broadcast([P, TILES, experts]), ALU.subtract).then_inc(shifted_ready, 1)
            rank(dve, chain, k, rank_of[:, :, :], logits[:, :, :], experts)
            dve.wait_ge(expd_ready, 1)
            for n in range(2):
                chain.done(dve.tensor_scalar(slot[n][:, :, :], rank_of[:, :, :], float(n), None, ALU.is_equal))
                chain.done(dve.tensor_tensor(kept[:, :, :], slot[n][:, :, :], expd[:, :, :], ALU.mult))
                chain.done(dve.tensor_reduce(weight[n][:, :, 0], kept[:, :, :], AX_X, ALU.add))
            chain.done(dve.tensor_tensor(total[:, :], weight[0][:, :, 0], weight[1][:, :, 0], ALU.add))
            chain.done(dve.reciprocal(total[:, :], total[:, :]))
            dve.wait_ge(zeroed, 2)
            for n in range(2):
                chain.done(dve.tensor_tensor(weight[n][:, :, 0], weight[n][:, :, 0], total[:, :], ALU.mult))
                chain.done(dve.tensor_copy(parts[:, :, 8 * n:8 * n + 8], slot[n][:, :, :]))
                at = 16 + 3 * n
                chain.done(dve.tensor_copy(parts[:, :, at:at + 1], weight[n][:, :, :]))
                chain.done(dve.tensor_tensor(rest[:, :, :], weight[n][:, :, :], parts[:, :, at:at + 1], ALU.subtract))
                chain.done(dve.tensor_copy(parts[:, :, at + 1:at + 2], rest[:, :, :]))
                chain.done(dve.tensor_tensor(rest[:, :, :], rest[:, :, :], parts[:, :, at + 1:at + 2], ALU.subtract))
                last = dve.tensor_copy(parts[:, :, at + 2:at + 3], rest[:, :, :])
                if n == 0:
                    chain.done(last)
            last.then_inc(parts_ready, 1)
            dve.wait_ge(turned, 1)
            dve.tensor_copy(parts_t[:, :], k.bank[6].bitcast(BF16)).then_inc(parts_t_ready, 1)
            dve.wait_ge(table_copied, len(tables))
            for n, (w, c, half) in enumerate(rows):
                cols = slice(half * HALF, (half + 1) * HALF)
                dve.wait_ge(row_hi_ready, n + 1)
                need(dve, am_ready, 4 * n)
                dve.tensor_tensor(row_lo[:, :], k.bank[4 + n % 2], f32(row_hi[:, :]), ALU.subtract)\
                    .then_inc(row_lo_ready, 1)
                dve.tensor_tensor(am_hi[w][0][:, c, cols], f32(row_hi[:, :]), mask[0][:, c, cols], ALU.mult)\
                    .then_inc(am_ready, 1)
                dve.wait_ge(row_lo_ready, n + 1)
                dve.tensor_tensor(am_lo[w][0][:, c, cols], f32(row_lo[:, :]), mask[0][:, c, cols], ALU.mult)\
                    .then_inc(am_ready, 1)

            def mask_rows(j, half, n):
                dve.wait_ge(y_done, j + 1)
                need(dve, a2_added, j)
                cols = slice(half * HALF, (half + 1) * HALF)
                dve.tensor_tensor(masked[:, :, :], a2_ps, mask[n][:, :, cols], ALU.mult).then_inc(a2_masked, 1)

            def body(b, s, _more):
                for half in range(2):
                    cols = slice(half * HALF, (half + 1) * HALF)
                    for n in range(2):
                        j = b * 4 + half * 2 + n
                        dve.wait_ge(silu_ready, j + 1)
                        dve.wait_ge(x3_made, j + 1)
                        dve.tensor_tensor(act32[n][:, :], act32[n][:, :], x3_ps, ALU.mult).then_inc(gated_ready, 1)
                        dve.wait_ge(gated_ready, j + 1)
                        dve.tensor_tensor(act32[n][:, :], act32[n][:, :], weight_row[:, n, cols], ALU.mult)\
                            .then_inc(weighted_ready, 1)
                        dve.wait_ge(x2_hi_ready, j + 1)
                        dve.tensor_tensor(x2_lo[n][:, :], act32[n][:, :], f32(x2_hi[n][:, :]), ALU.subtract)\
                            .then_inc(x2_lo_ready, 1)
                        if not (static(b) and j == 0):
                            mask_rows(j - 1, half if n == 1 else 1 - half, 1 - n)

            over_blocks(dve, body)
            mask_rows(units - 1, 1, 1)
            for half in range(2):
                cols = slice(half * HALF, (half + 1) * HALF)
                dve.wait_ge(u_hi_ready, half + 1)
                dve.tensor_tensor(u_lo[:, :, cols], u[:, :, cols], f32(u_hi[:, :, cols]), ALU.subtract)\
                    .then_inc(u_lo_ready, 1)
            for half in range(2):
                cols = slice(half * HALF, (half + 1) * HALF)
                dve.wait_ge(y_whole, half + 1)
                for c in range(CH):
                    dve.scalar_tensor_tensor(k.x[:, c, cols], y[c][half], k.gates[:, gate:gate + 1], k.x[:, c, cols],
                                             ALU.mult, ALU.add).then_inc(k.x_ready, 1)

    k.at = base




def flamingo(nc, a, out):
    with ExitStack() as ctx:
        k = Core(nc, ctx)
        k.x = k.sb("x", [P, CH, TOK], F32)
        k.cen = k.sb("cen", [P, CH, TOK], F32)
        k.sq = k.sb("sq", [P, CH, TOK], F32)
        k.h_hi = k.sb("h_hi", [P, CH, TOK], F32R)
        k.h_lo = k.sb("h_lo", [P, CH, TOK], F32R)
        k.mean_w = k.sb("mean_w", [P, P], F32)
        k.ident = k.sb("ident", [P, P], F32)
        k.ident_bf = k.sb("ident_bf", [P, P], BF16)
        k.zeros = k.sb("zeros", [P, HALF], BF16)
        k.ctx_hi = k.sb("ctx_hi", [P, TOK], F32R)
        k.ctx_lo = k.sb("ctx_lo", [P, TOK], F32R)
        k.keys_hi = k.sb("keys_hi", [P, TILES, CD], F32R)
        k.keys_lo = k.sb("keys_lo", [P, TILES, CD], F32R)
        k.mask_bias = k.sb("mask_bias", [P, TOK], F32)
        k.any_key = k.sb("any_key", [P, B], F32)
        k.head_w = k.sb("head_w", [P, 1], F32)
        k.minus_half = k.sb("minus_half", [P, 1], F32)
        k.one = k.sb("one", [P, 1], F32)
        k.var = k.sb("var", [P, TILES], F32)
        k.rstd = k.sb("rstd", [P, TILES], F32)
        k.gates = k.sb("gates", [P, 8], F32)
        k.before = k.sb("before", [P, 256], BF16)
        k.psum = ctx.enter_context(nc.psum_tensor("psum", [P, 8 * HALF], F32))
        k.bank = [k.psum[:, i * HALF:(i + 1) * HALF] for i in range(8)]

        base = k.at
        mask = k.sb("mask", [P, TOK], U8)
        ctx_raw = k.sb("ctx_raw", [P, TOK], F32)
        keys_raw = k.sb("keys_raw", [P, TILES, CD], F32)
        k.at = base
        ctx_loaded, parts_ready, mask_ready = k.sem("ctx_loaded"), k.sem("parts_ready"), k.sem("mask_ready")
        k.rope_freq = 0.01
        x_loaded, consts_loaded, const_set, stored = (k.sem(n) for n in (
            "x_loaded", "consts_loaded", "const_set", "stored"))
        with nc.Block() as block:

            @block.sync
            def _(sp):
                sp.dma_start(k.x[:, :, :], a["x"]).then_inc(x_loaded, 16)
                sp.dma_start(k.ident[:, :], a["ident"]).then_inc(consts_loaded, 16)
                sp.dma_start(k.before[:, :], a["before"].partition_broadcast(P)).then_inc(consts_loaded, 16)

            @block.gpsimd
            def _(pool):
                pool.memset(k.mean_w[:, :], 1.0 / D).then_inc(const_set, 1)
                pool.memset(k.zeros[:, :], 0.0).then_inc(const_set, 1)
                pool.memset(k.one[:, :], 1.0).then_inc(const_set, 1)
                pool.memset(k.minus_half[:, :], -0.5).then_inc(const_set, 1)
                pool.memset(k.head_w[:, :], 1.0 / HD).then_inc(const_set, 1)

            @block.scalar
            def _(act):
                act.dma_start(ctx_raw[:, :], a["ctx"]).then_inc(ctx_loaded, 16)
                act.dma_start(keys_raw[:, :, :], a["keys"]).then_inc(ctx_loaded, 16)
                act.dma_start(mask[:, :], a["mask"].partition_broadcast(P)).then_inc(ctx_loaded, 16)
                act.dma_start(k.gates[:, 0:4], a["g_xattn"].partition_broadcast(P)).then_inc(consts_loaded, 16)
                act.dma_start(k.gates[:, 4:8], a["g_ffn"].partition_broadcast(P)).then_inc(consts_loaded, 16)
                act.wait_ge(consts_loaded, 64)
                act.activation(k.gates[:, :], k.gates[:, :], ACT.Tanh).then_inc(const_set, 1)
                act.activation(k.ident_bf[:, :], k.ident[:, :], ACT.Copy).then_inc(const_set, 1)
                act.wait_ge(ctx_loaded, 48)
                act.activation(k.ctx_hi[:, :], ctx_raw[:, :], ACT.Copy).then_inc(parts_ready, 1)
                act.activation(k.keys_hi[:, :, :], keys_raw[:, :, :], ACT.Copy).then_inc(parts_ready, 1)

            @block.vector
            def _(dve):
                dve.wait_ge(ctx_loaded, 48)
                dve.tensor_scalar(k.mask_bias[:, :], mask[:, :], 1.0e30, -1.0e30, ALU.mult, ALU.add)\
                    .then_inc(mask_ready, 1)
                dve.tensor_reduce(k.any_key[:, :], mask[:, :].rearrange("p (b n) -> p b n", b=B), AX_X, ALU.max)\
                    .then_inc(mask_ready, 1)
                dve.wait_ge(parts_ready, 2)
                dve.tensor_tensor(k.ctx_lo[:, :], ctx_raw[:, :], f32(k.ctx_hi[:, :]), ALU.subtract)\
                    .then_inc(parts_ready, 1)
                dve.tensor_tensor(k.keys_lo[:, :, :], keys_raw[:, :, :], f32(k.keys_hi[:, :, :]), ALU.subtract)\
                    .then_inc(parts_ready, 1)
                dve.wait_ge(const_set, 7)
                dve.wait_ge(x_loaded, 16)

        for step in STEPS:
            with nc.cleanup_on_exit():
                k.phase_sems()
                step(k, a)

        with nc.Block() as block:

            @block.sync
            def _(sp):
                sp.dma_start(out, k.x[:, :, :]).then_inc(stored, 16)
                sp.wait_ge(stored, 16)


def l0_ffn(k, a):
    ffn_phase(k, "f0", "sigmoid_top4", 16, True, 17, 4, a["f0_w"], a["f0_router"], a["f0_sel"], a["f0_bias"])


def l1_ffn(k, a):
    ffn_phase(k, "f1", "softmax_top2", 8, False, 32, 5, a["f1_w"], a["f1_router"], a["f1_sel"], None)


def l3_ffn(k, a):
    ffn_phase(k, "f3", "group_top4", 16, True, 25, 7, a["f3_w"], a["f3_router"], a["f3_sel"], None)


def l1_xattn(k, a):
    xattn_phase(k, "x1", True, 1, a["x1_w"], a["x1_gq"], a["x1_gk"], False)


def l3_xattn(k, a):
    xattn_phase(k, "x3", False, 3, a["x3_w"], None, None, True)


STEPS = (quant_phase, l0_ffn, l1_xattn, l1_ffn, rope_phase, lora_phase, l3_xattn, l3_ffn)




def _feature_major(w):
    return w.reshape(-1, P, w.shape[-1]).transpose(1, 0, 2)


def _ffn_blocks(np, gates, ups, downs):
    blocks = -(-gates.shape[0] // P)
    out = np.zeros((blocks, P, BLOCK), np.float32)
    for at, w in ((0, gates), (D, ups)):
        full = np.zeros((blocks * P, D), np.float32)
        full[:w.shape[0]] = w
        out[:, :, at:at + D] = full.reshape(blocks, P, CH, P).transpose(0, 3, 2, 1).reshape(blocks, P, D)
    full = np.zeros((blocks * P, D), np.float32)
    full[:downs.shape[1]] = downs.T
    out[:, :, 2 * D:] = full.reshape(blocks, P, D)
    return out


def _bf16(np, table):
    return (table.view(np.uint32) >> 16).astype(np.uint16)


def _select(np, widths, blocks):
    expert = np.repeat(np.arange(len(widths)), widths)
    sel = np.zeros((P, blocks * P), np.float32)
    for part in range(3):
        sel[32 * part + expert, np.arange(len(expert))] = 1.0
    return _bf16(np, sel)


def _heads(np, parts):
    return np.concatenate(parts, 2)


def _by_head(w):
    return w.reshape(w.shape[0], -1, HD).transpose(1, 0, 2)


def _columns(w):
    return w.reshape(CH, P, -1, P).transpose(2, 1, 0, 3).reshape(-1, P, CH * P)


def _slots(np):
    out = np.zeros((P, 8, P), np.float32)
    for c in range(CH):
        for row in range(P):
            expert = 4 * c + row // 32
            out[expert, c, row] = 1.0
            out[8 + expert, 2 + c, row] = 1.0
            out[8 + expert, 4 + c, row] = 1.0
            out[expert, 4 + c, row] = -1.0
    out[16:19, 6, :] = 1.0
    out[19:22, 7, :] = 1.0
    return out.reshape(P, 8 * P)


def _spread(np):
    out = np.zeros((P, 16, P), np.float32)
    for g in range(4):
        for s in range(GROUP):
            for d in range(SMALL):
                row = (GROUP * g + s) * SMALL + d
                for n, places in enumerate(((0, 16), (8, 24), (0, 8), (16, 24))):
                    for place in places:
                        out[row, 4 * g + n, 32 * s + place + d] = 1.0
    return out.reshape(P, 16 * P)


def _arrays(np, i):
    cat = np.concatenate
    flat = lambda w: w.reshape(-1, w.shape[-1])
    side = lambda w: w.transpose(1, 0, 2).reshape(w.shape[1], -1)
    a = {
        "x": _feature_major(i["x"].reshape(TOK, D).T),
        "g_xattn": i["g_xattn"], "g_ffn": i["g_ffn"],
        "ident": np.eye(P, dtype=np.float32),
        "before": _bf16(np, np.tril(np.ones((16, 16), np.float32), -1).reshape(256)),
        "fside": i["fside_BxS2xS2_0"].transpose(2, 0, 1).reshape(CH, P, TOK).transpose(1, 0, 2),
        "ctx": i["ctx_1024"].reshape(TOK, CD).T,
        "keys": i["ctx_1024"].reshape(TILES, P, CD).transpose(1, 0, 2),
        "mask": i["mask_BxS2_bf1"].reshape(TOK).view(np.uint8),
        "x1_w": _heads(np, [
            _by_head(i["L1_xattn_Wq"]).reshape(HEADS, CH, P, HD).transpose(0, 2, 1, 3).reshape(HEADS, P, D),
            _by_head(i["L1_xattn_Wk"]), _by_head(i["L1_xattn_Wv"]).transpose(0, 2, 1),
            i["L1_xattn_Wo"].reshape(HEADS, HD, D)]),
        "x1_gq": i["L1_xattn_gq"], "x1_gk": i["L1_xattn_gk"],
        "x3_w": _heads(np, [
            _by_head(i["L3_xattn_Wq"]).transpose(0, 2, 1),
            _by_head(i["L3_xattn_Wk"]).transpose(0, 2, 1)[np.arange(HEADS) // 2],
            _by_head(i["L3_xattn_Wv"]).transpose(0, 2, 1)[np.arange(HEADS) // 2],
            i["L3_xattn_Wo"].reshape(HEADS, HD, D)]),
        "r_pos": i["fside_BxSx2_0"].reshape(TILES, P, 2).transpose(1, 0, 2),
        "r_w": cat([_feature_major(i["L2_xattn_Wq"]).reshape(P, 512),
                    _feature_major(i["L2_xattn_Wq"][:, np.arange(D) ^ 1]).reshape(P, 512),
                    i["L2_xattn_Wkv"][:, :D], i["L2_xattn_Wkv"][:, np.arange(D) ^ 1], i["L2_xattn_Wkv"][:, D:],
                    _feature_major(i["L2_xattn_Wout"]).reshape(P, 512)], 1),
        "r_spread": _spread(np), "r_bout": i["L2_xattn_bout"].reshape(CH, P).T,
        "l_router": _feature_major(i["L2_ffn_Wg"].T),
        "l_small": cat([_feature_major(flat(i["L2_ffn_A1"]).T).reshape(P, 512),
                        _feature_major(flat(i["L2_ffn_A3"]).T).reshape(P, 512),
                        _feature_major(i["L2_ffn_B2"].transpose(0, 2, 1).reshape(D, D)).reshape(P, 512)], 1),
        "l_w": cat([_columns(i["L2_ffn_W1"].T), _columns(i["L2_ffn_W3"].T),
                    _columns(i["L2_ffn_B1"].transpose(0, 2, 1).reshape(D, -1)),
                    _columns(i["L2_ffn_B3"].transpose(0, 2, 1).reshape(D, -1)),
                    i["L2_ffn_W2"].T.reshape(-1, P, D), flat(i["L2_ffn_A2"]).T.reshape(-1, P, D)], 2),
        "l_select": _bf16(np, _slots(np)),
        "f0_w": _ffn_blocks(np, cat([flat(i["L0_ffn_expert_gate_w"]), i["L0_ffn_shared_gate_w"]]),
                            cat([flat(i["L0_ffn_expert_up_w"]), i["L0_ffn_shared_up_w"]]),
                            cat([side(i["L0_ffn_expert_down_w"]), i["L0_ffn_shared_down_w"]], 1)),
        "f0_router": _feature_major(i["L0_ffn_router_w"].T), "f0_bias": i["L0_ffn_router_bias"],
        "f0_sel": _select(np, [128] * 17, 17),
        "f1_w": _ffn_blocks(np, flat(i["L1_ffn_w0_kernel"].transpose(0, 2, 1)),
                            flat(i["L1_ffn_w1_kernel"].transpose(0, 2, 1)), flat(i["L1_ffn_wo_kernel"]).T),
        "f1_router": _feature_major(i["L1_ffn_gate_kernel"]), "f1_sel": _select(np, [512] * 8, 32),
        "f3_w": _ffn_blocks(np, cat([flat(i["L3_ffn_W1"]), i["L3_ffn_Ws1"]]),
                            cat([flat(i["L3_ffn_W3"]), i["L3_ffn_Ws3"]]),
                            cat([side(i["L3_ffn_W2"]), i["L3_ffn_Ws2"]], 1)),
        "f3_router": _feature_major(i["L3_ffn_gate_w"].T), "f3_sel": _select(np, [176] * 16 + [352], 25),
    }
    return a


def kernel(**inputs):
    import numpy as np
    import concourse.bacc as bacc
    from concourse.bass_utils import run_bass_kernel_spmd

    nc = bacc.Bacc("TRN2", target_bir_lowering=False, num_devices=1)
    arrays, args = {}, {}
    for name, value in _arrays(np, {n: np.asarray(v) for n, v in inputs.items()}).items():
        value = np.ascontiguousarray(value)
        arrays[f"in_{name}"] = value
        args[name] = nc.dram_tensor(f"in_{name}", value.shape, mybir.dt.from_np(value.dtype),
                                    kind="ExternalInput").ap()
    out = nc.dram_tensor("out", (P, CH, TOK), F32, kind="ExternalOutput").ap()
    for name in ("before", "l_select", "f0_sel", "f1_sel", "f3_sel"):
        args[name] = args[name].bitcast(BF16)
    flamingo(nc, args, out)
    got = run_bass_kernel_spmd(nc, [arrays], core_ids=[0]).results[0]["out"]
    return got.transpose(2, 1, 0).reshape(B, S, D)
```
